# Optimizing a Trainium2 kernel written in Bass

```python
import numpy as np
import jax
import jax.numpy as jnp

def _softmax(x, axis=-1):
    return jax.nn.softmax(x, axis=axis)

def _gelu(x):
    return jax.nn.gelu(x, approximate=True)

def _silu(x):
    return jax.nn.silu(x)

def _sigmoid(x):
    return jax.nn.sigmoid(x)

def _layernorm(x, axis=-1, eps=1e-05):
    m = jnp.mean(x, axis=axis, keepdims=True)
    v = jnp.var(x, axis=axis, keepdims=True)
    return (x - m) / jnp.sqrt(v + eps)

def _scatter_add(tgt, idx, src, axis=0):
    return tgt.at[idx].add(src)

def _segment_sum(src, seg, n):
    return jax.ops.segment_sum(src, seg, n)
kernel_name = 'mk_flamingo_gated_d2_seqx_r8_96cc16'

def setup_inputs(seed: int=0):
    np.random.seed(seed)
    _w = jnp.asarray

    def _rec_inputs():
        import jax
        import jax.numpy as jnp
        _rk = jax.random.key(seed)
        x = 0.002226 + 0.9996 * jax.random.normal(jax.random.fold_in(_rk, 1), (32, 64, 128), jnp.float32)
        _lenS = 64 - jax.random.randint(jax.random.fold_in(_rk, 7), (32,), 0, max(1, 64 // 4) + 1, jnp.int32)
        _lenS2 = 64 - jax.random.randint(jax.random.fold_in(_rk, 8), (32,), 0, max(1, 64 // 4) + 1, jnp.int32)
        _ctx_1024P = jax.random.normal(jax.random.fold_in(_rk, 11), (32, 16, 128), jnp.float32)
        _ctx_1024c = jax.random.dirichlet(jax.random.fold_in(_rk, 511), 0.3 * jnp.ones((16,), jnp.float32), (32, 64))
        _ctx_1024t = jnp.einsum('bsk,bkd->bsd', _ctx_1024c, _ctx_1024P)
        _ctx_1024t = _ctx_1024t * jax.lax.rsqrt(jnp.mean(jnp.square(_ctx_1024t)) + 1e-12) * 0.953939
        ctx_1024 = -7.10856e-05 + 0.999911 * (_ctx_1024t + 0.3 * jax.random.normal(jax.random.fold_in(_rk, 611), (32, 64, 128), jnp.float32))
        _validS = jnp.arange(64)[None, :] < _lenS[:, None]
        _validS2 = jnp.arange(64)[None, :] < _lenS2[:, None]
        _causal = jnp.tril(jnp.ones((64, 64), dtype=bool))
        mask_BxS2_bk0 = jnp.logical_not(jnp.broadcast_to(_validS2[:, :], (32, 64)))
        _g = jax.random.normal(jax.random.fold_in(_rk, 9001), (2, 2), jnp.float32)
        _g = jnp.sign(_g) * jnp.maximum(jnp.abs(_g), 1.0) + (_g == 0) * 1.0
        g_xattn = _g[0]
        g_ffn = _g[1]
        return (x, ctx_1024, mask_BxS2_bk0, g_xattn, g_ffn)
    x, ctx_1024, mask_BxS2_bk0, g_xattn, g_ffn = _rec_inputs()

    def _L0_xattn_setup():
        import jax, jax.numpy as jnp
        import numpy as np
        DIM, DIM_HEAD, HEADS, SCALE = (128, 64, 8, 8.0)
        INNER = DIM_HEAD * HEADS
        LN_EPS = 1e-05
        L2_EPS = 1e-12

        def layer_norm(x, w, b):
            mu = jnp.mean(x, axis=-1, keepdims=True)
            var = jnp.mean(jnp.square(x - mu), axis=-1, keepdims=True)
            return (x - mu) * jax.lax.rsqrt(var + LN_EPS) * w + b

        def l2norm(t):
            n = jnp.sqrt(jnp.sum(jnp.square(t), axis=-1, keepdims=True))
            return t / jnp.maximum(n, L2_EPS)
        key = jax.random.key(seed)
        ks = jax.random.split(key, 8)
        b, n, m = (8, 1024, 64)
        x = jax.random.normal(ks[0], (b, n, DIM), dtype=jnp.float32)
        latents = jax.random.normal(ks[1], (b, m, DIM), dtype=jnp.float32)
        mask = jax.random.randint(ks[2], (b, n), 0, 2) > 0
        Wq = jax.random.normal(ks[3], (DIM, INNER), dtype=jnp.float32) * DIM ** (-0.5)
        Wkv = jax.random.normal(ks[4], (DIM, 2 * INNER), dtype=jnp.float32) * DIM ** (-0.5)
        Wo = jax.random.normal(ks[5], (INNER, DIM), dtype=jnp.float32) * INNER ** (-0.5)
        return {'x': x, 'latents': latents, 'mask': mask, 'ln_x_w': jnp.ones((DIM,)), 'ln_x_b': jnp.zeros((DIM,)), 'ln_l_w': jnp.ones((DIM,)), 'ln_l_b': jnp.zeros((DIM,)), 'Wq': Wq, 'Wkv': Wkv, 'q_scale': jnp.ones((DIM_HEAD,)), 'k_scale': jnp.ones((DIM_HEAD,)), 'Wo': Wo, 'ln_o_w': jnp.ones((DIM,)), 'ln_o_b': jnp.zeros((DIM,))}
    _L0_xattn_all = _L0_xattn_setup()
    _L0_xattn_in = {k: v for k, v in _L0_xattn_all.items() if k in ('ln_x_w', 'ln_x_b', 'ln_l_w', 'ln_l_b', 'Wq', 'Wkv', 'q_scale', 'k_scale', 'Wo', 'ln_o_w', 'ln_o_b')}
    del _L0_xattn_all

    def _L0_ffn_setup():
        import jax, jax.numpy as jnp
        import numpy as np
        B, S, D = (4, 512, 128)
        E, F_EXP = (16, 256)
        F_C = 2.0
        F_SH = 256
        key = jax.random.key(seed)
        ks = jax.random.split(key, 8)
        s = 0.02
        return {'hidden_states': jax.random.normal(ks[0], (B, S, D), jnp.float32), 'gate_w': jax.random.normal(ks[1], (E, D), jnp.float32) * s, 'Wg': jax.random.normal(ks[2], (E, F_EXP, D), jnp.float32) * s, 'Wu': jax.random.normal(ks[3], (E, F_EXP, D), jnp.float32) * s, 'Wd': jax.random.normal(ks[4], (E, D, F_EXP), jnp.float32) * s, 'Ws_g': jax.random.normal(ks[5], (F_SH, D), jnp.float32) * s, 'Ws_u': jax.random.normal(ks[6], (F_SH, D), jnp.float32) * s, 'Ws_d': jax.random.normal(ks[7], (D, F_SH), jnp.float32) * s}
    _L0_ffn_all = _L0_ffn_setup()
    _L0_ffn_in = {k: v for k, v in _L0_ffn_all.items() if k in ('gate_w', 'Wg', 'Wu', 'Wd', 'Ws_g', 'Ws_u', 'Ws_d')}
    del _L0_ffn_all

    def _L1_xattn_setup():
        import jax, jax.numpy as jnp
        import numpy as np
        B, T, D, H = (2, 256, 128, 16)
        DH = D // H
        key = jax.random.key(seed)
        ks = jax.random.split(key, 11)
        s = 1.0 / np.sqrt(D)
        return {'q': jax.random.normal(ks[0], (B, T, D), jnp.float32), 'k': jax.random.normal(ks[1], (B, T, D), jnp.float32), 'v': jax.random.normal(ks[2], (B, T, D), jnp.float32), 'wq_w': jax.random.normal(ks[3], (D, D), jnp.float32) * s, 'wq_b': jnp.zeros((D,), jnp.float32), 'wk_w': jax.random.normal(ks[4], (D, D), jnp.float32) * s, 'wk_b': jnp.zeros((D,), jnp.float32), 'wv_w': jax.random.normal(ks[5], (D, D), jnp.float32) * s, 'wv_b': jnp.zeros((D,), jnp.float32), 'wo_w': jax.random.normal(ks[6], (D, D), jnp.float32) * s, 'wo_b': jnp.zeros((D,), jnp.float32)}
    _L1_xattn_all = _L1_xattn_setup()
    _L1_xattn_in = {k: v for k, v in _L1_xattn_all.items() if k in ('wq_w', 'wq_b', 'wk_w', 'wk_b', 'wv_w', 'wv_b', 'wo_w', 'wo_b')}
    del _L1_xattn_all

    def _L1_ffn_setup():
        import jax, jax.numpy as jnp
        import numpy as np
        EPS = 1e-05

        def act_quant(x):
            scale = 127.0 / jnp.clip(jnp.max(jnp.abs(x), axis=-1, keepdims=True), EPS, None)
            xq = jnp.clip(jnp.round(x * scale), -128.0, 127.0)
            return (xq, scale)

        def weight_quant(w):
            scale = 1.0 / jnp.clip(jnp.mean(jnp.abs(w)), EPS, None)
            wq = jnp.clip(jnp.round(w * scale), -1.0, 1.0)
            return (wq, scale)

        def qlinear(x, w, b):
            xq, sx = act_quant(x)
            wq, sw = weight_quant(w)
            y = jnp.einsum('bsd,hd->bsh', xq, wq) / (sx * sw)
            return y + b

        def layernorm(x, gamma, beta):
            mu = jnp.mean(x, axis=-1, keepdims=True)
            var = jnp.mean(jnp.square(x - mu), axis=-1, keepdims=True)
            return (x - mu) * jax.lax.rsqrt(var + EPS) * gamma + beta
        key = jax.random.key(seed)
        ks = jax.random.split(key, 6)
        dim, hidden = (128, 512)
        B, S = (4, 256)
        x = jax.random.normal(ks[0], (B, S, dim), dtype=jnp.float32)
        w1 = jax.random.normal(ks[1], (hidden, dim), dtype=jnp.float32) * (1.0 / np.sqrt(dim))
        b1 = jnp.zeros((hidden,), dtype=jnp.float32)
        w2 = jax.random.normal(ks[2], (dim, hidden), dtype=jnp.float32) * (1.0 / np.sqrt(hidden))
        b2 = jnp.zeros((dim,), dtype=jnp.float32)
        gamma = jnp.ones((dim,), dtype=jnp.float32)
        beta = jnp.zeros((dim,), dtype=jnp.float32)
        return {'x': x, 'w1': w1, 'b1': b1, 'w2': w2, 'b2': b2, 'gamma': gamma, 'beta': beta}
    _L1_ffn_all = _L1_ffn_setup()
    _L1_ffn_in = {k: v for k, v in _L1_ffn_all.items() if k in ('w1', 'b1', 'w2', 'b2', 'gamma', 'beta')}
    del _L1_ffn_all
    return {'x': x, 'ctx_1024': ctx_1024, 'mask_BxS2_bk0': mask_BxS2_bk0, 'g_xattn': g_xattn, 'g_ffn': g_ffn, 'L0_xattn_ln_x_w': _L0_xattn_in['ln_x_w'], 'L0_xattn_ln_x_b': _L0_xattn_in['ln_x_b'], 'L0_xattn_ln_l_w': _L0_xattn_in['ln_l_w'], 'L0_xattn_ln_l_b': _L0_xattn_in['ln_l_b'], 'L0_xattn_Wq': _L0_xattn_in['Wq'], 'L0_xattn_Wkv': _L0_xattn_in['Wkv'], 'L0_xattn_q_scale': _L0_xattn_in['q_scale'], 'L0_xattn_k_scale': _L0_xattn_in['k_scale'], 'L0_xattn_Wo': _L0_xattn_in['Wo'], 'L0_xattn_ln_o_w': _L0_xattn_in['ln_o_w'], 'L0_xattn_ln_o_b': _L0_xattn_in['ln_o_b'], 'L0_ffn_gate_w': _L0_ffn_in['gate_w'], 'L0_ffn_Wg': _L0_ffn_in['Wg'], 'L0_ffn_Wu': _L0_ffn_in['Wu'], 'L0_ffn_Wd': _L0_ffn_in['Wd'], 'L0_ffn_Ws_g': _L0_ffn_in['Ws_g'], 'L0_ffn_Ws_u': _L0_ffn_in['Ws_u'], 'L0_ffn_Ws_d': _L0_ffn_in['Ws_d'], 'L1_xattn_wq_w': _L1_xattn_in['wq_w'], 'L1_xattn_wq_b': _L1_xattn_in['wq_b'], 'L1_xattn_wk_w': _L1_xattn_in['wk_w'], 'L1_xattn_wk_b': _L1_xattn_in['wk_b'], 'L1_xattn_wv_w': _L1_xattn_in['wv_w'], 'L1_xattn_wv_b': _L1_xattn_in['wv_b'], 'L1_xattn_wo_w': _L1_xattn_in['wo_w'], 'L1_xattn_wo_b': _L1_xattn_in['wo_b'], 'L1_ffn_w1': _L1_ffn_in['w1'], 'L1_ffn_b1': _L1_ffn_in['b1'], 'L1_ffn_w2': _L1_ffn_in['w2'], 'L1_ffn_b2': _L1_ffn_in['b2'], 'L1_ffn_gamma': _L1_ffn_in['gamma'], 'L1_ffn_beta': _L1_ffn_in['beta']}

def reference(x, ctx_1024, mask_BxS2_bk0, g_xattn, g_ffn, L0_xattn_ln_x_w, L0_xattn_ln_x_b, L0_xattn_ln_l_w, L0_xattn_ln_l_b, L0_xattn_Wq, L0_xattn_Wkv, L0_xattn_q_scale, L0_xattn_k_scale, L0_xattn_Wo, L0_xattn_ln_o_w, L0_xattn_ln_o_b, L0_ffn_gate_w, L0_ffn_Wg, L0_ffn_Wu, L0_ffn_Wd, L0_ffn_Ws_g, L0_ffn_Ws_u, L0_ffn_Ws_d, L1_xattn_wq_w, L1_xattn_wq_b, L1_xattn_wk_w, L1_xattn_wk_b, L1_xattn_wv_w, L1_xattn_wv_b, L1_xattn_wo_w, L1_xattn_wo_b, L1_ffn_w1, L1_ffn_b1, L1_ffn_w2, L1_ffn_b2, L1_ffn_gamma, L1_ffn_beta):
    import jax
    import jax.numpy as jnp

    def _L0_xattn_ref(x, latents, mask, ln_x_w, ln_x_b, ln_l_w, ln_l_b, Wq, Wkv, q_scale, k_scale, Wo, ln_o_w, ln_o_b):
        import jax, jax.numpy as jnp
        import numpy as np
        DIM, DIM_HEAD, HEADS, SCALE = (128, 64, 8, 8.0)
        INNER = DIM_HEAD * HEADS
        LN_EPS = 1e-05
        L2_EPS = 1e-12

        def layer_norm(x, w, b):
            mu = jnp.mean(x, axis=-1, keepdims=True)
            var = jnp.mean(jnp.square(x - mu), axis=-1, keepdims=True)
            return (x - mu) * jax.lax.rsqrt(var + LN_EPS) * w + b

        def l2norm(t):
            n = jnp.sqrt(jnp.sum(jnp.square(t), axis=-1, keepdims=True))
            return t / jnp.maximum(n, L2_EPS)
        b, n, _ = x.shape
        m = latents.shape[1]
        x = layer_norm(x, ln_x_w, ln_x_b)
        latents = layer_norm(latents, ln_l_w, ln_l_b)
        q = latents @ Wq
        kv_input = jnp.concatenate([x, latents], axis=1)
        kv = kv_input @ Wkv
        k, v = jnp.split(kv, 2, axis=-1)

        def to_heads(t):
            return t.reshape(t.shape[0], t.shape[1], HEADS, DIM_HEAD).transpose(0, 2, 1, 3)
        q, k, v = map(to_heads, (q, k, v))
        q = l2norm(q) * q_scale
        k = l2norm(k) * k_scale
        sim = jnp.einsum('bhid,bhjd->bhij', q, k) * SCALE
        full_mask = jnp.concatenate([mask, jnp.ones((b, m), dtype=bool)], axis=1)[:, None, None, :]
        max_neg = -jnp.finfo(sim.dtype).max
        sim = jnp.where(full_mask, sim, max_neg)
        attn = jax.nn.softmax(sim.astype(jnp.float32), axis=-1).astype(sim.dtype)
        out = jnp.einsum('bhij,bhjd->bhid', attn, v)
        out = out.transpose(0, 2, 1, 3).reshape(b, m, INNER)
        return layer_norm(out @ Wo, ln_o_w, ln_o_b)

    def _L0_ffn_ref(hidden_states, gate_w, Wg, Wu, Wd, Ws_g, Ws_u, Ws_d):
        import jax, jax.numpy as jnp
        import numpy as np
        B, S, D = (4, 512, 128)
        E, F_EXP = (16, 256)
        F_C = 2.0
        F_SH = 256
        b, s, d = hidden_states.shape
        e = gate_w.shape[0]
        cap = int(s * F_C / e)
        logits = jnp.einsum('bsd,ed->bse', hidden_states, gate_w)
        scores = jax.nn.softmax(logits, axis=-1).transpose(0, 2, 1)
        topk_w, topk_idx = jax.lax.top_k(scores, cap)
        x_tok = jnp.take_along_axis(hidden_states[:, None, :, :], topk_idx[..., None], axis=2)
        g = jnp.einsum('becd,efd->becf', x_tok, Wg)
        u = jnp.einsum('becd,efd->becf', x_tok, Wu)
        h = jax.nn.gelu(g, approximate=False) * u
        eo = jnp.einsum('becf,edf->becd', h, Wd) * topk_w[..., None]
        offs = (jnp.arange(b) * s)[:, None, None]
        flat_idx = (topk_idx + offs).reshape(-1)
        flat = jnp.zeros((b * s, d), hidden_states.dtype)
        flat = flat.at[flat_idx].add(eo.reshape(-1, d))
        out = flat.reshape(b, s, d)
        gs = jnp.einsum('bsd,fd->bsf', hidden_states, Ws_g)
        us = jnp.einsum('bsd,fd->bsf', hidden_states, Ws_u)
        shared = jnp.einsum('bsf,df->bsd', jax.nn.gelu(gs, approximate=False) * us, Ws_d)
        return out + shared

    def _L1_xattn_ref(q, k, v, wq_w, wq_b, wk_w, wk_b, wv_w, wv_b, wo_w, wo_b):
        import jax, jax.numpy as jnp
        import numpy as np
        B, T, D, H = (2, 256, 128, 16)
        DH = D // H
        b, t, d = q.shape
        wq = (q @ wq_w.T + wq_b).reshape(b, t, H, DH)
        wk = (k @ wk_w.T + wk_b).reshape(b, t, H, DH)
        wv = (v @ wv_w.T + wv_b).reshape(b, t, H, DH)
        scores = jnp.einsum('bthd,bshd->bhts', wq, wk) / jnp.sqrt(jnp.float32(DH))
        probs = jax.nn.softmax(scores, axis=-1)
        attn = jnp.einsum('bhts,bshd->bthd', probs, wv)
        attn = attn.reshape(b, t, d)
        return attn @ wo_w.T + wo_b

    def _L1_ffn_ref(x, w1, b1, w2, b2, gamma, beta):
        import jax, jax.numpy as jnp
        import numpy as np
        EPS = 1e-05

        def act_quant(x):
            scale = 127.0 / jnp.clip(jnp.max(jnp.abs(x), axis=-1, keepdims=True), EPS, None)
            xq = jnp.clip(jnp.round(x * scale), -128.0, 127.0)
            return (xq, scale)

        def weight_quant(w):
            scale = 1.0 / jnp.clip(jnp.mean(jnp.abs(w)), EPS, None)
            wq = jnp.clip(jnp.round(w * scale), -1.0, 1.0)
            return (wq, scale)

        def qlinear(x, w, b):
            xq, sx = act_quant(x)
            wq, sw = weight_quant(w)
            y = jnp.einsum('bsd,hd->bsh', xq, wq) / (sx * sw)
            return y + b

        def layernorm(x, gamma, beta):
            mu = jnp.mean(x, axis=-1, keepdims=True)
            var = jnp.mean(jnp.square(x - mu), axis=-1, keepdims=True)
            return (x - mu) * jax.lax.rsqrt(var + EPS) * gamma + beta
        h = layernorm(x, gamma, beta)
        h = qlinear(h, w1, b1)
        h = jax.nn.gelu(h, approximate=False)
        out = qlinear(h, w2, b2)
        return out
    x = x + jnp.tanh(g_xattn[0]) * _L0_xattn_ref(ctx_1024, _layernorm(x, axis=-1), mask_BxS2_bk0, L0_xattn_ln_x_w, L0_xattn_ln_x_b, L0_xattn_ln_l_w, L0_xattn_ln_l_b, L0_xattn_Wq, L0_xattn_Wkv, L0_xattn_q_scale, L0_xattn_k_scale, L0_xattn_Wo, L0_xattn_ln_o_w, L0_xattn_ln_o_b)
    x = x + jnp.tanh(g_ffn[0]) * _L0_ffn_ref(_layernorm(x, axis=-1), L0_ffn_gate_w, L0_ffn_Wg, L0_ffn_Wu, L0_ffn_Wd, L0_ffn_Ws_g, L0_ffn_Ws_u, L0_ffn_Ws_d)
    x = x + jnp.tanh(g_xattn[1]) * _L1_xattn_ref(_layernorm(x, axis=-1), ctx_1024, ctx_1024, L1_xattn_wq_w, L1_xattn_wq_b, L1_xattn_wk_w, L1_xattn_wk_b, L1_xattn_wv_w, L1_xattn_wv_b, L1_xattn_wo_w, L1_xattn_wo_b)
    x = x + jnp.tanh(g_ffn[1]) * _L1_ffn_ref(_layernorm(x, axis=-1), L1_ffn_w1, L1_ffn_b1, L1_ffn_w2, L1_ffn_b2, L1_ffn_gamma, L1_ffn_beta)
    return x

_drawn_inputs = setup_inputs


def setup_inputs(seed=0):
    import zlib

    import numpy as np

    out = dict(_drawn_inputs(seed))
    spreads = {'g_ffn': (-1.0, 0.6),
     'L0_xattn_ln_x_w': (1.0, 0.2),
     'L0_xattn_ln_x_b': (0.0, 0.1),
     'L0_xattn_ln_l_w': (1.0, 0.2),
     'L0_xattn_ln_l_b': (0.0, 0.1),
     'L0_xattn_q_scale': (1.0, 0.2),
     'L0_xattn_k_scale': (1.0, 0.2),
     'L0_xattn_ln_o_w': (1.0, 0.2),
     'L0_xattn_ln_o_b': (0.0, 0.1),
     'L1_xattn_wq_b': (0.0, 1.479),
     'L1_xattn_wk_b': (0.0, 2.0),
     'L1_xattn_wv_b': (0.0, 0.473),
     'L1_xattn_wo_b': (0.0, 0.421),
     'L1_ffn_b1': (0.0, 1.021),
     'L1_ffn_b2': (0.0, 0.416),
     'L1_ffn_gamma': (1.0, 0.6),
     'L1_ffn_beta': (0.0, 1.64)}
    factors = {'L0_ffn_gate_w': 8.0,
     'L0_ffn_Wg': 8.0,
     'L0_ffn_Wu': 8.0,
     'L0_ffn_Wd': 8.0,
     'L0_ffn_Ws_g': 8.0,
     'L0_ffn_Ws_u': 8.0,
     'L0_ffn_Ws_d': 8.0}
    for name, (base, spread) in spreads.items():
        noise = np.random.default_rng([zlib.crc32(name.encode()), seed]).standard_normal(out[name].shape)
        drawn = base * np.exp(spread * noise) if base else spread * noise
        out[name] = jnp.asarray(drawn.astype(out[name].dtype))
    for name, factor in factors.items():
        out[name] = (out[name] * factor).astype(out[name].dtype)
    return out
```

```python
from contextlib import ExitStack

import concourse.bass as bass
from concourse import mybir

ALU = mybir.AluOpType
ACT = mybir.ActivationFunctionType
AX = mybir.AxisListType
F32 = mybir.dt.float32
BF16 = mybir.dt.bfloat16
U8 = mybir.dt.uint8
U32 = mybir.dt.uint32

P = 128
STOP = "D"


def wait(eng, sem, count):
    if isinstance(count, int) and count <= 0:
        return
    eng.wait_ge(sem, count)


class Steps:

    def __init__(self, eng, sem, base=0):
        self.eng, self.sem, self.base, self.n = eng, sem, base, 0

    def __call__(self, ins, carried=None):
        self.n += 1
        ins.then_inc(self.sem, 1)
        if carried is not None:
            self.eng.wait_ge(carried, 1)
        self.eng.wait_ge(self.sem, self.base + self.n)


def pipelined(eng, tiles, front, back, both=None):
    if both is None:
        def both(t, tp):
            front(t + 1, 1 - tp)
            back(t, tp)
    front(0, 0)
    both(0, 0)
    both(1, 1)
    with eng.Fori(1, (tiles - 2) // 2) as j:
        both(2 * j, 0)
        both(2 * j + 1, 1)
    both(tiles - 2, 0)
    back(tiles - 1, 1)


def build(nc, x, ctx, mask, g_xattn, g_ffn, ln_x_w, ln_x_b, ln_l_w, ln_l_b, Wq, Wkv, q_scale, k_scale, Wo,
          ln_o_w, ln_o_b, gate_w, Wg, Wu, Wd, Ws_g, Ws_u, Ws_d, wq_w, wq_b, wk_w, wk_b, wv_w, wv_b,
          wo_w, wo_b, w1, b1, w2, b2, gamma, beta, out):
    B, S, D = x.shape
    NT = B * S // P
    E = Wg.shape[0]
    CAP = S * 2 // E
    FE = Wg.shape[1]
    INNER = Wq.shape[1]
    DH0 = q_scale.shape[0]
    H0 = INNER // DH0
    HP = H0 // 2
    FF = w1.shape[0]
    EPS = 1e-5
    MAGIC = 1.5 * 2.0 ** 23
    NEG = -1e30

    x_tiles = x.rearrange("b s d -> (b s) d").rearrange("(t p) d -> p t d", p=P)
    c_tiles = ctx.rearrange("b s d -> (b s) d").rearrange("(t p) d -> p t d", p=P)
    o_tiles = out.rearrange("b s d -> (b s) d").rearrange("(t p) d -> p t d", p=P)

    with ExitStack() as whole:
        def sb(name, shape, dt=F32, at=whole):
            return at.enter_context(nc.sbuf_tensor(name, shape, dt))

        def sem(name, at=whole):
            return at.enter_context(nc.semaphore(name))

        xs = sb("xs", [P, NT, D])
        cs = sb("cs", [P, NT, D])
        mean = sb("mean", [P, 2, NT])
        rstd = sb("rstd", [P, 2, NT])
        stats = sb("stats", [P, 2, NT, 6])
        neghalf = sb("neghalf", [P, 2 * NT])
        ident = sb("ident", [P, P])
        identb = sb("identb", [P, P], BF16)
        fold = sb("fold", [P, S])
        half = sb("half", [P, 2])
        tokid = sb("tokid", [P, 1])
        quad = sb("quad", [P, 4])
        halves = sb("halves", [E, 2, P], BF16)
        gates = sb("gates", [P, 4])
        cols = sb("cols", [P, 12])
        rows = sb("rows", [P, 6, D])
        b1row = sb("b1row", [P, FF])
        wq_a = sb("wq_a", [P, INNER])
        wkv_a = sb("wkv_a", [P, 2 * INNER])
        wo_a = sb("wo_a", [P, HP // 2, 2, D])
        maskrow = sb("maskrow", [1, B, S], U8)
        maskbias = sb("maskbias", [1, NT, 4, S], BF16)
        ones = sb("ones", [1, P], BF16)
        gw_t = sb("gw_t", [P, E])
        ws_t = sb("ws_t", [P, 6, P])
        w_c = sb("w_c", [P, 4, P])
        w1_t = sb("w1_t", [P, FF], BF16)
        w2_t = sb("w2_t", [P, FF // P, P], BF16)
        wmean = sb("wmean", [P, 2])

        wa_in = sem("wa_in")
        with ExitStack() as ph, nc.Block() as block:
            small_in, late_in, mask_in = (sem(n, ph) for n in ("small_in", "late_in", "mask_in"))
            x_in = [sem(f"x_in{c}", ph) for c in range(4)]
            c_in = [sem(f"c_in{c}", ph) for c in range(4)]
            s_const, s_dve, s_pe, s_copied, s_gate, s_gated, s_stats, s_rstd, s_pool = (
                sem(n, ph) for n in ("s_const", "s_dve", "s_pe", "s_copied", "s_gate", "s_gated",
                                     "s_stats", "s_rstd", "s_pool"))
            nat = sb("nat", [P, 6, P], at=ph)
            nat_c = sb("nat_c", [P, 4, P], at=ph)
            nat_g = sb("nat_g", [E, P], at=ph)
            nat_1 = sb("nat_1", [P, FF // P, P], at=ph)
            nat_2 = sb("nat_2", [P, FF], at=ph)
            q_1 = sb("q_1", [P, FF // P, P], BF16, at=ph)
            q_2 = sb("q_2", [P, FF], BF16, at=ph)
            tokrow = sb("tokrow", [P, P], at=ph)
            tmp = sb("tmp", [P, FF], at=ph)
            tmp2 = sb("tmp2", [P, 2, NT, 4], at=ph)
            gin = sb("gin", [P, 4], at=ph)
            onesf = sb("onesf", [P, P], at=ph)
            pw = [ph.enter_context(nc.psum_tensor(f"pw{i}", [P, 4, P], F32)) for i in range(4)]
            pwb = [ph.enter_context(nc.psum_tensor(f"pwb{i}", [P, 4, P], BF16)) for i in range(2)]
            psw = ph.enter_context(nc.psum_tensor("psw", [P, 512], F32))

            @block.sync
            def _(sp):
                for c in range(4):
                    n = NT // 4
                    sp.dma_start(xs[:, c * n:(c + 1) * n, :], x_tiles[:, c * n:(c + 1) * n, :]).then_inc(x_in[c], 16)
                sp.dma_start(wq_a[:], Wq).then_inc(wa_in, 16)
                sp.dma_start(wkv_a[:], Wkv).then_inc(wa_in, 16)
                for a in range(2):
                    for j in range(HP // 2):
                        src = Wo.rearrange("(j a h d) n -> j a d h n", j=HP // 2, a=2, h=2)[j, a]
                        sp.dma_start(wo_a[a * DH0:(a + 1) * DH0, j], src).then_inc(wa_in, 16)
                for i, w in enumerate((Ws_g, Ws_u)):
                    sp.dma_start(nat[:, 2 * i:2 * i + 2, :], w.rearrange("(c p) d -> p c d", p=P)).then_inc(late_in, 16)
                sp.dma_start(nat[:, 4:6, :], Ws_d.rearrange("d (c f) -> d c f", f=P)).then_inc(late_in, 16)
                sp.dma_start(nat_g[:], gate_w).then_inc(late_in, 16)
                for i, w in enumerate((wq_w, wk_w, wv_w, wo_w)):
                    sp.dma_start(nat_c[:, i, :], w).then_inc(late_in, 16)
                sp.dma_start(nat_1[:], w1.rearrange("(c p) d -> p c d", p=P)).then_inc(late_in, 16)
                sp.dma_start(nat_2[:], w2).then_inc(late_in, 16)
                sp.wait_ge(late_in, 160)

            @block.scalar
            def _(act):
                for c in range(4):
                    n = NT // 4
                    act.dma_start(cs[:, c * n:(c + 1) * n, :], c_tiles[:, c * n:(c + 1) * n, :]).then_inc(c_in[c], 16)
                act.dma_start(maskrow[:], mask.rearrange("(o b) s -> o b s", o=1)).then_inc(mask_in, 16)
                for i, v in enumerate((ln_x_w, ln_x_b, ln_l_w, ln_l_b)):
                    act.dma_start(cols[:, i:i + 1], v.rearrange("(d o) -> d o", o=1)).then_inc(small_in, 16)
                for i, v in ((8, q_scale), (9, k_scale)):
                    for a in range(2):
                        act.dma_start(cols[a * DH0:(a + 1) * DH0, i:i + 1],
                                      v.rearrange("(d o) -> d o", o=1)).then_inc(small_in, 16)
                for i, v in enumerate((wq_b, wk_b, wv_b)):
                    act.dma_start(cols[:, 5 + i:6 + i], v.rearrange("(d o) -> d o", o=1)).then_inc(small_in, 16)
                for i, v in enumerate((ln_o_w, ln_o_b, wo_b, b2, gamma, beta)):
                    act.dma_start(rows[:, i, :], v.rearrange("(o d) -> o d", o=1).to_broadcast([P, D])).then_inc(small_in, 16)
                act.dma_start(b1row[:], b1.rearrange("(o d) -> o d", o=1).to_broadcast([P, FF])).then_inc(small_in, 16)
                for i, v in enumerate((g_xattn, g_ffn)):
                    act.dma_start(gin[:, 2 * i:2 * i + 2], v.rearrange("(o d) -> o d", o=1).to_broadcast([P, 2])).then_inc(small_in, 16)
                act.wait_ge(small_in, 16 * 20)
                nc.scalar.activation(gates[:], gin[:], ACT.Tanh).then_inc(s_gate, 1)

            @block.gpsimd
            def _(pool):
                pc = Steps(pool, s_pool)
                pc(nc.gpsimd.memset(ident[:], 0.0))
                pc(nc.gpsimd.affine_select(out=ident[:], in_=ident[:], compare_op=ALU.not_equal, fill=1.0,
                                           base=0, pattern=[[-1, P]], channel_multiplier=1))
                nc.gpsimd.iota(tokrow[:], pattern=[[0, 2], [1, S]], base=0, channel_multiplier=0,
                               allow_small_or_imprecise_dtypes=True).then_inc(s_const, 1)
                pool.wait_ge(s_stats, 1)
                nc.gpsimd.tensor_tensor(rstd[:].rearrange("p a t -> p (a t)"), rstd[:].rearrange("p a t -> p (a t)"),
                                        neghalf[:], ALU.pow).then_inc(s_rstd, 1)
                pool.wait_ge(s_rstd, 1)

            @block.vector
            def _(dve):
                d = Steps(dve, s_dve)
                d(nc.vector.memset(neghalf[:], -0.5))
                d(nc.vector.memset(ones[:], 1.0))
                d(nc.vector.memset(halves[:], 0.0))
                for b in range(2):
                    d(nc.vector.memset(halves[:, b, b * S:(b + 1) * S], 1.0))
                d(nc.vector.memset(onesf[:], 1.0))
                dve.wait_ge(s_pool, 2)
                dve.wait_ge(s_const, 1)
                d(nc.vector.tensor_copy(identb[:], ident[:]))
                d(nc.vector.tensor_tensor(fold[:], ident[:, 0:S], ident[:, S:P], ALU.add))
                d(nc.vector.tensor_reduce(half[:], ident[:].rearrange("p (a s) -> p a s", a=2), AX.X, ALU.add))
                d(nc.vector.tensor_tensor(tmp[:, 0:P], ident[:], tokrow[:], ALU.mult))
                d(nc.vector.tensor_reduce(tokid[:], tmp[:, 0:P], AX.X, ALU.add))
                d(nc.vector.tensor_reduce(tmp[:, 128:144], ident[:].rearrange("p (h e) -> p h e", e=8), AX.X, ALU.add))
                d(nc.vector.tensor_reduce(quad[:], tmp[:, 128:144].rearrange("p (g h) -> p h g", h=4), AX.X, ALU.add))
                for c in range(4):
                    for which, src, landed in ((1, xs, x_in), (0, cs, c_in)):
                        dve.wait_ge(landed[c], 16)
                        for t in range(c * NT // 4, (c + 1) * NT // 4):
                            last = nc.vector.bn_stats(stats[:, which, t, :], src[:, t, :])
                    d(last)
                m_sum, m_dif, var = tmp2[:, :, :, 0], tmp2[:, :, :, 1], tmp2[:, :, :, 2]
                d(nc.vector.tensor_tensor(m_sum, stats[:, :, :, 1], stats[:, :, :, 4], ALU.add))
                d(nc.vector.tensor_tensor(m_dif, stats[:, :, :, 1], stats[:, :, :, 4], ALU.subtract))
                d(nc.vector.tensor_scalar(mean[:], m_sum, 0.5, None, ALU.mult))
                d(nc.vector.scalar_tensor_tensor(m_dif, m_dif, 0.25, m_dif, ALU.mult, ALU.mult))
                d(nc.vector.tensor_tensor(var, stats[:, :, :, 2], stats[:, :, :, 5], ALU.add))
                d(nc.vector.scalar_tensor_tensor(var, var, 1.0 / D, m_dif, ALU.mult, ALU.add))
                d(nc.vector.tensor_scalar(rstd[:, 0, :], var[:, 0], EPS, None, ALU.add))
                d(nc.vector.tensor_scalar(rstd[:, 1, :], var[:, 1], 1.0 + EPS, EPS * EPS, ALU.mult, ALU.add))
                nc.vector.memset(tmp2[:, 0, 0, 3:4], 0.0).then_inc(s_stats, 1)
                dve.wait_ge(mask_in, 16)
                d(nc.vector.memset(maskbias[:], 0.0))
                d(nc.vector.tensor_scalar(maskbias[:, :, 0:4:3, :], maskrow[:].rearrange("o (t b) s -> o t b s", b=2),
                                          1.0, -NEG, ALU.subtract, ALU.mult))
                dve.wait_ge(s_gate, 1)
                d(nc.vector.scalar_tensor_tensor(cols[:, 4:5], cols[:, 8:9], 8.0, cols[:, 9:10], ALU.mult, ALU.mult))
                d(nc.vector.tensor_scalar(rows[:, 0:2, :], rows[:, 0:2, :], gates[:, 0:1], None, ALU.mult))
                d(nc.vector.tensor_scalar(rows[:, 2, :], rows[:, 2, :], gates[:, 1:2], None, ALU.mult))
                d(nc.vector.tensor_scalar(rows[:, 3, :], rows[:, 3, :], gates[:, 3:4], None, ALU.mult))
                d(nc.vector.tensor_scalar(cols[:, 5:6], cols[:, 5:6], 8.0 ** -0.5, None, ALU.mult))
                dve.wait_ge(late_in, 160)
                d(nc.vector.tensor_reduce(tmp2[:, 0, 0:1, 0], nat_1[:].rearrange("p c d -> p (c d)"), AX.X, ALU.add,
                                          apply_absolute_value=True))
                d(nc.vector.tensor_reduce(tmp2[:, 0, 1:2, 0], nat_2[:], AX.X, ALU.add, apply_absolute_value=True))
                nc.vector.tensor_copy(tmp2[:, 1, 0:2, 0], tmp2[:, 0, 0:2, 0]).then_inc(s_gated, 1)
                dve.wait_ge(s_pe, 1)
                d(nc.vector.tensor_scalar(wmean[:], psw[:, 0:2], 1.0 / (FF * D), EPS, ALU.mult, ALU.max))
                d(nc.vector.reciprocal(tmp2[:, 1, 0:2, 1], wmean[:]))
                for i, (w, q) in enumerate(((nat_1[:].rearrange("p c d -> p (c d)"), q_1[:].rearrange("p c d -> p (c d)")),
                                            (nat_2[:], q_2[:]))):
                    d(nc.vector.tensor_scalar(tmp[:], w, tmp2[:, 1, i:i + 1, 1], MAGIC, ALU.mult, ALU.add))
                    d(nc.vector.tensor_scalar(tmp[:], tmp[:], MAGIC, 1.0, ALU.subtract, ALU.min))
                    ins = nc.vector.tensor_scalar(q, tmp[:], -1.0, None, ALU.max)
                    ins.then_inc(s_gated, 1)
                    dve.wait_ge(s_gated, 2 + i)
                dve.wait_ge(s_pe, 2)
                d(nc.vector.tensor_copy(ws_t[:, 0:4, :], pw[0][:]))
                d(nc.vector.tensor_copy(ws_t[:, 4:6, :], pw[1][:, 0:2, :]))
                d(nc.vector.tensor_copy(gw_t[:], pw[1][:, 2, 0:E]))
                d(nc.vector.tensor_copy(w_c[:, 0:3, :], pw[2][:, 0:3, :]))
                d(nc.vector.tensor_scalar(w_c[:, 3, :], pw[2][:, 3, :], gates[:, 1:2], None, ALU.mult))
                dve.wait_ge(s_pe, 3)
                d(nc.vector.tensor_copy(w1_t[:], pwb[0][:].rearrange("p c d -> p (c d)")))
                d(nc.vector.tensor_copy(w2_t[:], pwb[1][:]))

            @block.tensor
            def _(pe):
                pe.wait_ge(s_gated, 1)
                nc.tensor.matmul(psw[:, 0:2], onesf[:], tmp2[:, 1, 0:2, 0], start=True, stop=True).then_inc(s_pe, 1)
                pe.wait_ge(late_in, 160)
                for i in range(4):
                    nc.tensor.transpose(pw[0][:, i, :], nat[:, i, :], ident[:])
                for i in range(2):
                    nc.tensor.transpose(pw[1][:, i, :], nat[:, 4 + i, :], ident[:])
                nc.tensor.transpose(pw[1][:, 2, 0:E], nat_g[:], ident[0:E, 0:E])
                for i in range(4):
                    last = nc.tensor.transpose(pw[2][:, i, :], nat_c[:, i, :], ident[:])
                last.then_inc(s_pe, 1)
                pe.wait_ge(s_gated, 3)
                for i in range(4):
                    nc.tensor.transpose(pwb[0][:, i, :], q_1[:, i, :], identb[:])
                for i in range(4):
                    last = nc.tensor.transpose(pwb[1][:, i, :], q_2[:, i * P:(i + 1) * P], identb[:])
                last.then_inc(s_pe, 1)

        attention_0(nc, locals())
        if STOP == "A":
            return store(nc, o_tiles, xs)
        with ExitStack() as moe:
            x_tok = sb("x_tok", [P, E, NT, 2, CAP], at=moe)
            eo_T = sb("eo_T", [P, B, E, CAP], at=moe)
            sel_w = sb("sel_w", [P, NT, E * CAP], at=moe)
            xnT_all = sb("xnT_all", [P, NT, P], at=moe)
            routing(nc, locals())
            experts(nc, locals())
            combine(nc, locals())
        if STOP == "B":
            return store(nc, o_tiles, xs)
        attention_1(nc, locals())
        if STOP == "C":
            return store(nc, o_tiles, xs)
        ffn_1(nc, locals(), o_tiles)


def store(nc, o_tiles, xs):
    with nc.semaphore("stored") as stored, nc.Block() as block:
        @block.sync
        def _(sp):
            sp.dma_start(o_tiles, xs[:]).then_inc(stored, 16)
            sp.wait_ge(stored, 16)


def attention_0(nc, v):
    xs, cs, mean, rstd, stats, neghalf, ident = (v[n] for n in "xs cs mean rstd stats neghalf ident".split())
    cols, rows, wq_a, wkv_a, wo_a, maskbias, ones = (
        v[n] for n in "cols rows wq_a wkv_a wo_a maskbias ones".split())
    NT, D, S, INNER, H0, HP, DH0, EPS = (v[n] for n in "NT D S INNER H0 HP DH0 EPS".split())
    with ExitStack() as ph, nc.Block() as block:
        def sb(name, shape, dt=F32):
            return ph.enter_context(nc.sbuf_tensor("a0_" + name, shape, dt))

        def pb(name):
            return ph.enter_context(nc.psum_tensor("a0_" + name, [P, 512], F32))

        def sem(name):
            return ph.enter_context(nc.semaphore("a0_" + name))

        xn = sb("xn", [P, 2, 2, D])
        kvT = sb("kvT", [P, 2, 4 * S])
        sq = sb("sq", [P, 2, INNER])
        ssq = sb("ssq", [P, 2, 3, H0])
        rn = sb("rn", [P, 2, 3, H0])
        qn = sb("qn", [P, 2, INNER])
        kn = sb("kn", [P, 2, INNER])
        qbd = sb("qbd", [P, 2, 2, HP, 2, S])
        kT = sb("kT", [P, 2, 2, HP, P])
        vaug = sb("vaug", [P, 2, 2, H0, DH0 + 1])
        mx = sb("mx", [P, 2, HP])
        pr = sb("pr", [P, 2, HP, P])
        prT = sb("prT", [P, 2, HP, P])
        rsum = sb("rsum", [P, 2, HP])
        att = sb("att", [P, 2, HP, DH0])
        attT = sb("attT", [P, 2, HP // 2, 2, 2, S])
        xb = sb("xb", [P, 2, D])
        yst = sb("yst", [P, 2, 6])
        ymv = sb("ymv", [P, 2, 2])
        yr = sb("yr", [P, 2, 1])
        yw = sb("yw", [P, 2, D])
        p_xT, p_w0, p_w1, p_tr, p_s, p_pT, p_o, p_y = (
            pb(n) for n in "xT w0 w1 tr s pT o y".split())
        proj_bank = (p_w0, p_w1)
        zeroed, xn_ready, xT_done, kvT_ready, proj_done, squared, reduced, normed, scaled, v_ready = (
            sem(n) for n in ("zeroed", "xn_ready", "xT_done", "kvT_ready", "proj_done", "squared", "reduced",
                             "normed", "scaled", "v_ready"))
        turned, turned_out, scored, shifted, exped, pT_done, prT_ready, mixed, att_ready, attT_done, attT_ready = (
            sem(n) for n in ("turned", "turned_out", "scored", "shifted", "exped", "pT_done", "prT_ready", "mixed",
                             "att_ready", "attT_done", "attT_ready"))
        y_done, y_stats, y_rstd, y_read, xb_ready, d_chain, y_chain, x_new, maxed, inverted = (
            sem(n) for n in ("y_done", "y_stats", "y_rstd", "y_read", "xb_ready", "d_chain", "y_chain", "x_new",
                             "maxed", "inverted"))

        Q, K0, V0, K1, V1 = range(5)

        @block.gpsimd
        def _(pool):
            nc.gpsimd.memset(qbd[:], 0.0).then_inc(zeroed, 1)
            nc.gpsimd.memset(vaug[:], 1.0).then_inc(zeroed, 1)

            def front(t, tp):
                for i in range(3):
                    pool.wait_ge(reduced, 3 * t + i + 1)
                    nc.gpsimd.tensor_tensor(rn[:, tp, i, :], ssq[:, tp, i, :], neghalf[:, 0:H0],
                                            ALU.pow).then_inc(normed, 1)

            def back(t, tp):
                wait(pool, x_new, t - 1)
                nc.gpsimd.tensor_tensor(xb[:, tp, :], xs[:, t, :], rows[:, 1, :], ALU.add).then_inc(xb_ready, 1)
                pool.wait_ge(y_stats, t + 1)
                nc.gpsimd.tensor_tensor(yr[:, tp, :], ymv[:, tp, 1:2], neghalf[:, 0:1], ALU.pow).then_inc(y_rstd, 1)

            pipelined(pool, NT, front, back)

        @block.tensor
        def _(pe):
            def xT(t, tp):
                pe.wait_ge(xn_ready, t + 1)
                wait(pe, kvT_ready, 2 * t)
                nc.tensor.transpose(p_xT[:, 0:P], xn[:, tp, 0, :], ident[:])
                nc.tensor.transpose(p_xT[:, P:2 * P], xn[:, tp, 1, :], ident[:]).then_inc(xT_done, 1)

            def project(t, tp, k):
                if k == Q:
                    pe.wait_ge(kvT_ready, 2 * t + 2)
                sem_, n = {Q: (scaled, 3 * t), K0: (v_ready, 2 * t), V0: (scaled, 3 * t + 1),
                           K1: (scaled, 3 * t + 2), V1: (v_ready, 2 * t + 1)}[k]
                wait(pe, sem_, n)
                bank = proj_bank[(5 * tp + k) % 2]
                if k == Q:
                    lhsT, rhs = kvT[:, tp, S:3 * S], wq_a[:]
                else:
                    b, is_v = (k - 1) // 2, (k - 1) % 2
                    lhsT, rhs = kvT[:, tp, b * 2 * S:(b + 1) * 2 * S], wkv_a[:, is_v * INNER:(is_v + 1) * INNER]
                nc.tensor.matmul(bank[:], lhsT, rhs, start=True, stop=True).then_inc(proj_done, 1)

            def turn(t, tp, i):
                pe.wait_ge(scaled, 3 * t + i + 1)
                wait(pe, turned_out, 4 * t + (0, 2, 3)[i])
                src = qn[:, tp, :] if i == 0 else kn[:, i - 1, :]
                for h in range(HP):
                    last = nc.tensor.transpose(p_tr[:, h * P:(h + 1) * P], src[:, h * P:(h + 1) * P], ident[:])
                last.then_inc(turned, 1)

            def scores(t, tp, b):
                pe.wait_ge(turned_out, 4 * t + 3 + b)
                wait(pe, shifted, 2 * t + b)
                nc.tensor.matmul(p_s[:], ones[:],
                                 maskbias[:, t, 2 * b:2 * b + 2, :].rearrange("o c s -> o (c s)").unsqueeze(1)
                                 .to_broadcast([1, HP, P]), start=True, stop=False, skip_group_check=True)
                for h in range(HP):
                    last = nc.tensor.matmul(p_s[:, h * P:(h + 1) * P], qbd[:, tp, b, h, :, :], kT[:, tp, b, h, :],
                                            start=False, stop=True, skip_group_check=True)
                last.then_inc(scored, 1)

            def probs_T(t, tp, b):
                pe.wait_ge(exped, 2 * t + b + 1)
                wait(pe, prT_ready, 2 * t + b)
                for h in range(HP):
                    last = nc.tensor.transpose(p_pT[:, h * P:(h + 1) * P], pr[:, b, h, :], ident[:])
                last.then_inc(pT_done, 1)

            def mix(t, tp, b):
                pe.wait_ge(prT_ready, 2 * t + b + 1)
                pe.wait_ge(v_ready, 2 * t + b + 1)
                wait(pe, att_ready, 2 * t + b)
                for h in range(HP):
                    for a in range(2):
                        last = nc.tensor.matmul(p_o[a * S:(a + 1) * S, h * (DH0 + 1):(h + 1) * (DH0 + 1)],
                                                prT[:, b, h, a * S:(a + 1) * S], vaug[:, tp, b, 2 * h + a, :],
                                                start=True, stop=True)
                last.then_inc(mixed, 1)

            def att_T(t, tp, b):
                pe.wait_ge(att_ready, 2 * t + b + 1)
                if b == 0:
                    wait(pe, y_read, t)
                else:
                    pe.wait_ge(attT_ready, 2 * t + 1)
                for j in range(HP // 2):
                    last = nc.tensor.transpose(p_y[:, j * P:(j + 1) * P],
                                               att[:, b, 2 * j:2 * j + 2, :], ident[:])
                last.then_inc(attT_done, 1)

            def out_proj(t, tp):
                pe.wait_ge(attT_ready, 2 * t + 2)
                for n in range(HP):
                    j, a = n // 2, n % 2
                    last = nc.tensor.matmul(p_y[:, 0:D], attT[:, tp, j, a, :, :], wo_a[:, j, a, :],
                                            start=(n == 0), stop=(n == HP - 1))
                last.then_inc(y_done, 1)

            pe.wait_ge(v["wa_in"], 16 * 6)

            def front(t, tp):
                xT(t, tp)
                for k in (Q, K0, V0):
                    project(t, tp, k)
                turn(t, tp, 0)
                project(t, tp, K1)
                turn(t, tp, 1)
                project(t, tp, V1)
                turn(t, tp, 2)

            def back(t, tp):
                scores(t, tp, 0)
                scores(t, tp, 1)
                probs_T(t, tp, 0)
                probs_T(t, tp, 1)
                mix(t, tp, 0)
                mix(t, tp, 1)
                att_T(t, tp, 0)
                att_T(t, tp, 1)
                out_proj(t, tp)

            def both(t, tp):
                f, fp = t + 1, 1 - tp
                scores(t, tp, 0)
                xT(f, fp)
                project(f, fp, Q)
                scores(t, tp, 1)
                project(f, fp, K0)
                probs_T(t, tp, 0)
                project(f, fp, V0)
                turn(f, fp, 0)
                probs_T(t, tp, 1)
                project(f, fp, K1)
                mix(t, tp, 0)
                turn(f, fp, 1)
                project(f, fp, V1)
                mix(t, tp, 1)
                att_T(t, tp, 0)
                turn(f, fp, 2)
                att_T(t, tp, 1)
                out_proj(t, tp)

            pipelined(pe, NT, front, back, both)

        @block.scalar
        def _(act):
            def affine(t, tp):
                act.wait_ge(xT_done, t + 1)
                wait(act, proj_done, 5 * (t - 1))
                groups = kvT[:, tp, :].rearrange("p (g s) -> p g s", g=4)
                for c, dst in ((0, groups[:, 0:4:3, :]), (1, groups[:, 1:3, :])):
                    nc.scalar.activation(dst, p_xT[:, c * P:(c + 1) * P].rearrange("p (b s) -> p b s", b=2),
                                         ACT.Identity, bias=cols[:, 2 * c + 1:2 * c + 2],
                                         scale=cols[:, 2 * c:2 * c + 1]).then_inc(kvT_ready, 1)

            def square(t, tp, i):
                k = (Q, K0, K1)[i]
                act.wait_ge(proj_done, 5 * t + k + 1)
                wait(act, reduced, 3 * t + i - 1)
                nc.scalar.activation(sq[:, (3 * tp + i) % 2, :], proj_bank[(5 * tp + k) % 2][:],
                                     ACT.Square).then_inc(squared, 1)

            def values(t, tp, b):
                k = (V0, V1)[b]
                act.wait_ge(proj_done, 5 * t + k + 1)
                if b == 0 and isinstance(t, int) and t == 0:
                    act.wait_ge(zeroed, 2)
                wait(act, mixed, 2 * (t - 2) + b + 1)
                nc.scalar.copy(vaug[:, tp, b, :, 0:DH0],
                               proj_bank[(5 * tp + k) % 2][:].rearrange("p (h d) -> p h d", h=H0)).then_inc(v_ready, 1)

            def queries_out(t, tp):
                act.wait_ge(turned, 3 * t + 1)
                wait(act, scored, 2 * (t - 1))
                for a in range(2):
                    nc.scalar.activation(qbd[a * S:(a + 1) * S, tp, :, :, a, :],
                                         p_tr[a * S:(a + 1) * S, :].rearrange("p (h b s) -> p b h s", h=HP, b=2),
                                         ACT.Copy).then_inc(turned_out, 1)

            def keys_out(t, tp, b):
                act.wait_ge(turned, 3 * t + 2 + b)
                wait(act, scored, 2 * (t - 2) + b + 1)
                nc.scalar.activation(kT[:, tp, b, :, :], p_tr[:].rearrange("p (h k) -> p h k", h=HP), ACT.Copy,
                                     scale=cols[:, 4:5]).then_inc(turned_out, 1)

            def exp(t, b):
                act.wait_ge(shifted, 2 * t + b + 1)
                nc.scalar.activation(pr[:, b], pr[:, b], ACT.Exp).then_inc(exped, 1)

            def probs_out(t, b):
                act.wait_ge(pT_done, 2 * t + b + 1)
                wait(act, mixed, 2 * (t - 1) + b + 1)
                nc.scalar.copy(prT[:, b].rearrange("p h k -> p (h k)"), p_pT[:]).then_inc(prT_ready, 1)

            def att_out(t, tp, b):
                act.wait_ge(attT_done, 2 * t + b + 1)
                wait(act, y_done, t - 1)
                nc.scalar.copy(attT[:, tp, :, :, b, :],
                               p_y[:, 0:HP // 2 * P].rearrange("p (j a s) -> p j a s", j=HP // 2, a=2)).then_inc(attT_ready, 1)

            def front(t, tp):
                affine(t, tp)
                square(t, tp, 0)
                square(t, tp, 1)
                values(t, tp, 0)
                queries_out(t, tp)
                square(t, tp, 2)
                keys_out(t, tp, 0)
                values(t, tp, 1)
                keys_out(t, tp, 1)

            def back(t, tp):
                exp(t, 0)
                probs_out(t, 0)
                exp(t, 1)
                probs_out(t, 1)
                att_out(t, tp, 0)
                att_out(t, tp, 1)

            def both(t, tp):
                f, fp = t + 1, 1 - tp
                affine(f, fp)
                exp(t, 0)
                square(f, fp, 0)
                square(f, fp, 1)
                probs_out(t, 0)
                exp(t, 1)
                values(f, fp, 0)
                queries_out(f, fp)
                probs_out(t, 1)
                square(f, fp, 2)
                keys_out(f, fp, 0)
                values(f, fp, 1)
                att_out(t, tp, 0)
                keys_out(f, fp, 1)
                att_out(t, tp, 1)

            act.wait_ge(zeroed, 1)
            pipelined(act, NT, front, back, both)

        @block.vector
        def _(dve):
            def normalise(t, tp):
                wait(dve, xT_done, t - 1)
                nc.vector.tensor_scalar(xn[:, tp, 0, :], cs[:, t, :], mean[:, 0, bass.ds(t, 1)], rstd[:, 0, bass.ds(t, 1)],
                                        ALU.subtract, ALU.mult)
                nc.vector.tensor_scalar(xn[:, tp, 1, :], xs[:, t, :], mean[:, 1, bass.ds(t, 1)], rstd[:, 1, bass.ds(t, 1)],
                                        ALU.subtract, ALU.mult).then_inc(xn_ready, 1)

            def reduce(t, tp, i):
                dve.wait_ge(squared, 3 * t + i + 1)
                n = d_count(t, i)
                wait(dve, normed, 3 * (t - 2) + i + 1)
                nc.vector.tensor_reduce(ssq[:, tp, i, :], sq[:, (3 * tp + i) % 2, :].rearrange("p (h d) -> p h d", h=H0),
                                        AX.X, ALU.add).then_inc(d_chain, 1)
                dve.wait_ge(d_chain, n)
                nc.vector.tensor_scalar(ssq[:, tp, i, :], ssq[:, tp, i, :], 1e-24, None, ALU.max).then_inc(reduced, 1)

            def d_count(t, i):
                return 3 * t + i + 1

            def scale(t, tp, i):
                k = (Q, K0, K1)[i]
                dve.wait_ge(normed, 3 * t + i + 1)
                if i == 0:
                    wait(dve, turned, 3 * (t - 2) + 1)
                    dst = qn[:, tp, :]
                else:
                    wait(dve, turned, 3 * (t - 1) + i + 1)
                    dst = kn[:, i - 1, :]
                nc.vector.tensor_tensor(dst.rearrange("p (h d) -> p h d", h=H0),
                                        proj_bank[(5 * tp + k) % 2][:].rearrange("p (h d) -> p h d", h=H0),
                                        rn[:, tp, i, :].unsqueeze(2).to_broadcast([P, H0, DH0]),
                                        ALU.mult).then_inc(scaled, 1)

            def shift(t, b):
                dve.wait_ge(scored, 2 * t + b + 1)
                s3 = p_s[:].rearrange("p (h k) -> p h k", h=HP)
                nc.vector.tensor_reduce(mx[:, b, :], s3, AX.X, ALU.max).then_inc(maxed, 1)
                dve.wait_ge(maxed, 2 * t + b + 1)
                wait(dve, pT_done, 2 * (t - 1) + b + 1)
                nc.vector.tensor_tensor(pr[:, b], s3, mx[:, b, :].unsqueeze(2).to_broadcast([P, HP, P]),
                                        ALU.subtract).then_inc(shifted, 1)

            def attend(t, b):
                dve.wait_ge(mixed, 2 * t + b + 1)
                o3 = p_o[:, 0:HP * (DH0 + 1)].rearrange("p (h d) -> p h d", h=HP)
                nc.vector.reciprocal(rsum[:, b, :], o3[:, :, DH0]).then_inc(inverted, 1)
                dve.wait_ge(inverted, 2 * t + b + 1)
                wait(dve, attT_done, 2 * (t - 1) + b + 1)
                nc.vector.tensor_tensor(att[:, b], o3[:, :, 0:DH0],
                                        rsum[:, b, :].unsqueeze(2).to_broadcast([P, HP, DH0]),
                                        ALU.mult).then_inc(att_ready, 1)

            def output(t, tp):
                dve.wait_ge(y_done, t + 1)
                y = Steps(dve, y_chain, 2 * t)
                y(nc.vector.bn_stats(yst[:, tp, :], p_y[:, 0:D]), carried=y_done)
                y(nc.vector.bn_aggr(ymv[:, tp, :], yst[:, tp, :]))
                nc.vector.tensor_scalar(ymv[:, tp, 1:2], ymv[:, tp, 1:2], EPS, None, ALU.add).then_inc(y_stats, 1)
                nc.vector.scalar_tensor_tensor(yw[:, tp, :], p_y[:, 0:D], ymv[:, tp, 0:1], rows[:, 0, :],
                                               ALU.subtract, ALU.mult).then_inc(y_read, 1)
                dve.wait_ge(y_read, t + 1)
                dve.wait_ge(y_rstd, t + 1)
                dve.wait_ge(xb_ready, t + 1)
                nc.vector.scalar_tensor_tensor(xs[:, t, :], yw[:, tp, :], yr[:, tp, :], xb[:, tp, :],
                                               ALU.mult, ALU.add).then_inc(x_new, 1)
                dve.wait_ge(x_new, t + 1)
                nc.vector.bn_stats(stats[:, 1, t, :], xs[:, t, :])

            def front(t, tp):
                normalise(t, tp)
                reduce(t, tp, 0)
                scale(t, tp, 0)
                reduce(t, tp, 1)
                scale(t, tp, 1)
                reduce(t, tp, 2)
                scale(t, tp, 2)

            def back(t, tp):
                shift(t, 0)
                shift(t, 1)
                attend(t, 0)
                attend(t, 1)
                output(t, tp)

            def both(t, tp):
                f, fp = t + 1, 1 - tp
                normalise(f, fp)
                shift(t, 0)
                reduce(f, fp, 0)
                shift(t, 1)
                scale(f, fp, 0)
                reduce(f, fp, 1)
                scale(f, fp, 1)
                attend(t, 0)
                reduce(f, fp, 2)
                scale(f, fp, 2)
                attend(t, 1)
                output(t, tp)

            pipelined(dve, NT, front, back, both)


def finish_stats(nc, dve, step, stats, mean, rstd, tmp, D, EPS):
    m_sum, m_dif, var = tmp[:, :, 0], tmp[:, :, 1], tmp[:, :, 2]
    step(nc.vector.tensor_tensor(m_sum, stats[:, 1, :, 1], stats[:, 1, :, 4], ALU.add))
    step(nc.vector.tensor_tensor(m_dif, stats[:, 1, :, 1], stats[:, 1, :, 4], ALU.subtract))
    step(nc.vector.tensor_scalar(mean[:, 1, :], m_sum, 0.5, None, ALU.mult))
    step(nc.vector.scalar_tensor_tensor(m_dif, m_dif, 0.25, m_dif, ALU.mult, ALU.mult))
    step(nc.vector.tensor_tensor(var, stats[:, 1, :, 2], stats[:, 1, :, 5], ALU.add))
    step(nc.vector.scalar_tensor_tensor(var, var, 1.0 / D, m_dif, ALU.mult, ALU.add))
    return nc.vector.tensor_scalar(rstd[:, 1, :], var, EPS, None, ALU.add)


def routing(nc, v):
    xs, mean, rstd, stats, neghalf, ident, tokid, gw_t = (
        v[n] for n in "xs mean rstd stats neghalf ident tokid gw_t".split())
    x_tok, sel_w, xnT_all, halves = (v[n] for n in "x_tok sel_w xnT_all halves".split())
    NT, D, S, E, CAP, EPS = (v[n] for n in "NT D S E CAP EPS".split())
    with ExitStack() as ph, nc.Block() as block:
        def sb(name, shape, dt=F32):
            return ph.enter_context(nc.sbuf_tensor("r_" + name, shape, dt))

        def pb(name):
            return ph.enter_context(nc.psum_tensor("r_" + name, [P, 512], F32))

        def sem(name):
            return ph.enter_context(nc.semaphore("r_" + name))

        tmp = sb("tmp", [P, NT, 4])
        xn = sb("xn", [P, 2, D])
        xnT = sb("xnT", [P, 2, P])
        negmax = sb("negmax", [P, 2, 1])
        ex = sb("ex", [P, 2, E])
        esum = sb("esum", [P, 2, 1])
        sc = sb("sc", [P, 2, E])
        scT = sb("scT", [E, 2, P])
        top = sb("top", [E, 2, 2, CAP])
        idx = sb("idx", [E, 2, 2, CAP], U32)
        idxf = sb("idxf", [E, 2, 2, CAP])
        spread = sb("spread", [E, 2, 2, E, CAP], BF16)
        spare = sb("spare", [P, 1])
        sel = sb("sel", [P, 2, E * CAP])
        p_T, p_L, p_sT, p_I, p_g0, p_g1 = (pb(n) for n in "T L sT I g0 g1".split())
        p_g = (p_g0, p_g1)
        (var_ready, norm_ready, chain, xn_ready, xT_done, xT_ready, xT_kept, logits_done, max_ready, exp_done,
         sc_ready, scT_done, scT_ready, top_chain, spread_ready, index_done, sel_ready, sel_w_ready, gathered,
         taken, inverse_ready) = (
            sem(n) for n in ("var_ready", "norm_ready", "chain", "xn_ready", "xT_done", "xT_ready", "xT_kept",
                             "logits_done", "max_ready", "exp_done", "sc_ready", "scT_done", "scT_ready",
                             "top_chain", "spread_ready", "index_done", "sel_ready", "sel_w_ready", "gathered",
                             "taken", "inverse_ready"))

        @block.gpsimd
        def _(pool):
            pool.wait_ge(var_ready, 1)
            nc.gpsimd.tensor_tensor(rstd[:, 1, :], rstd[:, 1, :], neghalf[:, 0:NT], ALU.pow).then_inc(norm_ready, 1)

            def keep(t, tp):
                pool.wait_ge(xT_ready, t + 1)
                nc.gpsimd.tensor_copy(xnT_all[:, t, :], xnT[:, tp, :]).then_inc(xT_kept, 1)

            pipelined(pool, NT, keep, lambda t, tp: None)

        @block.tensor
        def _(pe):
            def front(t, tp):
                pe.wait_ge(xn_ready, t + 1)
                wait(pe, xT_ready, t)
                nc.tensor.transpose(p_T[:, 0:P], xn[:, tp, :], ident[:]).then_inc(xT_done, 1)
                pe.wait_ge(xT_ready, t + 1)
                wait(pe, exp_done, t)
                nc.tensor.matmul(p_L[:, 0:E], xnT[:, tp, :], gw_t[:], start=True, stop=True).then_inc(logits_done, 1)

            def turn(t, tp):
                pe.wait_ge(sc_ready, t + 1)
                wait(pe, scT_ready, t)
                nc.tensor.transpose(p_sT[0:E, 0:P], sc[:, tp, :], ident[:]).then_inc(scT_done, 1)

            def gather(t, tp):
                pe.wait_ge(spread_ready, t + 1)
                wait(pe, sel_ready, t)
                for b in range(2):
                    last = nc.tensor.matmul(p_I[:, 0:E * CAP], halves[:, b, :],
                                            spread[:, tp, b].rearrange("e f c -> e (f c)"),
                                            start=(b == 0), stop=(b == 1))
                last.then_inc(index_done, 1)
                pe.wait_ge(sel_ready, t + 1)
                for b in range(2):
                    wait(pe, taken, 2 * t + b - 1 + (1 - b) * 0 if isinstance(t, int) and t == 0 else 2 * t)
                    nc.tensor.matmul(p_g[b][:, 0:E * CAP], xn[b * S:(b + 1) * S, tp, :], sel[b * S:(b + 1) * S, tp, :],
                                     start=True, stop=True).then_inc(gathered, 1)

            def back(t, tp):
                turn(t, tp)
                gather(t, tp)

            def both(t, tp):
                turn(t, tp)
                front(t + 1, 1 - tp)
                gather(t, tp)

            pipelined(pe, NT, front, back, both)

        @block.scalar
        def _(act):
            def front(t, tp):
                act.wait_ge(xT_done, t + 1)
                wait(act, logits_done, t - 1)
                wait(act, xT_kept, t - 1)
                nc.scalar.copy(xnT[:, tp, :], p_T[:, 0:P]).then_inc(xT_ready, 1)
                act.wait_ge(max_ready, t + 1)
                wait(act, sc_ready, t - 1)
                nc.scalar.activation(ex[:, tp, :], p_L[:, 0:E], ACT.Exp, bias=negmax[:, tp, :],
                                     accum_out=esum[:, tp, :]).then_inc(exp_done, 1)

            def back(t, tp):
                act.wait_ge(scT_done, t + 1)
                wait(act, spread_ready, t - 1)
                nc.scalar.copy(scT[:, tp, :], p_sT[0:E, 0:P]).then_inc(scT_ready, 1)

            def both(t, tp):
                back(t, tp)
                front(t + 1, 1 - tp)

            pipelined(act, NT, front, back, both)

        @block.vector
        def _(dve):
            finish_stats(nc, dve, Steps(dve, chain), stats, mean, rstd, tmp, D, EPS).then_inc(var_ready, 1)
            dve.wait_ge(norm_ready, 1)

            def front(t, tp):
                wait(dve, gathered, 2 * (t - 1))
                nc.vector.tensor_scalar(xn[:, tp, :], xs[:, t, :], mean[:, 1, bass.ds(t, 1)], rstd[:, 1, bass.ds(t, 1)],
                                        ALU.subtract, ALU.mult).then_inc(xn_ready, 1)
                dve.wait_ge(logits_done, t + 1)
                nc.vector.tensor_reduce(negmax[:, tp, :], p_L[:, 0:E], AX.X, ALU.max, negate=True).then_inc(max_ready, 1)
                dve.wait_ge(exp_done, t + 1)
                nc.vector.reciprocal(esum[:, tp, :], esum[:, tp, :]).then_inc(inverse_ready, 1)
                dve.wait_ge(inverse_ready, t + 1)
                nc.vector.tensor_scalar(sc[:, tp, :], ex[:, tp, :], esum[:, tp, :], None, ALU.mult).then_inc(sc_ready, 1)

            def choose(t, tp):
                dve.wait_ge(scT_ready, t + 1)
                nc.vector.memset(spare[:], 0.0)
                step = Steps(dve, top_chain, 4 * t)
                for b in range(2):
                    last = nc.vector.max(top[:, tp, b, :], scT[:, tp, b * S:(b + 1) * S])
                step(last)
                nc.vector.memset(spare[:], 0.0)
                for b in range(2):
                    last = nc.vector.max_index(idx[:, tp, b, :], top[:, tp, b, :], scT[:, tp, b * S:(b + 1) * S])
                step(last)
                step(nc.vector.tensor_copy(idxf[:, tp], idx[:, tp]))
                for b in range(2):
                    last = nc.vector.tensor_tensor(spread[:, tp, b], ident[0:E, 0:E].unsqueeze(2).to_broadcast([E, E, CAP]),
                                                   idxf[:, tp, b, :].unsqueeze(1).to_broadcast([E, E, CAP]), ALU.mult)
                    if b == 0:
                        step(last)
                last.then_inc(spread_ready, 1)

            def select(t, tp):
                dve.wait_ge(index_done, t + 1)
                nc.vector.tensor_scalar(sel[:, tp, :], p_I[:, 0:E * CAP], tokid[:], None, ALU.is_equal).then_inc(sel_ready, 1)
                dve.wait_ge(sel_ready, t + 1)
                nc.vector.tensor_tensor(sel_w[:, t, :].rearrange("p (e c) -> p e c", c=CAP),
                                        sel[:, tp, :].rearrange("p (e c) -> p e c", c=CAP),
                                        sc[:, tp, :].unsqueeze(2).to_broadcast([P, E, CAP]), ALU.mult).then_inc(sel_w_ready, 1)
                for b in range(2):
                    dve.wait_ge(gathered, 2 * t + b + 1)
                    nc.vector.tensor_copy(x_tok[:, :, t, b, :],
                                          p_g[b][:, 0:E * CAP].rearrange("p (e c) -> p e c", c=CAP)).then_inc(taken, 1)

            def back(t, tp):
                choose(t, tp)
                select(t, tp)

            def both(t, tp):
                choose(t, tp)
                front(t + 1, 1 - tp)
                select(t, tp)

            pipelined(dve, NT, front, back, both)


def experts(nc, v):
    ident, x_tok, eo_T, Wg, Wu, Wd = (v[n] for n in "ident x_tok eo_T Wg Wu Wd".split())
    NT, E, CAP, B = (v[n] for n in "NT E CAP B".split())
    N = B * CAP
    with ExitStack() as ph, nc.Block() as block:
        def sb(name, shape, dt=F32):
            return ph.enter_context(nc.sbuf_tensor("e_" + name, shape, dt))

        def pb(name):
            return ph.enter_context(nc.psum_tensor("e_" + name, [P, 512], F32))

        def sem(name):
            return ph.enter_context(nc.semaphore("e_" + name))

        w_nat = sb("w_nat", [P, 2, 6, P])
        w_T = sb("w_T", [P, 2, 6, P])
        hg = sb("hg", [P, 2, 2 * N])
        h = sb("h", [P, 2, 2 * N])
        p_w0, p_w1, p_g0, p_g1, p_u0, p_u1, p_e0, p_e1 = (pb(n) for n in "w0 w1 g0 g1 u0 u1 e0 e1".split())
        p_g, p_u, p_e = (p_g0, p_g1), (p_u0, p_u1), (p_e0, p_e1)
        w_in = (sem("w_in0"), sem("w_in1"))
        turned, wT_gu, wT_d, gate_done, up_done, act_done, h_ready, down_done, out_ready = (
            sem(n) for n in ("turned", "wT_gu", "wT_d", "gate_done", "up_done", "act_done", "h_ready", "down_done",
                             "out_ready"))

        @block.sync
        def _(sp):
            def load(e, ep, n):
                wait(sp, turned, 2 * (e - 1))
                sp.dma_start(w_nat[:, ep, 0:2, :], Wg[e].rearrange("(c p) d -> p c d", p=P)).then_inc(w_in[ep], 16)
                sp.dma_start(w_nat[:, ep, 2:4, :], Wu[e].rearrange("(c p) d -> p c d", p=P)).then_inc(w_in[ep], 16)
                sp.dma_start(w_nat[:, ep, 4:6, :], Wd[e].rearrange("d (c f) -> d c f", f=P)).then_inc(w_in[ep], 16)

            load(0, 0, 0)
            load(1, 1, 0)
            with sp.Fori(1, E // 2) as j:
                load(2 * j, 0, j)
                load(2 * j + 1, 1, j)

        @block.tensor
        def _(pe):
            def turn(e, ep, turns):
                pe.wait_ge(w_in[ep], 48 * (turns + 1))
                wait(pe, wT_gu, e)
                for i in range(4):
                    last = nc.tensor.transpose(p_w0[:, i * P:(i + 1) * P], w_nat[:, ep, i, :], ident[:])
                last.then_inc(turned, 1)
                wait(pe, wT_d, e)
                for i in range(2):
                    last = nc.tensor.transpose(p_w1[:, i * P:(i + 1) * P], w_nat[:, ep, 4 + i, :], ident[:])
                last.then_inc(turned, 1)

            def up(e, ep):
                pe.wait_ge(wT_gu, e + 1)
                tokens = x_tok[:, e].rearrange("p t b c -> p (t b c)")
                wait(pe, act_done, e - 1)
                for i in range(2):
                    last = nc.tensor.matmul(p_g[ep][:, i * N:(i + 1) * N], w_T[:, ep, i, :], tokens,
                                            start=True, stop=True)
                last.then_inc(gate_done, 1)
                wait(pe, h_ready, e - 1)
                for i in range(2):
                    last = nc.tensor.matmul(p_u[ep][:, i * N:(i + 1) * N], w_T[:, ep, 2 + i, :], tokens,
                                            start=True, stop=True)
                last.then_inc(up_done, 1)

            def down(e, ep):
                pe.wait_ge(h_ready, e + 1)
                pe.wait_ge(wT_d, e + 1)
                wait(pe, out_ready, e - 1)
                for i in range(2):
                    last = nc.tensor.matmul(p_e[ep][:, 0:N], w_T[:, ep, 4 + i, :], h[:, ep, i * N:(i + 1) * N],
                                            start=(i == 0), stop=(i == 1))
                last.then_inc(down_done, 1)

            def both(e, ep, turns):
                turn(e + 1, 1 - ep, turns)
                down(e, ep)
                up(e + 1, 1 - ep)

            turn(0, 0, 0)
            up(0, 0)
            both(0, 0, 0)
            both(1, 1, 1)
            with pe.Fori(1, E // 2 - 1) as j:
                both(2 * j, 0, j)
                both(2 * j + 1, 1, j + 1)
            both(E - 2, 0, E // 2 - 1)
            down(E - 1, 1)

        @block.scalar
        def _(act):
            def front(e, ep):
                act.wait_ge(turned, 2 * e + 1)
                wait(act, up_done, e - 1)
                nc.scalar.copy(w_T[:, ep, 0:4, :].rearrange("p i k -> p (i k)"), p_w0[:]).then_inc(wT_gu, 1)

            def gelu(e, ep):
                act.wait_ge(gate_done, e + 1)
                wait(act, h_ready, e - 1)
                nc.scalar.activation(hg[:, ep, :], p_g[ep][:], ACT.Gelu).then_inc(act_done, 1)

            pipelined(act, E, lambda e, ep: (front(e, ep), gelu(e, ep)), lambda e, ep: None)

        @block.vector
        def _(dve):
            def front(e, ep):
                dve.wait_ge(turned, 2 * e + 2)
                wait(dve, down_done, e - 1)
                nc.vector.tensor_copy(w_T[:, ep, 4:6, :].rearrange("p i k -> p (i k)"), p_w1[:, 0:2 * P]).then_inc(wT_d, 1)

            def product(e, ep):
                dve.wait_ge(act_done, e + 1)
                dve.wait_ge(up_done, e + 1)
                wait(dve, down_done, e - 1)
                nc.vector.tensor_tensor(h[:, ep, :], hg[:, ep, :], p_u[ep][:], ALU.mult).then_inc(h_ready, 1)

            def back(e, ep):
                dve.wait_ge(down_done, e + 1)
                nc.vector.tensor_copy(eo_T[:, :, e, :], p_e[ep][:, 0:N].rearrange("p (b c) -> p b c", c=CAP))\
                    .then_inc(out_ready, 1)

            def both(e, ep):
                front(e + 1, 1 - ep)
                back(e, ep)
                product(e + 1, 1 - ep)

            pipelined(dve, E, lambda e, ep: (front(e, ep), product(e, ep)), back, both)


def combine(nc, v):
    xs, stats, ident, gates, ws_t = (v[n] for n in "xs stats ident gates ws_t".split())
    eo_T, sel_w, xnT_all = (v[n] for n in "eo_T sel_w xnT_all".split())
    NT, D, S, E, CAP = (v[n] for n in "NT D S E CAP".split())
    with ExitStack() as ph, nc.Block() as block:
        def sb(name, shape, dt=F32):
            return ph.enter_context(nc.sbuf_tensor("c_" + name, shape, dt))

        def pb(name):
            return ph.enter_context(nc.psum_tensor("c_" + name, [P, 512], F32))

        def sem(name):
            return ph.enter_context(nc.semaphore("c_" + name))

        staged = sb("staged", [P, 2, 3, P])
        turned = sb("turned", [P, 2, 3, P])
        hg = sb("hg", [P, 2, 2 * P])
        h = sb("h", [P, 2, 2, P])
        p_t0, p_t1, p_h0, p_h1, p_y0, p_y1 = (pb(n) for n in "t0 t1 h0 h1 y0 y1".split())
        p_t, p_h, p_y = (p_t0, p_t1), (p_h0, p_h1), (p_y0, p_y1)
        stage_ready, turn_done, turn_ready, up_done, act_done, h_ready, y_done, x_new = (
            sem(n) for n in ("stage_ready", "turn_done", "turn_ready", "up_done", "act_done", "h_ready", "y_done", "x_new"))

        @block.gpsimd
        def _(pool):
            def stage(t, tp):
                wait(pool, turn_done, t - 1)
                nc.gpsimd.tensor_copy(staged[:, tp, 0:2, :],
                                      eo_T[:, bass.ds(2 * t, 2), :, :].rearrange("p b e c -> p b (e c)"))
                nc.gpsimd.tensor_copy(staged[:, tp, 2, :], sel_w[:, t, :]).then_inc(stage_ready, 1)

            pipelined(pool, NT, stage, lambda t, tp: None)

        @block.tensor
        def _(pe):
            def front(t, tp):
                pe.wait_ge(stage_ready, t + 1)
                wait(pe, turn_ready, t - 1)
                for i in range(3):
                    last = nc.tensor.transpose(p_t[tp][:, i * P:(i + 1) * P], staged[:, tp, i, :], ident[:])
                last.then_inc(turn_done, 1)
                wait(pe, h_ready, t - 1)
                for i in range(4):
                    last = nc.tensor.matmul(p_h[tp][:, i * P:(i + 1) * P], ws_t[:, i, :], xnT_all[:, t, :],
                                            start=True, stop=True)
                last.then_inc(up_done, 1)

            def back(t, tp):
                pe.wait_ge(h_ready, t + 1)
                pe.wait_ge(turn_ready, t + 1)
                wait(pe, x_new, t - 1)
                for i in range(2):
                    nc.tensor.matmul(p_y[tp][:, 0:D], h[:, tp, i, :], ws_t[:, 4 + i, :], start=(i == 0), stop=False,
                                     skip_group_check=True)
                for b in range(2):
                    last = nc.tensor.matmul(p_y[tp][b * S:(b + 1) * S, 0:D], turned[:, tp, 2, b * S:(b + 1) * S],
                                            turned[:, tp, b, :], start=False, stop=True, skip_group_check=True)
                last.then_inc(y_done, 1)

            pipelined(pe, NT, front, back)

        @block.scalar
        def _(act):
            def front(t, tp):
                act.wait_ge(turn_done, t + 1)
                wait(act, y_done, t - 1)
                nc.scalar.copy(turned[:, tp].rearrange("p i k -> p (i k)"), p_t[tp][:, 0:3 * P]).then_inc(turn_ready, 1)
                act.wait_ge(up_done, t + 1)
                wait(act, h_ready, t - 1)
                nc.scalar.activation(hg[:, tp, :], p_h[tp][:, 0:2 * P], ACT.Gelu).then_inc(act_done, 1)

            pipelined(act, NT, front, lambda t, tp: None)

        @block.vector
        def _(dve):
            def front(t, tp):
                dve.wait_ge(act_done, t + 1)
                wait(dve, y_done, t - 1)
                nc.vector.tensor_tensor(h[:, tp].rearrange("p i k -> p (i k)"), hg[:, tp, :], p_h[tp][:, 2 * P:4 * P],
                                        ALU.mult).then_inc(h_ready, 1)

            def back(t, tp):
                dve.wait_ge(y_done, t + 1)
                nc.vector.scalar_tensor_tensor(xs[:, t, :], p_y[tp][:, 0:D], gates[:, 2:3], xs[:, t, :],
                                               ALU.mult, ALU.add).then_inc(x_new, 1)
                dve.wait_ge(x_new, t + 1)
                nc.vector.bn_stats(stats[:, 1, t, :], xs[:, t, :])

            pipelined(dve, NT, front, back)


def attention_1(nc, v):
    xs, cs, mean, rstd, stats, neghalf, ident, fold, half, quad = (
        v[n] for n in "xs cs mean rstd stats neghalf ident fold half quad".split())
    cols, rows, w_c = (v[n] for n in "cols rows w_c".split())
    NT, D, S, EPS = (v[n] for n in "NT D S EPS".split())
    G, DH = 4, 8
    with ExitStack() as ph, nc.Block() as block:
        def sb(name, shape, dt=F32):
            return ph.enter_context(nc.sbuf_tensor("a1_" + name, shape, dt))

        def pb(name, shape=(P, 512)):
            return ph.enter_context(nc.psum_tensor("a1_" + name, list(shape), F32))

        def sem(name):
            return ph.enter_context(nc.semaphore("a1_" + name))

        tmp = sb("tmp", [P, NT, 4])
        xn = sb("xn", [P, 2, 2, D])
        cT = sb("cT", [P, 2, 2, 2, S])
        xT = sb("xT", [P, 2, P])
        q = sb("q", [P, 2, 2, S])
        k = sb("k", [P, 2, 2, S])
        q4 = sb("q4", [P, 2, 2, 4, S])
        vals = sb("vals", [P, 2, 2, G, 2, 2, DH + 1])
        mx = sb("mx", [P, 2, G, 4])
        pr = sb("pr", [P, 2, G, 2, 2, S])
        prT = sb("prT", [P, 2, G, P])
        rs = sb("rs", [P, 2, 2 * G * 4])
        att = sb("att", [P, 2, 2, D])
        oT = sb("oT", [P, 2, 2 * S])
        xb = sb("xb", [P, 2, D])
        p_s = pb("s", (P, G, 512))
        p_T, p_qkv, p_pT, p_o = (pb(n) for n in "T qkv pT o".split())
        WIDE = 4 * (DH + 1)
        (var_ready, norm_ready, chain, zeroed, c_ready, xn_ready, turned, turned_out, qkv_done, q_ready, k_ready,
         q4_ready, v_ready, scored, maxed, shifted, exped, pT_done, prT_ready, mixed, inverse, att_ready, folded,
         oT_ready, y_done, xb_ready, x_new) = (
            sem(n) for n in ("var_ready", "norm_ready", "chain", "zeroed", "c_ready", "xn_ready", "turned",
                             "turned_out", "qkv_done", "q_ready", "k_ready", "q4_ready", "v_ready", "scored", "maxed",
                             "shifted", "exped", "pT_done", "prT_ready", "mixed", "inverse", "att_ready", "folded",
                             "oT_ready", "y_done", "xb_ready", "x_new"))

        @block.gpsimd
        def _(pool):
            pool.wait_ge(var_ready, 1)
            nc.gpsimd.tensor_tensor(rstd[:, 1, :], rstd[:, 1, :], neghalf[:, 0:NT], ALU.pow).then_inc(norm_ready, 1)

            def front(t, tp):
                wait(pool, turned, t - 1)
                nc.gpsimd.tensor_copy(xn[:, tp, 0, :], cs[:, t, :]).then_inc(c_ready, 1)
                pool.wait_ge(q_ready, t + 1)
                wait(pool, scored, t - 1)
                for b in range(2):
                    last = nc.gpsimd.tensor_tensor(q4[:, tp, b], q[:, tp, b, :].unsqueeze(1).to_broadcast([P, 4, S]),
                                                   quad[:].unsqueeze(2).to_broadcast([P, 4, S]), ALU.mult)
                last.then_inc(q4_ready, 1)

            def back(t, tp):
                wait(pool, x_new, t - 1)
                nc.gpsimd.tensor_tensor(xb[:, tp, :], xs[:, t, :], rows[:, 2, :], ALU.add).then_inc(xb_ready, 1)

            pipelined(pool, NT, front, back)

        @block.tensor
        def _(pe):
            def turn(t, tp):
                pe.wait_ge(c_ready, t + 1)
                pe.wait_ge(xn_ready, t + 1)
                wait(pe, turned_out, 2 * t)
                nc.tensor.transpose(p_T[:, 0:P], xn[:, tp, 0, :], ident[:])
                nc.tensor.transpose(p_T[:, P:2 * P], xn[:, tp, 1, :], ident[:]).then_inc(turned, 1)

            def project(t, tp):
                pe.wait_ge(turned_out, 2 * t + 2)
                wait(pe, k_ready, t)
                wait(pe, v_ready, 4 * t)
                nc.tensor.matmul(p_qkv[:, 0:P], w_c[:, 0, :], xT[:, tp, :], start=True, stop=True)
                nc.tensor.matmul(p_qkv[:, P:2 * P], w_c[:, 1, :], cT[:, tp, :, 0, :], start=True, stop=True)
                for b in range(2):
                    last = nc.tensor.matmul(p_qkv[:, (2 + b) * P:(3 + b) * P], cT[:, tp, b].rearrange("p c s -> p (c s)"),
                                            w_c[:, 2, :], start=True, stop=True)
                last.then_inc(qkv_done, 1)

            def scores(t, tp):
                pe.wait_ge(q4_ready, t + 1)
                pe.wait_ge(k_ready, t + 1)
                wait(pe, shifted, t)
                for b in range(2):
                    for c in range(2):
                        for g in range(G):
                            r = slice(32 * g, 32 * g + 32)
                            last = nc.tensor.matmul(p_s[:, g, (2 * b + c) * S:(2 * b + c + 1) * S],
                                                    q4[r, tp, b, 2 * c:2 * c + 2, :].rearrange("p h s -> p (h s)"),
                                                    k[r, tp, b, :], start=True, stop=True)
                last.then_inc(scored, 1)

            def probs_T(t, tp, b):
                pe.wait_ge(exped, t + 1)
                wait(pe, prT_ready, 2 * t + b)
                for g in range(G):
                    last = nc.tensor.transpose(p_pT[:, g * P:(g + 1) * P], pr[:, tp, g, b].rearrange("p c s -> p (c s)"),
                                               ident[:])
                last.then_inc(pT_done, 1)

            def mix(t, tp, b):
                pe.wait_ge(prT_ready, 2 * t + b + 1)
                pe.wait_ge(v_ready, 4 * t + 4)
                wait(pe, x_new, t)
                for g in range(G):
                    last = nc.tensor.matmul(p_o[:, (b * G + g) * WIDE:(b * G + g + 1) * WIDE], prT[:, b, g, :],
                                            vals[:, tp, b, g].rearrange("p c h e -> p (c h e)"), start=True, stop=True)
                last.then_inc(mixed, 1)

            def out(t, tp):
                pe.wait_ge(att_ready, t + 1)
                for b in range(2):
                    last = nc.tensor.matmul(p_o[:, 320 + b * S:320 + (b + 1) * S], att[:, tp, b, :], fold[:],
                                            start=True, stop=True)
                last.then_inc(folded, 1)
                pe.wait_ge(oT_ready, t + 1)
                nc.tensor.matmul(p_o[:, 0:D], oT[:, tp, :], w_c[:, 3, :], start=True, stop=True).then_inc(y_done, 1)

            def front(t, tp):
                turn(t, tp)
                project(t, tp)
                scores(t, tp)

            def back(t, tp):
                probs_T(t, tp, 0)
                probs_T(t, tp, 1)
                mix(t, tp, 0)
                mix(t, tp, 1)
                out(t, tp)

            def both(t, tp):
                f, fp = t + 1, 1 - tp
                turn(f, fp)
                probs_T(t, tp, 0)
                project(f, fp)
                probs_T(t, tp, 1)
                mix(t, tp, 0)
                scores(f, fp)
                mix(t, tp, 1)
                out(t, tp)

            pe.wait_ge(zeroed, 2)
            pipelined(pe, NT, front, back, both)

        @block.scalar
        def _(act):
            def turn_out(t, tp):
                act.wait_ge(turned, t + 1)
                wait(act, qkv_done, t - 1)
                nc.scalar.copy(cT[:, tp], p_T[:, 0:P].rearrange("p (b s) -> p b s", b=2).unsqueeze(2)
                               .to_broadcast([P, 2, 2, S])).then_inc(turned_out, 1)
                nc.scalar.copy(xT[:, tp, :], p_T[:, P:2 * P]).then_inc(turned_out, 1)

            def qkv_out(t, tp):
                act.wait_ge(qkv_done, t + 1)
                wait(act, q4_ready, t - 1)
                nc.scalar.activation(q[:, tp].rearrange("p b s -> p (b s)"), p_qkv[:, 0:P], ACT.Identity,
                                     bias=cols[:, 5:6], scale=DH ** -0.5).then_inc(q_ready, 1)
                wait(act, scored, t - 1)
                nc.scalar.activation(k[:, tp].rearrange("p b s -> p (b s)"), p_qkv[:, P:2 * P], ACT.Identity,
                                     bias=cols[:, 6:7]).then_inc(k_ready, 1)
                wait(act, mixed, 2 * (t - 1))
                for b in range(2):
                    for a in range(2):
                        src = p_qkv[a * S:(a + 1) * S, (2 + b) * P:(3 + b) * P].rearrange("p (g c h e) -> p g c h e", g=G, c=2, h=2)
                        nc.scalar.copy(vals[a * S:(a + 1) * S, tp, b, :, a, :, 0:DH], src[:, :, a]).then_inc(v_ready, 1)

            def exp(t, tp):
                act.wait_ge(shifted, t + 1)
                flat = pr[:, tp].rearrange("p g b c s -> p (g b c s)")
                nc.scalar.activation(flat, flat, ACT.Exp).then_inc(exped, 1)

            def probs_out(t, b):
                act.wait_ge(pT_done, 2 * t + b + 1)
                wait(act, mixed, 2 * (t - 1) + b + 1)
                nc.scalar.copy(prT[:, b].rearrange("p g k -> p (g k)"), p_pT[:]).then_inc(prT_ready, 1)

            def att_out(t, tp):
                act.wait_ge(folded, t + 1)
                wait(act, y_done, t - 1)
                nc.scalar.activation(oT[:, tp, :], p_o[:, 320:320 + P], ACT.Identity, bias=cols[:, 7:8]).then_inc(oT_ready, 1)

            def front(t, tp):
                turn_out(t, tp)
                qkv_out(t, tp)
                exp(t, tp)

            def back(t, tp):
                probs_out(t, 0)
                probs_out(t, 1)
                att_out(t, tp)

            def both(t, tp):
                f, fp = t + 1, 1 - tp
                turn_out(f, fp)
                probs_out(t, 0)
                qkv_out(f, fp)
                probs_out(t, 1)
                exp(f, fp)
                att_out(t, tp)

            act.wait_ge(zeroed, 2)
            pipelined(act, NT, front, back, both)

        @block.vector
        def _(dve):
            finish_stats(nc, dve, Steps(dve, chain), stats, mean, rstd, tmp, D, EPS).then_inc(var_ready, 1)
            nc.vector.memset(vals[:], 0.0).then_inc(zeroed, 1)
            dve.wait_ge(zeroed, 1)
            for a in range(2):
                last = nc.vector.memset(vals[a * S:(a + 1) * S, :, :, :, a, :, DH:DH + 1].rearrange("p x b g h o -> p (x b g) (h o)"), 1.0)
            last.then_inc(zeroed, 1)
            dve.wait_ge(norm_ready, 1)
            s4 = p_s[:, :, 0:4 * S].rearrange("p g (i s) -> p g i s", s=S)

            def normalise(t, tp):
                wait(dve, turned, t - 1)
                nc.vector.tensor_scalar(xn[:, tp, 1, :], xs[:, t, :], mean[:, 1, bass.ds(t, 1)], rstd[:, 1, bass.ds(t, 1)],
                                        ALU.subtract, ALU.mult).then_inc(xn_ready, 1)

            def shift(t, tp):
                dve.wait_ge(scored, t + 1)
                nc.vector.tensor_reduce(mx[:, tp], s4, AX.X, ALU.max).then_inc(maxed, 1)
                dve.wait_ge(maxed, t + 1)
                wait(dve, pT_done, 2 * (t - 1))
                nc.vector.tensor_tensor(pr[:, tp].rearrange("p g b c s -> p g (b c) s"), s4,
                                        mx[:, tp].unsqueeze(3).to_broadcast([P, G, 4, S]),
                                        ALU.subtract).then_inc(shifted, 1)

            def attend(t, tp):
                dve.wait_ge(mixed, 2 * t + 2)
                o3 = p_o[:, 0:2 * G * WIDE].rearrange("p (n e) -> p n e", e=DH + 1)
                step = Steps(dve, inverse, 2 * t)
                step(nc.vector.reciprocal(rs[:, tp, :], o3[:, :, DH]))
                step(nc.vector.tensor_tensor(rs[:, tp, :].rearrange("p (n h) -> p n h", h=2),
                                             rs[:, tp, :].rearrange("p (n h) -> p n h", h=2),
                                             half[:].unsqueeze(1).to_broadcast([P, 4 * G, 2]), ALU.mult))
                wait(dve, folded, t - 1)
                nc.vector.tensor_tensor(att[:, tp].rearrange("p b (n e) -> p (b n) e", e=DH), o3[:, :, 0:DH],
                                        rs[:, tp, :].unsqueeze(2).to_broadcast([P, 8 * G, DH]), ALU.mult).then_inc(att_ready, 1)

            def output(t, tp):
                dve.wait_ge(y_done, t + 1)
                dve.wait_ge(xb_ready, t + 1)
                nc.vector.tensor_tensor(xs[:, t, :], p_o[:, 0:D], xb[:, tp, :], ALU.add).then_inc(x_new, 1)
                dve.wait_ge(x_new, t + 1)
                nc.vector.bn_stats(stats[:, 1, t, :], xs[:, t, :])

            def front(t, tp):
                normalise(t, tp)
                shift(t, tp)

            def back(t, tp):
                attend(t, tp)
                output(t, tp)

            def both(t, tp):
                normalise(t + 1, 1 - tp)
                shift(t + 1, 1 - tp)
                attend(t, tp)
                output(t, tp)

            pipelined(dve, NT, front, back, both)


def ffn_1(nc, v, o_tiles):
    xs, mean, rstd, stats, neghalf, identb = (v[n] for n in "xs mean rstd stats neghalf identb".split())
    gates, rows, b1row, w1_t, w2_t, wmean = (v[n] for n in "gates rows b1row w1_t w2_t wmean".split())
    NT, D, FF, EPS, MAGIC = (v[n] for n in "NT D FF EPS MAGIC".split())
    C = FF // P
    with ExitStack() as ph, nc.Block() as block:
        def sb(name, shape, dt=F32):
            return ph.enter_context(nc.sbuf_tensor("f_" + name, shape, dt))

        def pb(name, dt=F32, n=512):
            return ph.enter_context(nc.psum_tensor("f_" + name, [P, n], dt))

        def sem(name):
            return ph.enter_context(nc.semaphore("f_" + name))

        tmp = sb("tmp", [P, NT, 4])
        hn = sb("hn", [P, 2, D])
        hq = sb("hq", [P, 2, D], BF16)
        hT = sb("hT", [P, 2, P], BF16)
        hid = sb("hid", [P, 2, FF])
        ge = sb("ge", [P, 2, FF])
        gq = sb("gq", [P, 2, FF], BF16)
        gT = sb("gT", [P, 2, C, P], BF16)
        small = sb("small", [P, 2, 2, 4])
        wback = sb("wback", [P, 2])
        xb = sb("xb", [P, 2, D])
        p_a0, p_a1 = pb("a0", BF16, 1024), pb("a1", BF16, 1024)
        p_b0, p_b1 = pb("b0", BF16, 1024), pb("b1", BF16, 1024)
        p_h0, p_h1, p_y0, p_y1 = (pb(n) for n in "h0 h1 y0 y1".split())
        p_a, p_b, p_h, p_y = (p_a0, p_a1), (p_b0, p_b1), (p_h0, p_h1), (p_y0, p_y1)
        (var_ready, norm_ready, chain, norm_chain, hq_ready, aT_done, aT_ready, up_done, hid_ready, gelu_done,
         quant_chain, gq_ready, bT_done, bT_ready, y_done, xb_ready, x_new, stored) = (
            sem(n) for n in ("var_ready", "norm_ready", "chain", "norm_chain", "hq_ready", "aT_done", "aT_ready",
                             "up_done", "hid_ready", "gelu_done", "quant_chain", "gq_ready", "bT_done", "bT_ready",
                             "y_done", "xb_ready", "x_new", "stored"))

        @block.sync
        def _(sp):
            with sp.Fori(0, NT) as t:
                sp.wait_ge(x_new, t + 1)
                sp.dma_start(o_tiles[:, t, :], xs[:, t, :]).then_inc(stored, 16)
            sp.wait_ge(stored, 16 * NT)

        @block.gpsimd
        def _(pool):
            pool.wait_ge(var_ready, 1)
            nc.gpsimd.tensor_tensor(rstd[:, 1, :], rstd[:, 1, :], neghalf[:, 0:NT], ALU.pow).then_inc(norm_ready, 1)

            def front(t, tp):
                wait(pool, x_new, t - 1)
                nc.gpsimd.tensor_tensor(xb[:, tp, :], xs[:, t, :], rows[:, 3, :], ALU.add).then_inc(xb_ready, 1)

            pipelined(pool, NT, front, lambda t, tp: None)

        @block.tensor
        def _(pe):
            def turn(t, tp):
                pe.wait_ge(hq_ready, t + 1)
                wait(pe, aT_ready, t - 1)
                nc.tensor.transpose(p_a[tp][:, 0:P], hq[:, tp, :], identb[:]).then_inc(aT_done, 1)

            def up(t, tp):
                pe.wait_ge(aT_ready, t + 1)
                wait(pe, hid_ready, t - 1)
                nc.tensor.matmul(p_h[tp][:], hT[:, tp, :], w1_t[:], start=True, stop=True).then_inc(up_done, 1)

            def turn_hidden(t, tp):
                pe.wait_ge(gq_ready, t + 1)
                wait(pe, bT_ready, t - 1)
                for c in range(C):
                    last = nc.tensor.transpose(p_b[tp][:, c * P:(c + 1) * P], gq[:, tp, c * P:(c + 1) * P], identb[:])
                last.then_inc(bT_done, 1)

            def down(t, tp):
                pe.wait_ge(bT_ready, t + 1)
                wait(pe, x_new, t - 1)
                for c in range(C):
                    last = nc.tensor.matmul(p_y[tp][:, 0:D], gT[:, tp, c, :], w2_t[:, c, :], start=(c == 0), stop=(c == C - 1))
                last.then_inc(y_done, 1)

            def both(t, tp):
                turn(t + 1, 1 - tp)
                turn_hidden(t, tp)
                up(t + 1, 1 - tp)
                down(t, tp)

            pipelined(pe, NT, lambda t, tp: (turn(t, tp), up(t, tp)),
                      lambda t, tp: (turn_hidden(t, tp), down(t, tp)), both)

        @block.scalar
        def _(act):
            def front(t, tp):
                act.wait_ge(aT_done, t + 1)
                wait(act, up_done, t - 1)
                nc.scalar.copy(hT[:, tp, :], p_a[tp][:, 0:P]).then_inc(aT_ready, 1)

            def gelu(t, tp):
                act.wait_ge(hid_ready, t + 1)
                wait(act, gq_ready, t - 1)
                nc.scalar.activation(ge[:, tp, :], hid[:, tp, :], ACT.Gelu).then_inc(gelu_done, 1)

            def back(t, tp):
                act.wait_ge(bT_done, t + 1)
                wait(act, y_done, t - 1)
                nc.scalar.copy(gT[:, tp].rearrange("p c k -> p (c k)"), p_b[tp][:, 0:FF]).then_inc(bT_ready, 1)

            def both(t, tp):
                front(t + 1, 1 - tp)
                back(t, tp)
                gelu(t + 1, 1 - tp)

            pipelined(act, NT, lambda t, tp: (front(t, tp), gelu(t, tp)), back, both)

        @block.vector
        def _(dve):
            step = Steps(dve, chain)
            step(nc.vector.tensor_scalar(wback[:], wmean[:], 1.0 / 127.0, None, ALU.mult))
            step(nc.vector.tensor_scalar(wback[:, 1:2], wback[:, 1:2], gates[:, 3:4], None, ALU.mult))
            finish_stats(nc, dve, step, stats, mean, rstd, tmp, D, EPS).then_inc(var_ready, 1)
            dve.wait_ge(norm_ready, 1)

            def quantise(step, src, dst, sm, layer):
                step(nc.vector.tensor_reduce(sm[:, 0:1], src, AX.X, ALU.max, apply_absolute_value=True))
                step(nc.vector.tensor_scalar(sm[:, 0:1], sm[:, 0:1], EPS, None, ALU.max))
                step(nc.vector.reciprocal(sm[:, 1:2], sm[:, 0:1]))
                step(nc.vector.tensor_scalar(sm[:, 2:3], sm[:, 0:1], wback[:, layer:layer + 1], None, ALU.mult))
                step(nc.vector.tensor_scalar(sm[:, 1:2], sm[:, 1:2], 127.0, None, ALU.mult))
                step(nc.vector.tensor_scalar(src, src, sm[:, 1:2], MAGIC, ALU.mult, ALU.add))
                return nc.vector.tensor_scalar(dst, src, MAGIC, 127.0, ALU.subtract, ALU.min)

            def norm(t, tp):
                step = Steps(dve, norm_chain, 8 * t)
                step(nc.vector.scalar_tensor_tensor(hn[:, tp, :], xs[:, t, :], mean[:, 1, bass.ds(t, 1)], rows[:, 4, :],
                                                    ALU.subtract, ALU.mult))
                step(nc.vector.scalar_tensor_tensor(hn[:, tp, :], hn[:, tp, :], rstd[:, 1, bass.ds(t, 1)], rows[:, 5, :],
                                                    ALU.mult, ALU.add))
                wait(dve, aT_done, t - 1)
                quantise(step, hn[:, tp, :], hq[:, tp, :], small[:, tp, 0, :], 0).then_inc(hq_ready, 1)

            def hidden(t, tp):
                dve.wait_ge(up_done, t + 1)
                wait(dve, gelu_done, t - 1)
                nc.vector.scalar_tensor_tensor(hid[:, tp, :], p_h[tp][:], small[:, tp, 0, 2:3], v["b1row"][:],
                                               ALU.mult, ALU.add).then_inc(hid_ready, 1)

            def requantise(t, tp):
                dve.wait_ge(gelu_done, t + 1)
                wait(dve, bT_done, t - 1)
                quantise(Steps(dve, quant_chain, 6 * t), ge[:, tp, :], gq[:, tp, :], small[:, tp, 1, :], 1)\
                    .then_inc(gq_ready, 1)

            def output(t, tp):
                dve.wait_ge(y_done, t + 1)
                dve.wait_ge(xb_ready, t + 1)
                nc.vector.scalar_tensor_tensor(xs[:, t, :], p_y[tp][:, 0:D], small[:, tp, 1, 2:3], xb[:, tp, :],
                                               ALU.mult, ALU.add).then_inc(x_new, 1)

            def both(t, tp):
                norm(t + 1, 1 - tp)
                requantise(t, tp)
                hidden(t + 1, 1 - tp)
                output(t, tp)

            pipelined(dve, NT, lambda t, tp: (norm(t, tp), hidden(t, tp)),
                      lambda t, tp: (requantise(t, tp), output(t, tp)), both)


_INS = ["x", "ctx_1024", "mask_BxS2_bk0", "g_xattn", "g_ffn",
        "L0_xattn_ln_x_w", "L0_xattn_ln_x_b", "L0_xattn_ln_l_w", "L0_xattn_ln_l_b", "L0_xattn_Wq", "L0_xattn_Wkv",
        "L0_xattn_q_scale", "L0_xattn_k_scale", "L0_xattn_Wo", "L0_xattn_ln_o_w", "L0_xattn_ln_o_b",
        "L0_ffn_gate_w", "L0_ffn_Wg", "L0_ffn_Wu", "L0_ffn_Wd", "L0_ffn_Ws_g", "L0_ffn_Ws_u", "L0_ffn_Ws_d",
        "L1_xattn_wq_w", "L1_xattn_wq_b", "L1_xattn_wk_w", "L1_xattn_wk_b", "L1_xattn_wv_w", "L1_xattn_wv_b",
        "L1_xattn_wo_w", "L1_xattn_wo_b", "L1_ffn_w1", "L1_ffn_b1", "L1_ffn_w2", "L1_ffn_b2", "L1_ffn_gamma",
        "L1_ffn_beta"]
_OUTS = [((32, 64, 128), "float32")]


def kernel(**inputs):
    import numpy as _np
    import concourse.bacc as _bacc
    from concourse import mybir as _mybir
    from concourse.bass_utils import run_bass_kernel_spmd as _run

    nc = _bacc.Bacc("TRN2", target_bir_lowering=False, num_devices=1)
    arrays, args = {}, []
    for name in _INS:
        a = _np.ascontiguousarray(inputs[name])
        arrays[f"in_{name}_dram"] = a
        args.append(nc.dram_tensor(f"in_{name}_dram", a.shape, _mybir.dt.from_np(a.dtype), kind="ExternalInput").ap())
    for i, (shape, dtype) in enumerate(_OUTS):
        dt = _mybir.dt.from_np(_np.dtype(dtype))
        args.append(nc.dram_tensor(f"out_{i}_dram", shape, dt, kind="ExternalOutput").ap())
    build(nc, *args)
    r = _run(nc, [arrays], core_ids=[0])
    got = tuple(r.results[0][f"out_{i}_dram"] for i in range(len(_OUTS)))
    return got[0]
```

```python
from contextlib import ExitStack

import concourse.bass as bass
from concourse import mybir

ALU = mybir.AluOpType
ACT = mybir.ActivationFunctionType
AX = mybir.AxisListType
F32 = mybir.dt.float32
BF16 = mybir.dt.bfloat16
U8 = mybir.dt.uint8
U32 = mybir.dt.uint32

P = 128
STOP = "D"


def wait(eng, sem, count):
    if isinstance(count, int) and count <= 0:
        return
    eng.wait_ge(sem, count)


class Steps:

    def __init__(self, eng, sem, base=0):
        self.eng, self.sem, self.base, self.n = eng, sem, base, 0

    def __call__(self, ins):
        self.n += 1
        ins.then_inc(self.sem, 1)
        self.eng.wait_ge(self.sem, self.base + self.n)


def pipelined(eng, tiles, front, back, both=None):
    if both is None:
        def both(t, tp):
            front(t + 1, 1 - tp)
            back(t, tp)
    front(0, 0)
    both(0, 0)
    both(1, 1)
    with eng.Fori(1, (tiles - 2) // 2) as j:
        both(2 * j, 0)
        both(2 * j + 1, 1)
    both(tiles - 2, 0)
    back(tiles - 1, 1)


def turns(eng, tiles, turn, first, last):
    for s in range(first, 3):
        turn(s, s % 2)
    ahead = -first
    passes = (tiles - ahead - 3) // 2
    with eng.Fori(0, passes) as j:
        turn(2 * j + 3, 1)
        turn(2 * j + 4, 0)
    for s in range(3 + 2 * passes, last + 1):
        turn(s, s % 2)


def exists(t, tiles):
    return not isinstance(t, int) or 0 <= t < tiles


def build(nc, x, ctx, mask, g_xattn, g_ffn, ln_x_w, ln_x_b, ln_l_w, ln_l_b, Wq, Wkv, q_scale, k_scale, Wo,
          ln_o_w, ln_o_b, gate_w, Wg, Wu, Wd, Ws_g, Ws_u, Ws_d, wq_w, wq_b, wk_w, wk_b, wv_w, wv_b,
          wo_w, wo_b, w1, b1, w2, b2, gamma, beta, out):
    B, S, D = x.shape
    NT = B * S // P
    E = Wg.shape[0]
    CAP = S * 2 // E
    FE = Wg.shape[1]
    INNER = Wq.shape[1]
    DH0 = q_scale.shape[0]
    H0 = INNER // DH0
    HP = H0 // 2
    FF = w1.shape[0]
    EPS = 1e-5
    MAGIC = 1.5 * 2.0 ** 23
    NEG = -1e30

    x_tiles = x.rearrange("b s d -> (b s) d").rearrange("(t p) d -> p t d", p=P)
    c_tiles = ctx.rearrange("b s d -> (b s) d").rearrange("(t p) d -> p t d", p=P)
    o_tiles = out.rearrange("b s d -> (b s) d").rearrange("(t p) d -> p t d", p=P)

    with ExitStack() as whole:
        def sb(name, shape, dt=F32, at=whole):
            return at.enter_context(nc.sbuf_tensor(name, shape, dt))

        def sem(name, at=whole):
            return at.enter_context(nc.semaphore(name))

        xs = sb("xs", [P, NT, D])
        cs = sb("cs", [P, NT, D])
        mean = sb("mean", [P, 2, NT])
        rstd = sb("rstd", [P, 2, NT])
        stats = sb("stats", [P, 2, NT, 6])
        neghalf = sb("neghalf", [P, 2 * NT])
        ident = sb("ident", [P, P])
        identb = sb("identb", [P, P], BF16)
        fold = sb("fold", [P, S])
        half = sb("half", [P, 2])
        tokid = sb("tokid", [P, 1])
        quad = sb("quad", [P, 4])
        halves = sb("halves", [E, 2, P], BF16)
        gates = sb("gates", [P, 4])
        cols = sb("cols", [P, 12])
        rows = sb("rows", [P, 6, D])
        b1row = sb("b1row", [P, FF])
        wq_a = sb("wq_a", [P, INNER])
        wkv_a = sb("wkv_a", [P, 2 * INNER])
        wo_a = sb("wo_a", [P, HP // 2, 2, D])
        maskrow = sb("maskrow", [1, B, S], U8)
        maskbias = sb("maskbias", [1, NT, 4, S], BF16)
        ones = sb("ones", [1, P], BF16)
        gw_t = sb("gw_t", [P, E])
        ws_t = sb("ws_t", [P, 6, P])
        w_c = sb("w_c", [P, 4, P])
        w1_t = sb("w1_t", [P, FF], BF16)
        w2_t = sb("w2_t", [P, FF // P, P], BF16)
        wmean = sb("wmean", [P, 2])

        wa_in = sem("wa_in")
        with ExitStack() as ph, nc.Block() as block:
            small_in, late_in, mask_in = (sem(n, ph) for n in ("small_in", "late_in", "mask_in"))
            x_in = [sem(f"x_in{c}", ph) for c in range(4)]
            c_in = [sem(f"c_in{c}", ph) for c in range(4)]
            s_const, s_dve, s_pe, s_copied, s_gate, s_gated, s_stats, s_rstd, s_pool = (
                sem(n, ph) for n in ("s_const", "s_dve", "s_pe", "s_copied", "s_gate", "s_gated",
                                     "s_stats", "s_rstd", "s_pool"))
            nat = sb("nat", [P, 6, P], at=ph)
            nat_c = sb("nat_c", [P, 4, P], at=ph)
            nat_g = sb("nat_g", [E, P], at=ph)
            nat_1 = sb("nat_1", [P, FF // P, P], at=ph)
            nat_2 = sb("nat_2", [P, FF], at=ph)
            q_1 = sb("q_1", [P, FF // P, P], BF16, at=ph)
            q_2 = sb("q_2", [P, FF], BF16, at=ph)
            tokrow = sb("tokrow", [P, P], at=ph)
            tmp = sb("tmp", [P, FF], at=ph)
            tmp2 = sb("tmp2", [P, 2, NT, 4], at=ph)
            gin = sb("gin", [P, 4], at=ph)
            onesf = sb("onesf", [P, P], at=ph)
            pw = [ph.enter_context(nc.psum_tensor(f"pw{i}", [P, 4, P], F32)) for i in range(4)]
            pwb = [ph.enter_context(nc.psum_tensor(f"pwb{i}", [P, 4, P], BF16)) for i in range(2)]
            psw = ph.enter_context(nc.psum_tensor("psw", [P, 512], F32))

            @block.sync
            def _(sp):
                for c in range(4):
                    n = NT // 4
                    sp.dma_start(xs[:, c * n:(c + 1) * n, :], x_tiles[:, c * n:(c + 1) * n, :]).then_inc(x_in[c], 16)
                sp.dma_start(wq_a[:], Wq).then_inc(wa_in, 16)
                sp.dma_start(wkv_a[:], Wkv).then_inc(wa_in, 16)
                for a in range(2):
                    for j in range(HP // 2):
                        src = Wo.rearrange("(j a h d) n -> j a d h n", j=HP // 2, a=2, h=2)[j, a]
                        sp.dma_start(wo_a[a * DH0:(a + 1) * DH0, j], src).then_inc(wa_in, 16)
                for i, w in enumerate((Ws_g, Ws_u)):
                    sp.dma_start(nat[:, 2 * i:2 * i + 2, :], w.rearrange("(c p) d -> p c d", p=P)).then_inc(late_in, 16)
                sp.dma_start(nat[:, 4:6, :], Ws_d.rearrange("d (c f) -> d c f", f=P)).then_inc(late_in, 16)
                sp.dma_start(nat_g[:], gate_w).then_inc(late_in, 16)
                for i, w in enumerate((wq_w, wk_w, wv_w, wo_w)):
                    sp.dma_start(nat_c[:, i, :], w).then_inc(late_in, 16)
                sp.dma_start(nat_1[:], w1.rearrange("(c p) d -> p c d", p=P)).then_inc(late_in, 16)
                sp.dma_start(nat_2[:], w2).then_inc(late_in, 16)
                sp.wait_ge(late_in, 160)

            @block.scalar
            def _(act):
                for c in range(4):
                    n = NT // 4
                    act.dma_start(cs[:, c * n:(c + 1) * n, :], c_tiles[:, c * n:(c + 1) * n, :]).then_inc(c_in[c], 16)
                act.dma_start(maskrow[:], mask.rearrange("(o b) s -> o b s", o=1)).then_inc(mask_in, 16)
                for i, v in enumerate((ln_x_w, ln_x_b, ln_l_w, ln_l_b)):
                    act.dma_start(cols[:, i:i + 1], v.rearrange("(d o) -> d o", o=1)).then_inc(small_in, 16)
                for i, v in ((8, q_scale), (9, k_scale)):
                    for a in range(2):
                        act.dma_start(cols[a * DH0:(a + 1) * DH0, i:i + 1],
                                      v.rearrange("(d o) -> d o", o=1)).then_inc(small_in, 16)
                for i, v in enumerate((wq_b, wk_b, wv_b)):
                    act.dma_start(cols[:, 5 + i:6 + i], v.rearrange("(d o) -> d o", o=1)).then_inc(small_in, 16)
                for i, v in enumerate((ln_o_w, ln_o_b, wo_b, b2, gamma, beta)):
                    act.dma_start(rows[:, i, :], v.rearrange("(o d) -> o d", o=1).to_broadcast([P, D])).then_inc(small_in, 16)
                act.dma_start(b1row[:], b1.rearrange("(o d) -> o d", o=1).to_broadcast([P, FF])).then_inc(small_in, 16)
                for i, v in enumerate((g_xattn, g_ffn)):
                    act.dma_start(gin[:, 2 * i:2 * i + 2], v.rearrange("(o d) -> o d", o=1).to_broadcast([P, 2])).then_inc(small_in, 16)
                act.wait_ge(small_in, 16 * 20)
                nc.scalar.activation(gates[:], gin[:], ACT.Tanh).then_inc(s_gate, 1)

            @block.gpsimd
            def _(pool):
                pc = Steps(pool, s_pool)
                pc(nc.gpsimd.memset(ident[:], 0.0))
                pc(nc.gpsimd.affine_select(out=ident[:], in_=ident[:], compare_op=ALU.not_equal, fill=1.0,
                                           base=0, pattern=[[-1, P]], channel_multiplier=1))
                nc.gpsimd.iota(tokrow[:], pattern=[[0, 2], [1, S]], base=0, channel_multiplier=0,
                               allow_small_or_imprecise_dtypes=True).then_inc(s_const, 1)
                pool.wait_ge(s_stats, 1)
                nc.gpsimd.tensor_tensor(rstd[:].rearrange("p a t -> p (a t)"), rstd[:].rearrange("p a t -> p (a t)"),
                                        neghalf[:], ALU.pow).then_inc(s_rstd, 1)
                pool.wait_ge(s_rstd, 1)

            @block.vector
            def _(dve):
                d = Steps(dve, s_dve)
                d(nc.vector.memset(neghalf[:], -0.5))
                d(nc.vector.memset(ones[:], 1.0))
                d(nc.vector.memset(halves[:], 0.0))
                for b in range(2):
                    d(nc.vector.memset(halves[:, b, b * S:(b + 1) * S], 1.0))
                d(nc.vector.memset(onesf[:], 1.0))
                dve.wait_ge(s_pool, 2)
                dve.wait_ge(s_const, 1)
                d(nc.vector.tensor_copy(identb[:], ident[:]))
                d(nc.vector.tensor_tensor(fold[:], ident[:, 0:S], ident[:, S:P], ALU.add))
                d(nc.vector.tensor_reduce(half[:], ident[:].rearrange("p (a s) -> p a s", a=2), AX.X, ALU.add))
                d(nc.vector.tensor_tensor(tmp[:, 0:P], ident[:], tokrow[:], ALU.mult))
                d(nc.vector.tensor_reduce(tokid[:], tmp[:, 0:P], AX.X, ALU.add))
                d(nc.vector.tensor_reduce(tmp[:, 128:144], ident[:].rearrange("p (h e) -> p h e", e=8), AX.X, ALU.add))
                d(nc.vector.tensor_reduce(quad[:], tmp[:, 128:144].rearrange("p (g h) -> p h g", h=4), AX.X, ALU.add))
                d(nc.vector.tensor_scalar(quad[:], quad[:], 8.0 ** -0.5, None, ALU.mult))
                for c in range(4):
                    for which, src, landed in ((1, xs, x_in), (0, cs, c_in)):
                        dve.wait_ge(landed[c], 16)
                        for t in range(c * NT // 4, (c + 1) * NT // 4):
                            last = nc.vector.bn_stats(stats[:, which, t, :], src[:, t, :])
                    d(last)
                m_sum, m_dif, var = tmp2[:, :, :, 0], tmp2[:, :, :, 1], tmp2[:, :, :, 2]
                d(nc.vector.tensor_tensor(m_sum, stats[:, :, :, 1], stats[:, :, :, 4], ALU.add))
                d(nc.vector.tensor_tensor(m_dif, stats[:, :, :, 1], stats[:, :, :, 4], ALU.subtract))
                d(nc.vector.tensor_scalar(mean[:], m_sum, 0.5, None, ALU.mult))
                d(nc.vector.scalar_tensor_tensor(m_dif, m_dif, 0.25, m_dif, ALU.mult, ALU.mult))
                d(nc.vector.tensor_tensor(var, stats[:, :, :, 2], stats[:, :, :, 5], ALU.add))
                d(nc.vector.scalar_tensor_tensor(var, var, 1.0 / D, m_dif, ALU.mult, ALU.add))
                d(nc.vector.tensor_scalar(rstd[:, 0, :], var[:, 0], EPS, None, ALU.add))
                d(nc.vector.tensor_scalar(rstd[:, 1, :], var[:, 1], 1.0 + EPS, EPS * EPS, ALU.mult, ALU.add))
                nc.vector.memset(tmp2[:, 0, 0, 3:4], 0.0).then_inc(s_stats, 1)
                dve.wait_ge(mask_in, 16)
                d(nc.vector.memset(maskbias[:], 0.0))
                d(nc.vector.tensor_scalar(maskbias[:, :, 0:4:3, :], maskrow[:].rearrange("o (t b) s -> o t b s", b=2),
                                          1.0, -NEG, ALU.subtract, ALU.mult))
                dve.wait_ge(s_gate, 1)
                d(nc.vector.scalar_tensor_tensor(cols[:, 4:5], cols[:, 8:9], 8.0, cols[:, 9:10], ALU.mult, ALU.mult))
                d(nc.vector.tensor_scalar(rows[:, 0:2, :], rows[:, 0:2, :], gates[:, 0:1], None, ALU.mult))
                d(nc.vector.tensor_scalar(rows[:, 2, :], rows[:, 2, :], gates[:, 1:2], None, ALU.mult))
                d(nc.vector.tensor_scalar(rows[:, 3, :], rows[:, 3, :], gates[:, 3:4], None, ALU.mult))
                dve.wait_ge(late_in, 160)
                d(nc.vector.tensor_reduce(tmp2[:, 0, 0:1, 0], nat_1[:].rearrange("p c d -> p (c d)"), AX.X, ALU.add,
                                          apply_absolute_value=True))
                d(nc.vector.tensor_reduce(tmp2[:, 0, 1:2, 0], nat_2[:], AX.X, ALU.add, apply_absolute_value=True))
                nc.vector.tensor_copy(tmp2[:, 1, 0:2, 0], tmp2[:, 0, 0:2, 0]).then_inc(s_gated, 1)
                dve.wait_ge(s_pe, 1)
                d(nc.vector.tensor_scalar(wmean[:], psw[:, 0:2], 1.0 / (FF * D), EPS, ALU.mult, ALU.max))
                d(nc.vector.reciprocal(tmp2[:, 1, 0:2, 1], wmean[:]))
                for i, (w, q) in enumerate(((nat_1[:].rearrange("p c d -> p (c d)"), q_1[:].rearrange("p c d -> p (c d)")),
                                            (nat_2[:], q_2[:]))):
                    d(nc.vector.tensor_scalar(tmp[:], w, tmp2[:, 1, i:i + 1, 1], MAGIC, ALU.mult, ALU.add))
                    d(nc.vector.tensor_scalar(tmp[:], tmp[:], MAGIC, 1.0, ALU.subtract, ALU.min))
                    ins = nc.vector.tensor_scalar(q, tmp[:], -1.0, None, ALU.max)
                    ins.then_inc(s_gated, 1)
                    dve.wait_ge(s_gated, 2 + i)
                dve.wait_ge(s_pe, 2)
                d(nc.vector.tensor_copy(ws_t[:, 0:4, :], pw[0][:]))
                d(nc.vector.tensor_copy(ws_t[:, 4:6, :], pw[1][:, 0:2, :]))
                d(nc.vector.tensor_copy(gw_t[:], pw[1][:, 2, 0:E]))
                d(nc.vector.tensor_copy(w_c[:, 0:3, :], pw[2][:, 0:3, :]))
                d(nc.vector.tensor_scalar(w_c[:, 3, :], pw[2][:, 3, :], gates[:, 1:2], None, ALU.mult))
                dve.wait_ge(s_pe, 3)
                d(nc.vector.tensor_copy(w1_t[:], pwb[0][:].rearrange("p c d -> p (c d)")))
                d(nc.vector.tensor_copy(w2_t[:], pwb[1][:]))

            @block.tensor
            def _(pe):
                pe.wait_ge(s_gated, 1)
                nc.tensor.matmul(psw[:, 0:2], onesf[:], tmp2[:, 1, 0:2, 0], start=True, stop=True).then_inc(s_pe, 1)
                pe.wait_ge(late_in, 160)
                for i in range(4):
                    nc.tensor.transpose(pw[0][:, i, :], nat[:, i, :], ident[:])
                for i in range(2):
                    nc.tensor.transpose(pw[1][:, i, :], nat[:, 4 + i, :], ident[:])
                nc.tensor.transpose(pw[1][:, 2, 0:E], nat_g[:], ident[0:E, 0:E])
                for i in range(4):
                    last = nc.tensor.transpose(pw[2][:, i, :], nat_c[:, i, :], ident[:])
                last.then_inc(s_pe, 1)
                pe.wait_ge(s_gated, 3)
                for i in range(4):
                    nc.tensor.transpose(pwb[0][:, i, :], q_1[:, i, :], identb[:])
                for i in range(4):
                    last = nc.tensor.transpose(pwb[1][:, i, :], q_2[:, i * P:(i + 1) * P], identb[:])
                last.then_inc(s_pe, 1)

        attention_0(nc, locals())
        if STOP == "A":
            return store(nc, o_tiles, xs)
        with ExitStack() as moe:
            x_tok = sb("x_tok", [P, E, NT, 2, CAP], at=moe)
            eo_T = sb("eo_T", [P, B, E, CAP], at=moe)
            sel_w = sb("sel_w", [P, NT, E * CAP], at=moe)
            xnT_all = sb("xnT_all", [P, NT, P], at=moe)
            routing(nc, locals())
            experts(nc, locals())
            combine(nc, locals())
        if STOP == "B":
            return store(nc, o_tiles, xs)
        attention_1(nc, locals())
        if STOP == "C":
            return store(nc, o_tiles, xs)
        ffn_1(nc, locals(), o_tiles)


def store(nc, o_tiles, xs):
    with nc.semaphore("stored") as stored, nc.Block() as block:
        @block.sync
        def _(sp):
            sp.dma_start(o_tiles, xs[:]).then_inc(stored, 16)
            sp.wait_ge(stored, 16)


def attention_0(nc, v):
    xs, cs, mean, rstd, stats, neghalf, ident = (v[n] for n in "xs cs mean rstd stats neghalf ident".split())
    cols, rows, wq_a, wkv_a, wo_a, maskbias, ones = (
        v[n] for n in "cols rows wq_a wkv_a wo_a maskbias ones".split())
    NT, D, S, INNER, H0, HP, DH0, EPS = (v[n] for n in "NT D S INNER H0 HP DH0 EPS".split())
    with ExitStack() as ph, nc.Block() as block:
        def sb(name, shape, dt=F32):
            return ph.enter_context(nc.sbuf_tensor("a0_" + name, shape, dt))

        def pb(name):
            return ph.enter_context(nc.psum_tensor("a0_" + name, [P, 512], F32))

        def sem(name):
            return ph.enter_context(nc.semaphore("a0_" + name))

        xn = sb("xn", [P, 2, 2, D])
        kvT = sb("kvT", [P, 2, 4 * S])
        sq = sb("sq", [P, 2, INNER])
        ssq = sb("ssq", [P, 2, 3, H0])
        rn = sb("rn", [P, 2, 3, H0])
        qn = sb("qn", [P, 2, INNER])
        kn = sb("kn", [P, 2, INNER])
        qbd = sb("qbd", [P, 2, 2, HP, 2, S])
        kT = sb("kT", [P, 2, 2, HP, P])
        vaug = sb("vaug", [P, 2, 2, H0, DH0 + 1])
        mx = sb("mx", [P, 2, HP])
        pr = sb("pr", [P, 2, HP, P])
        prT = sb("prT", [P, 2, HP, P])
        rsum = sb("rsum", [P, 2, HP])
        att = sb("att", [P, 2, HP, DH0])
        attT = sb("attT", [P, 2, HP // 2, 2, 2, S])
        xb = sb("xb", [P, 2, D])
        yst = sb("yst", [P, 2, 6])
        ymv = sb("ymv", [P, 2, 2])
        yr = sb("yr", [P, 2, 1])
        yw = sb("yw", [P, 2, D])
        spare = sb("spare", [P, 1])
        p_q, p_k0, p_k1, p_v, p_tr, p_s, p_pT, p_o = (pb(n) for n in "q k0 k1 v tr s pT o".split())
        qk_bank = (p_q, p_k0, p_k1)
        vproj_done = sem("vproj_done")
        zeroed, xn_ready, xT_done, kvT_ready, proj_done, squared, reduced, normed, scaled, v_ready = (
            sem(n) for n in ("zeroed", "xn_ready", "xT_done", "kvT_ready", "proj_done", "squared", "reduced",
                             "normed", "scaled", "v_ready"))
        turned, turned_out, scored, shifted, exped, pT_done, prT_ready, mixed, att_ready, attT_done, attT_ready = (
            sem(n) for n in ("turned", "turned_out", "scored", "shifted", "exped", "pT_done", "prT_ready", "mixed",
                             "att_ready", "attT_done", "attT_ready"))
        y_done, y_stats, y_rstd, y_read, xb_ready, y_chain, x_new, maxed, inverted = (
            sem(n) for n in ("y_done", "y_stats", "y_rstd", "y_read", "xb_ready", "y_chain", "x_new",
                             "maxed", "inverted"))

        FIRST, LAST = -1, NT + 1

        @block.gpsimd
        def _(pool):
            nc.gpsimd.memset(qbd[:], 0.0).then_inc(zeroed, 1)
            nc.gpsimd.memset(vaug[:], 1.0).then_inc(zeroed, 1)

            def inverse_norm(t, tp, i):
                pool.wait_ge(reduced, 3 * t + i + 1)
                nc.gpsimd.tensor_tensor(rn[:, tp, i, :], ssq[:, tp, i, :], neghalf[:, 0:H0], ALU.pow)\
                    .then_inc(normed, 1)

            def out_norm(t, tp):
                nc.gpsimd.tensor_tensor(xb[:, tp, :], xs[:, t, :], rows[:, 1, :], ALU.add).then_inc(xb_ready, 1)
                pool.wait_ge(y_stats, t + 1)
                nc.gpsimd.tensor_tensor(yr[:, tp, :], ymv[:, tp, 1:2], neghalf[:, 0:1], ALU.pow).then_inc(y_rstd, 1)

            def turn(s, sp):
                if exists(s, NT):
                    inverse_norm(s, sp, 0)
                    inverse_norm(s, sp, 1)
                if exists(s - 2, NT):
                    out_norm(s - 2, sp)
                if exists(s, NT):
                    inverse_norm(s, sp, 2)

            turns(pool, NT, turn, FIRST, LAST)

        @block.tensor
        def _(pe):
            pe.wait_ge(v["wa_in"], 16 * 6)

            def xT(t, tp):
                pe.wait_ge(xn_ready, t + 1)
                wait(pe, turned_out, 4 * (t - 1))
                nc.tensor.transpose(p_tr[:, 0:P], xn[:, tp, 0, :], ident[:])
                nc.tensor.transpose(p_tr[:, P:2 * P], xn[:, tp, 1, :], ident[:]).then_inc(xT_done, 1)

            def project(t, tp, i):
                if i == 0:
                    pe.wait_ge(kvT_ready, 2 * t + 2)
                wait(pe, scaled, 3 * (t - 1) + i + 1)
                cols_ = slice(S, 3 * S) if i == 0 else slice((i - 1) * 2 * S, i * 2 * S)
                nc.tensor.matmul(qk_bank[i][:], kvT[:, tp, cols_], wq_a[:] if i == 0 else wkv_a[:, 0:INNER],
                                 start=True, stop=True).then_inc(proj_done, 1)

            def project_v(t, tp, b):
                wait(pe, v_ready, 2 * t + b)
                nc.tensor.matmul(p_v[:], kvT[:, tp, b * 2 * S:(b + 1) * 2 * S], wkv_a[:, INNER:2 * INNER],
                                 start=True, stop=True).then_inc(vproj_done, 1)

            def turn_over(t, tp, i):
                pe.wait_ge(scaled, 3 * t + i + 1)
                if i == 0:
                    pe.wait_ge(kvT_ready, 2 * t + (4 if exists(t + 1, NT) else 2))
                else:
                    pe.wait_ge(turned_out, 4 * t + i + 1)
                src = qn[:, tp, :] if i == 0 else kn[:, i - 1, :]
                for h in range(HP):
                    last = nc.tensor.transpose(p_tr[:, h * P:(h + 1) * P], src[:, h * P:(h + 1) * P], ident[:])
                last.then_inc(turned, 1)

            def scores(t, tp, b):
                pe.wait_ge(turned_out, 4 * t + 3 + b)
                wait(pe, shifted, 2 * t + b)
                nc.tensor.matmul(p_s[:], ones[:],
                                 maskbias[:, t, 2 * b:2 * b + 2, :].rearrange("o c s -> o (c s)").unsqueeze(1)
                                 .to_broadcast([1, HP, P]), start=True, stop=False, skip_group_check=True)
                for h in range(HP):
                    last = nc.tensor.matmul(p_s[:, h * P:(h + 1) * P], qbd[:, tp, b, h, :, :], kT[:, tp, b, h, :],
                                            start=False, stop=True, skip_group_check=True)
                last.then_inc(scored, 1)

            def probs_T(t, tp, b):
                pe.wait_ge(exped, 2 * t + b + 1)
                wait(pe, prT_ready, 2 * t + b)
                for h in range(HP):
                    last = nc.tensor.transpose(p_pT[:, h * P:(h + 1) * P], pr[:, b, h, :], ident[:])
                last.then_inc(pT_done, 1)

            def mix(t, tp, b):
                pe.wait_ge(prT_ready, 2 * t + b + 1)
                pe.wait_ge(v_ready, 2 * t + b + 1)
                if b == 0:
                    wait(pe, y_read, t)
                else:
                    pe.wait_ge(attT_ready, 2 * t + 1)
                for h in range(HP):
                    for a in range(2):
                        last = nc.tensor.matmul(p_o[a * S:(a + 1) * S, h * (DH0 + 1):(h + 1) * (DH0 + 1)],
                                                prT[:, b, h, a * S:(a + 1) * S], vaug[:, tp, b, 2 * h + a, :],
                                                start=True, stop=True)
                last.then_inc(mixed, 1)

            def att_T(t, tp, b):
                pe.wait_ge(att_ready, 2 * t + b + 1)
                for j in range(HP // 2):
                    last = nc.tensor.transpose(p_o[:, j * P:(j + 1) * P],
                                               att[:, b, 2 * j:2 * j + 2, :], ident[:])
                last.then_inc(attT_done, 1)

            def out_proj(t, tp):
                pe.wait_ge(attT_ready, 2 * t + 2)
                for n in range(HP):
                    j, a = n // 2, n % 2
                    last = nc.tensor.matmul(p_o[:, 0:D], attT[:, tp, j, a, :, :], wo_a[:, j, a, :],
                                            start=(n == 0), stop=(n == HP - 1))
                last.then_inc(y_done, 1)

            def turn(s, sp):
                now, back, tail = exists(s, NT), exists(s - 1, NT), exists(s - 2, NT)
                if now:
                    project(s, sp, 0)
                if back:
                    turn_over(s - 1, 1 - sp, 2)
                if tail:
                    att_T(s - 2, sp, 1)
                if back:
                    scores(s - 1, 1 - sp, 0)
                if now:
                    project(s, sp, 1)
                if exists(s + 1, NT):
                    xT(s + 1, 1 - sp)
                if tail:
                    out_proj(s - 2, sp)
                if back:
                    scores(s - 1, 1 - sp, 1)
                if now:
                    project(s, sp, 2)
                if back:
                    probs_T(s - 1, 1 - sp, 0)
                if now:
                    project_v(s, sp, 0)
                if back:
                    mix(s - 1, 1 - sp, 0)
                    probs_T(s - 1, 1 - sp, 1)
                if now:
                    turn_over(s, sp, 0)
                    project_v(s, sp, 1)
                if back:
                    att_T(s - 1, 1 - sp, 0)
                if now:
                    turn_over(s, sp, 1)
                if back:
                    mix(s - 1, 1 - sp, 1)

            turns(pe, NT, turn, FIRST, LAST)

        @block.scalar
        def _(act):
            def affine(t, tp):
                act.wait_ge(xT_done, t + 1)
                wait(act, vproj_done, 2 * (t - 1))
                groups = kvT[:, tp, :].rearrange("p (g s) -> p g s", g=4)
                for c, dst in ((0, groups[:, 0:4:3, :]), (1, groups[:, 1:3, :])):
                    nc.scalar.activation(dst, p_tr[:, c * P:(c + 1) * P].rearrange("p (b s) -> p b s", b=2),
                                         ACT.Identity, bias=cols[:, 2 * c + 1:2 * c + 2],
                                         scale=cols[:, 2 * c:2 * c + 1]).then_inc(kvT_ready, 1)

            def square(t, tp, i):
                act.wait_ge(proj_done, 3 * t + i + 1)
                wait(act, reduced, 3 * t + i - 1)
                nc.scalar.activation(sq[:, (3 * tp + i) % 2, :], qk_bank[i][:], ACT.Square).then_inc(squared, 1)

            def values(t, tp, b):
                act.wait_ge(vproj_done, 2 * t + b + 1)
                wait(act, mixed, 2 * (t - 2) + b + 1)
                nc.scalar.copy(vaug[:, tp, b, :, 0:DH0],
                               p_v[:].rearrange("p (h d) -> p h d", h=H0)).then_inc(v_ready, 1)

            def queries_out(t, tp):
                act.wait_ge(turned, 3 * t + 1)
                wait(act, scored, 2 * (t - 1))
                for a in range(2):
                    nc.scalar.activation(qbd[a * S:(a + 1) * S, tp, :, :, a, :],
                                         p_tr[a * S:(a + 1) * S, :].rearrange("p (h b s) -> p b h s", h=HP, b=2),
                                         ACT.Copy).then_inc(turned_out, 1)

            def keys_out(t, tp, b):
                act.wait_ge(turned, 3 * t + 2 + b)
                wait(act, scored, 2 * (t - 2) + b + 1)
                nc.scalar.activation(kT[:, tp, b, :, :], p_tr[:].rearrange("p (h k) -> p h k", h=HP), ACT.Copy,
                                     scale=cols[:, 4:5]).then_inc(turned_out, 1)

            def exp(t, b):
                act.wait_ge(shifted, 2 * t + b + 1)
                nc.scalar.activation(pr[:, b], pr[:, b], ACT.Exp).then_inc(exped, 1)

            def probs_out(t, b):
                act.wait_ge(pT_done, 2 * t + b + 1)
                wait(act, mixed, 2 * (t - 1) + b + 1)
                nc.scalar.copy(prT[:, b].rearrange("p h k -> p (h k)"), p_pT[:]).then_inc(prT_ready, 1)

            def att_out(t, tp, b):
                act.wait_ge(attT_done, 2 * t + b + 1)
                wait(act, y_done, t)
                nc.scalar.copy(attT[:, tp, :, :, b, :],
                               p_o[:, 0:HP // 2 * P].rearrange("p (j a s) -> p j a s", j=HP // 2, a=2)).then_inc(attT_ready, 1)

            def turn(s, sp):
                now, back = exists(s, NT), exists(s - 1, NT)
                if now:
                    square(s, sp, 0)
                if back:
                    keys_out(s - 1, 1 - sp, 1)
                if exists(s - 2, NT):
                    att_out(s - 2, sp, 1)
                if now:
                    square(s, sp, 1)
                if exists(s + 1, NT):
                    affine(s + 1, 1 - sp)
                if back:
                    exp(s - 1, 0)
                if now:
                    square(s, sp, 2)
                if back:
                    probs_out(s - 1, 0)
                    exp(s - 1, 1)
                if now:
                    values(s, sp, 0)
                if back:
                    probs_out(s - 1, 1)
                if now:
                    queries_out(s, sp)
                    values(s, sp, 1)
                if back:
                    att_out(s - 1, 1 - sp, 0)
                if now:
                    keys_out(s, sp, 0)

            act.wait_ge(zeroed, 2)
            turns(act, NT, turn, FIRST, LAST)

        @block.vector
        def _(dve):
            def normalise(t, tp):
                wait(dve, xT_done, t - 1)
                nc.vector.tensor_scalar(xn[:, tp, 0, :], cs[:, t, :], mean[:, 0, bass.ds(t, 1)], rstd[:, 0, bass.ds(t, 1)],
                                        ALU.subtract, ALU.mult)
                nc.vector.tensor_scalar(xn[:, tp, 1, :], xs[:, t, :], mean[:, 1, bass.ds(t, 1)], rstd[:, 1, bass.ds(t, 1)],
                                        ALU.subtract, ALU.mult).then_inc(xn_ready, 1)

            def reduce(t, tp, i):
                dve.wait_ge(squared, 3 * t + i + 1)
                wait(dve, normed, 3 * (t - 2) + i + 1)
                nc.vector.tensor_reduce(ssq[:, tp, i, :], sq[:, (3 * tp + i) % 2, :].rearrange("p (h d) -> p h d", h=H0),
                                        AX.X, ALU.add).then_inc(reduced, 1)

            def scale(t, tp, i):
                dve.wait_ge(normed, 3 * t + i + 1)
                if i == 0:
                    wait(dve, turned, 3 * (t - 2) + 1)
                    dst = qn[:, tp, :]
                else:
                    wait(dve, turned, 3 * (t - 1) + i + 1)
                    dst = kn[:, i - 1, :]
                nc.vector.scalar_tensor_tensor(dst.rearrange("p (h d) -> p h d", h=H0),
                                               rn[:, tp, i, :].unsqueeze(2).to_broadcast([P, H0, DH0]), 1e12,
                                               qk_bank[i][:].rearrange("p (h d) -> p h d", h=H0),
                                               ALU.min, ALU.mult).then_inc(scaled, 1)

            s3 = p_s[:].rearrange("p (h k) -> p h k", h=HP)

            def shift(t, b):
                dve.wait_ge(scored, 2 * t + b + 1)
                nc.vector.tensor_reduce(mx[:, b, :], s3, AX.X, ALU.max).then_inc(maxed, 1)
                dve.wait_ge(maxed, 2 * t + b + 1)
                wait(dve, pT_done, 2 * (t - 1) + b + 1)
                nc.vector.tensor_tensor(pr[:, b], s3, mx[:, b, :].unsqueeze(2).to_broadcast([P, HP, P]),
                                        ALU.subtract).then_inc(shifted, 1)

            def attend(t, b):
                dve.wait_ge(mixed, 2 * t + b + 1)
                o3 = p_o[:, 0:HP * (DH0 + 1)].rearrange("p (h d) -> p h d", h=HP)
                nc.vector.reciprocal(rsum[:, b, :], o3[:, :, DH0]).then_inc(inverted, 1)
                dve.wait_ge(inverted, 2 * t + b + 1)
                wait(dve, attT_done, 2 * (t - 1) + b + 1)
                nc.vector.tensor_tensor(att[:, b], o3[:, :, 0:DH0],
                                        rsum[:, b, :].unsqueeze(2).to_broadcast([P, HP, DH0]),
                                        ALU.mult).then_inc(att_ready, 1)

            def read_output(t, tp):
                dve.wait_ge(y_done, t + 1)
                y = Steps(dve, y_chain, 2 * t)
                y(nc.vector.bn_stats(yst[:, tp, :], p_o[:, 0:D]))
                nc.vector.memset(spare[:], 0.0)
                y(nc.vector.bn_aggr(ymv[:, tp, :], yst[:, tp, :]))
                nc.vector.tensor_scalar(ymv[:, tp, 1:2], ymv[:, tp, 1:2], EPS, None, ALU.add).then_inc(y_stats, 1)
                nc.vector.scalar_tensor_tensor(yw[:, tp, :], p_o[:, 0:D], ymv[:, tp, 0:1], rows[:, 0, :],
                                               ALU.subtract, ALU.mult).then_inc(y_read, 1)

            def write_output(t, tp):
                dve.wait_ge(y_read, t + 1)
                dve.wait_ge(y_rstd, t + 1)
                dve.wait_ge(xb_ready, t + 1)
                nc.vector.scalar_tensor_tensor(xs[:, t, :], yw[:, tp, :], yr[:, tp, :], xb[:, tp, :],
                                               ALU.mult, ALU.add).then_inc(x_new, 1)

            def next_stats(t):
                dve.wait_ge(x_new, t + 1)
                nc.vector.bn_stats(stats[:, 1, t, :], xs[:, t, :])

            def turn(s, sp):
                now, back, tail = exists(s, NT), exists(s - 1, NT), exists(s - 2, NT)
                if tail:
                    attend(s - 2, 1)
                if exists(s + 1, NT):
                    normalise(s + 1, 1 - sp)
                if now:
                    reduce(s, sp, 0)
                if back:
                    shift(s - 1, 0)
                if now:
                    reduce(s, sp, 1)
                    scale(s, sp, 0)
                if tail:
                    read_output(s - 2, sp)
                if back:
                    shift(s - 1, 1)
                if now:
                    scale(s, sp, 1)
                    reduce(s, sp, 2)
                if tail:
                    write_output(s - 2, sp)
                if back:
                    attend(s - 1, 0)
                if now:
                    scale(s, sp, 2)
                if tail:
                    next_stats(s - 2)

            turns(dve, NT, turn, FIRST, LAST)


def finish_stats(nc, dve, step, stats, mean, rstd, tmp, D, EPS):
    m_sum, m_dif, var = tmp[:, :, 0], tmp[:, :, 1], tmp[:, :, 2]
    step(nc.vector.tensor_tensor(m_sum, stats[:, 1, :, 1], stats[:, 1, :, 4], ALU.add))
    step(nc.vector.tensor_tensor(m_dif, stats[:, 1, :, 1], stats[:, 1, :, 4], ALU.subtract))
    step(nc.vector.tensor_scalar(mean[:, 1, :], m_sum, 0.5, None, ALU.mult))
    step(nc.vector.scalar_tensor_tensor(m_dif, m_dif, 0.25, m_dif, ALU.mult, ALU.mult))
    step(nc.vector.tensor_tensor(var, stats[:, 1, :, 2], stats[:, 1, :, 5], ALU.add))
    step(nc.vector.scalar_tensor_tensor(var, var, 1.0 / D, m_dif, ALU.mult, ALU.add))
    return nc.vector.tensor_scalar(rstd[:, 1, :], var, EPS, None, ALU.add)


def routing(nc, v):
    xs, mean, rstd, stats, neghalf, ident, tokid, gw_t = (
        v[n] for n in "xs mean rstd stats neghalf ident tokid gw_t".split())
    x_tok, sel_w, xnT_all, halves = (v[n] for n in "x_tok sel_w xnT_all halves".split())
    NT, D, S, E, CAP, EPS = (v[n] for n in "NT D S E CAP EPS".split())
    with ExitStack() as ph, nc.Block() as block:
        def sb(name, shape, dt=F32):
            return ph.enter_context(nc.sbuf_tensor("r_" + name, shape, dt))

        def pb(name):
            return ph.enter_context(nc.psum_tensor("r_" + name, [P, 512], F32))

        def sem(name):
            return ph.enter_context(nc.semaphore("r_" + name))

        tmp = sb("tmp", [P, NT, 4])
        xn = sb("xn", [P, 2, D])
        xnT = sb("xnT", [P, 2, P])
        negmax = sb("negmax", [P, 2, 1])
        ex = sb("ex", [P, 2, E])
        esum = sb("esum", [P, 2, 1])
        sc = sb("sc", [P, 2, E])
        scT = sb("scT", [E, 2, P])
        top = sb("top", [E, 2, 2, CAP])
        idx = sb("idx", [E, 2, 2, CAP], U32)
        idxf = sb("idxf", [E, 2, 2, CAP])
        spread = sb("spread", [E, 2, 2, E, CAP], BF16)
        spare = sb("spare", [P, 1])
        sel = sb("sel", [P, 2, E * CAP])
        p_T, p_L, p_sT, p_I, p_g0, p_g1 = (pb(n) for n in "T L sT I g0 g1".split())
        p_g = (p_g0, p_g1)
        (var_ready, norm_ready, chain, xn_ready, xT_done, xT_ready, xT_kept, logits_done, max_ready, exp_done,
         sc_ready, scT_done, scT_ready, top_chain, spread_ready, index_done, sel_ready, sel_w_ready, gathered,
         taken, inverse_ready) = (
            sem(n) for n in ("var_ready", "norm_ready", "chain", "xn_ready", "xT_done", "xT_ready", "xT_kept",
                             "logits_done", "max_ready", "exp_done", "sc_ready", "scT_done", "scT_ready",
                             "top_chain", "spread_ready", "index_done", "sel_ready", "sel_w_ready", "gathered",
                             "taken", "inverse_ready"))

        @block.gpsimd
        def _(pool):
            pool.wait_ge(var_ready, 1)
            nc.gpsimd.tensor_tensor(rstd[:, 1, :], rstd[:, 1, :], neghalf[:, 0:NT], ALU.pow).then_inc(norm_ready, 1)

            def keep(t, tp):
                pool.wait_ge(xT_ready, t + 1)
                nc.gpsimd.tensor_copy(xnT_all[:, t, :], xnT[:, tp, :]).then_inc(xT_kept, 1)

            pipelined(pool, NT, keep, lambda t, tp: None)

        @block.tensor
        def _(pe):
            def front(t, tp):
                pe.wait_ge(xn_ready, t + 1)
                wait(pe, xT_ready, t)
                nc.tensor.transpose(p_T[:, 0:P], xn[:, tp, :], ident[:]).then_inc(xT_done, 1)
                pe.wait_ge(xT_ready, t + 1)
                wait(pe, exp_done, t)
                nc.tensor.matmul(p_L[:, 0:E], xnT[:, tp, :], gw_t[:], start=True, stop=True).then_inc(logits_done, 1)

            def turn(t, tp):
                pe.wait_ge(sc_ready, t + 1)
                wait(pe, scT_ready, t)
                nc.tensor.transpose(p_sT[0:E, 0:P], sc[:, tp, :], ident[:]).then_inc(scT_done, 1)

            def gather(t, tp):
                pe.wait_ge(spread_ready, t + 1)
                wait(pe, sel_ready, t)
                for b in range(2):
                    last = nc.tensor.matmul(p_I[:, 0:E * CAP], halves[:, b, :],
                                            spread[:, tp, b].rearrange("e f c -> e (f c)"),
                                            start=(b == 0), stop=(b == 1))
                last.then_inc(index_done, 1)
                pe.wait_ge(sel_ready, t + 1)
                for b in range(2):
                    wait(pe, taken, 2 * t + b - 1 + (1 - b) * 0 if isinstance(t, int) and t == 0 else 2 * t)
                    nc.tensor.matmul(p_g[b][:, 0:E * CAP], xn[b * S:(b + 1) * S, tp, :], sel[b * S:(b + 1) * S, tp, :],
                                     start=True, stop=True).then_inc(gathered, 1)

            def back(t, tp):
                turn(t, tp)
                gather(t, tp)

            def both(t, tp):
                turn(t, tp)
                front(t + 1, 1 - tp)
                gather(t, tp)

            pipelined(pe, NT, front, back, both)

        @block.scalar
        def _(act):
            def front(t, tp):
                act.wait_ge(xT_done, t + 1)
                wait(act, logits_done, t - 1)
                wait(act, xT_kept, t - 1)
                nc.scalar.copy(xnT[:, tp, :], p_T[:, 0:P]).then_inc(xT_ready, 1)
                act.wait_ge(max_ready, t + 1)
                wait(act, sc_ready, t - 1)
                nc.scalar.activation(ex[:, tp, :], p_L[:, 0:E], ACT.Exp, bias=negmax[:, tp, :],
                                     accum_out=esum[:, tp, :]).then_inc(exp_done, 1)

            def back(t, tp):
                act.wait_ge(scT_done, t + 1)
                wait(act, spread_ready, t - 1)
                nc.scalar.copy(scT[:, tp, :], p_sT[0:E, 0:P]).then_inc(scT_ready, 1)

            def both(t, tp):
                back(t, tp)
                front(t + 1, 1 - tp)

            pipelined(act, NT, front, back, both)

        @block.vector
        def _(dve):
            finish_stats(nc, dve, Steps(dve, chain), stats, mean, rstd, tmp, D, EPS).then_inc(var_ready, 1)
            dve.wait_ge(norm_ready, 1)

            def front(t, tp):
                wait(dve, gathered, 2 * (t - 1))
                nc.vector.tensor_scalar(xn[:, tp, :], xs[:, t, :], mean[:, 1, bass.ds(t, 1)], rstd[:, 1, bass.ds(t, 1)],
                                        ALU.subtract, ALU.mult).then_inc(xn_ready, 1)
                dve.wait_ge(logits_done, t + 1)
                nc.vector.tensor_reduce(negmax[:, tp, :], p_L[:, 0:E], AX.X, ALU.max, negate=True).then_inc(max_ready, 1)
                dve.wait_ge(exp_done, t + 1)
                nc.vector.reciprocal(esum[:, tp, :], esum[:, tp, :]).then_inc(inverse_ready, 1)
                dve.wait_ge(inverse_ready, t + 1)
                nc.vector.tensor_scalar(sc[:, tp, :], ex[:, tp, :], esum[:, tp, :], None, ALU.mult).then_inc(sc_ready, 1)

            def choose(t, tp):
                dve.wait_ge(scT_ready, t + 1)
                nc.vector.memset(spare[:], 0.0)
                step = Steps(dve, top_chain, 4 * t)
                for b in range(2):
                    last = nc.vector.max(top[:, tp, b, :], scT[:, tp, b * S:(b + 1) * S])
                step(last)
                nc.vector.memset(spare[:], 0.0)
                for b in range(2):
                    last = nc.vector.max_index(idx[:, tp, b, :], top[:, tp, b, :], scT[:, tp, b * S:(b + 1) * S])
                step(last)
                step(nc.vector.tensor_copy(idxf[:, tp], idx[:, tp]))
                for b in range(2):
                    last = nc.vector.tensor_tensor(spread[:, tp, b], ident[0:E, 0:E].unsqueeze(2).to_broadcast([E, E, CAP]),
                                                   idxf[:, tp, b, :].unsqueeze(1).to_broadcast([E, E, CAP]), ALU.mult)
                    if b == 0:
                        step(last)
                last.then_inc(spread_ready, 1)

            def select(t, tp):
                dve.wait_ge(index_done, t + 1)
                nc.vector.tensor_scalar(sel[:, tp, :], p_I[:, 0:E * CAP], tokid[:], None, ALU.is_equal).then_inc(sel_ready, 1)
                dve.wait_ge(sel_ready, t + 1)
                nc.vector.tensor_tensor(sel_w[:, t, :].rearrange("p (e c) -> p e c", c=CAP),
                                        sel[:, tp, :].rearrange("p (e c) -> p e c", c=CAP),
                                        sc[:, tp, :].unsqueeze(2).to_broadcast([P, E, CAP]), ALU.mult).then_inc(sel_w_ready, 1)
                for b in range(2):
                    dve.wait_ge(gathered, 2 * t + b + 1)
                    nc.vector.tensor_copy(x_tok[:, :, t, b, :],
                                          p_g[b][:, 0:E * CAP].rearrange("p (e c) -> p e c", c=CAP)).then_inc(taken, 1)

            def back(t, tp):
                choose(t, tp)
                select(t, tp)

            def both(t, tp):
                choose(t, tp)
                front(t + 1, 1 - tp)
                select(t, tp)

            pipelined(dve, NT, front, back, both)


def experts(nc, v):
    ident, x_tok, eo_T, Wg, Wu, Wd = (v[n] for n in "ident x_tok eo_T Wg Wu Wd".split())
    NT, E, CAP, B = (v[n] for n in "NT E CAP B".split())
    N = B * CAP
    with ExitStack() as ph, nc.Block() as block:
        def sb(name, shape, dt=F32):
            return ph.enter_context(nc.sbuf_tensor("e_" + name, shape, dt))

        def pb(name):
            return ph.enter_context(nc.psum_tensor("e_" + name, [P, 512], F32))

        def sem(name):
            return ph.enter_context(nc.semaphore("e_" + name))

        w_nat = sb("w_nat", [P, 2, 6, P])
        w_T = sb("w_T", [P, 2, 6, P])
        hg = sb("hg", [P, 2, 2 * N])
        h = sb("h", [P, 2, 2 * N])
        p_w0, p_w1, p_g0, p_g1, p_u0, p_u1, p_e0, p_e1 = (pb(n) for n in "w0 w1 g0 g1 u0 u1 e0 e1".split())
        p_g, p_u, p_e = (p_g0, p_g1), (p_u0, p_u1), (p_e0, p_e1)
        w_in = (sem("w_in0"), sem("w_in1"))
        turned, wT_gu, wT_d, gate_done, up_done, act_done, h_ready, down_done, out_ready = (
            sem(n) for n in ("turned", "wT_gu", "wT_d", "gate_done", "up_done", "act_done", "h_ready", "down_done",
                             "out_ready"))

        @block.sync
        def _(sp):
            def load(e, ep, n):
                wait(sp, turned, 2 * (e - 1))
                sp.dma_start(w_nat[:, ep, 0:2, :], Wg[e].rearrange("(c p) d -> p c d", p=P)).then_inc(w_in[ep], 16)
                sp.dma_start(w_nat[:, ep, 2:4, :], Wu[e].rearrange("(c p) d -> p c d", p=P)).then_inc(w_in[ep], 16)
                sp.dma_start(w_nat[:, ep, 4:6, :], Wd[e].rearrange("d (c f) -> d c f", f=P)).then_inc(w_in[ep], 16)

            load(0, 0, 0)
            load(1, 1, 0)
            with sp.Fori(1, E // 2) as j:
                load(2 * j, 0, j)
                load(2 * j + 1, 1, j)

        @block.tensor
        def _(pe):
            def turn(e, ep, turns):
                pe.wait_ge(w_in[ep], 48 * (turns + 1))
                wait(pe, wT_gu, e)
                for i in range(4):
                    last = nc.tensor.transpose(p_w0[:, i * P:(i + 1) * P], w_nat[:, ep, i, :], ident[:])
                last.then_inc(turned, 1)
                wait(pe, wT_d, e)
                for i in range(2):
                    last = nc.tensor.transpose(p_w1[:, i * P:(i + 1) * P], w_nat[:, ep, 4 + i, :], ident[:])
                last.then_inc(turned, 1)

            def up(e, ep):
                pe.wait_ge(wT_gu, e + 1)
                tokens = x_tok[:, e].rearrange("p t b c -> p (t b c)")
                wait(pe, act_done, e - 1)
                for i in range(2):
                    last = nc.tensor.matmul(p_g[ep][:, i * N:(i + 1) * N], w_T[:, ep, i, :], tokens,
                                            start=True, stop=True)
                last.then_inc(gate_done, 1)
                wait(pe, h_ready, e - 1)
                for i in range(2):
                    last = nc.tensor.matmul(p_u[ep][:, i * N:(i + 1) * N], w_T[:, ep, 2 + i, :], tokens,
                                            start=True, stop=True)
                last.then_inc(up_done, 1)

            def down(e, ep):
                pe.wait_ge(h_ready, e + 1)
                pe.wait_ge(wT_d, e + 1)
                wait(pe, out_ready, e - 1)
                for i in range(2):
                    last = nc.tensor.matmul(p_e[ep][:, 0:N], w_T[:, ep, 4 + i, :], h[:, ep, i * N:(i + 1) * N],
                                            start=(i == 0), stop=(i == 1))
                last.then_inc(down_done, 1)

            def both(e, ep, turns):
                turn(e + 1, 1 - ep, turns)
                down(e, ep)
                up(e + 1, 1 - ep)

            turn(0, 0, 0)
            up(0, 0)
            both(0, 0, 0)
            both(1, 1, 1)
            with pe.Fori(1, E // 2 - 1) as j:
                both(2 * j, 0, j)
                both(2 * j + 1, 1, j + 1)
            both(E - 2, 0, E // 2 - 1)
            down(E - 1, 1)

        @block.scalar
        def _(act):
            def front(e, ep):
                act.wait_ge(turned, 2 * e + 1)
                wait(act, up_done, e - 1)
                nc.scalar.copy(w_T[:, ep, 0:4, :].rearrange("p i k -> p (i k)"), p_w0[:]).then_inc(wT_gu, 1)

            def gelu(e, ep):
                act.wait_ge(gate_done, e + 1)
                wait(act, h_ready, e - 1)
                nc.scalar.activation(hg[:, ep, :], p_g[ep][:], ACT.Gelu).then_inc(act_done, 1)

            pipelined(act, E, lambda e, ep: (front(e, ep), gelu(e, ep)), lambda e, ep: None)

        @block.vector
        def _(dve):
            def front(e, ep):
                dve.wait_ge(turned, 2 * e + 2)
                wait(dve, down_done, e - 1)
                nc.vector.tensor_copy(w_T[:, ep, 4:6, :].rearrange("p i k -> p (i k)"), p_w1[:, 0:2 * P]).then_inc(wT_d, 1)

            def product(e, ep):
                dve.wait_ge(act_done, e + 1)
                dve.wait_ge(up_done, e + 1)
                wait(dve, down_done, e - 1)
                nc.vector.tensor_tensor(h[:, ep, :], hg[:, ep, :], p_u[ep][:], ALU.mult).then_inc(h_ready, 1)

            def back(e, ep):
                dve.wait_ge(down_done, e + 1)
                nc.vector.tensor_copy(eo_T[:, :, e, :], p_e[ep][:, 0:N].rearrange("p (b c) -> p b c", c=CAP))\
                    .then_inc(out_ready, 1)

            def both(e, ep):
                front(e + 1, 1 - ep)
                back(e, ep)
                product(e + 1, 1 - ep)

            pipelined(dve, E, lambda e, ep: (front(e, ep), product(e, ep)), back, both)


def combine(nc, v):
    xs, stats, ident, gates, ws_t = (v[n] for n in "xs stats ident gates ws_t".split())
    eo_T, sel_w, xnT_all = (v[n] for n in "eo_T sel_w xnT_all".split())
    NT, D, S, E, CAP = (v[n] for n in "NT D S E CAP".split())
    with ExitStack() as ph, nc.Block() as block:
        def sb(name, shape, dt=F32):
            return ph.enter_context(nc.sbuf_tensor("c_" + name, shape, dt))

        def pb(name):
            return ph.enter_context(nc.psum_tensor("c_" + name, [P, 512], F32))

        def sem(name):
            return ph.enter_context(nc.semaphore("c_" + name))

        staged = sb("staged", [P, 2, 3, P])
        turned = sb("turned", [P, 2, 3, P])
        hg = sb("hg", [P, 2, 2 * P])
        h = sb("h", [P, 2, 2, P])
        p_t0, p_t1, p_h0, p_h1, p_y0, p_y1 = (pb(n) for n in "t0 t1 h0 h1 y0 y1".split())
        p_t, p_h, p_y = (p_t0, p_t1), (p_h0, p_h1), (p_y0, p_y1)
        stage_ready, turn_done, turn_ready, up_done, act_done, h_ready, y_done, x_new = (
            sem(n) for n in ("stage_ready", "turn_done", "turn_ready", "up_done", "act_done", "h_ready", "y_done", "x_new"))

        @block.gpsimd
        def _(pool):
            def stage(t, tp):
                wait(pool, turn_done, t - 1)
                nc.gpsimd.tensor_copy(staged[:, tp, 0:2, :],
                                      eo_T[:, bass.ds(2 * t, 2), :, :].rearrange("p b e c -> p b (e c)"))
                nc.gpsimd.tensor_copy(staged[:, tp, 2, :], sel_w[:, t, :]).then_inc(stage_ready, 1)

            pipelined(pool, NT, stage, lambda t, tp: None)

        @block.tensor
        def _(pe):
            def front(t, tp):
                pe.wait_ge(stage_ready, t + 1)
                wait(pe, turn_ready, t - 1)
                for i in range(3):
                    last = nc.tensor.transpose(p_t[tp][:, i * P:(i + 1) * P], staged[:, tp, i, :], ident[:])
                last.then_inc(turn_done, 1)
                wait(pe, h_ready, t - 1)
                for i in range(4):
                    last = nc.tensor.matmul(p_h[tp][:, i * P:(i + 1) * P], ws_t[:, i, :], xnT_all[:, t, :],
                                            start=True, stop=True)
                last.then_inc(up_done, 1)

            def back(t, tp):
                pe.wait_ge(h_ready, t + 1)
                pe.wait_ge(turn_ready, t + 1)
                wait(pe, x_new, t - 1)
                for i in range(2):
                    nc.tensor.matmul(p_y[tp][:, 0:D], h[:, tp, i, :], ws_t[:, 4 + i, :], start=(i == 0), stop=False,
                                     skip_group_check=True)
                for b in range(2):
                    last = nc.tensor.matmul(p_y[tp][b * S:(b + 1) * S, 0:D], turned[:, tp, 2, b * S:(b + 1) * S],
                                            turned[:, tp, b, :], start=False, stop=True, skip_group_check=True)
                last.then_inc(y_done, 1)

            pipelined(pe, NT, front, back)

        @block.scalar
        def _(act):
            def front(t, tp):
                act.wait_ge(turn_done, t + 1)
                wait(act, y_done, t - 1)
                nc.scalar.copy(turned[:, tp].rearrange("p i k -> p (i k)"), p_t[tp][:, 0:3 * P]).then_inc(turn_ready, 1)
                act.wait_ge(up_done, t + 1)
                wait(act, h_ready, t - 1)
                nc.scalar.activation(hg[:, tp, :], p_h[tp][:, 0:2 * P], ACT.Gelu).then_inc(act_done, 1)

            pipelined(act, NT, front, lambda t, tp: None)

        @block.vector
        def _(dve):
            def front(t, tp):
                dve.wait_ge(act_done, t + 1)
                wait(dve, y_done, t - 1)
                nc.vector.tensor_tensor(h[:, tp].rearrange("p i k -> p (i k)"), hg[:, tp, :], p_h[tp][:, 2 * P:4 * P],
                                        ALU.mult).then_inc(h_ready, 1)

            def back(t, tp):
                dve.wait_ge(y_done, t + 1)
                nc.vector.scalar_tensor_tensor(xs[:, t, :], p_y[tp][:, 0:D], gates[:, 2:3], xs[:, t, :],
                                               ALU.mult, ALU.add).then_inc(x_new, 1)
                dve.wait_ge(x_new, t + 1)
                nc.vector.bn_stats(stats[:, 1, t, :], xs[:, t, :])

            pipelined(dve, NT, front, back)


def attention_1(nc, v):
    xs, cs, mean, rstd, stats, neghalf, ident, quad = (
        v[n] for n in "xs cs mean rstd stats neghalf ident quad".split())
    cols, rows, w_c = (v[n] for n in "cols rows w_c".split())
    NT, D, S, EPS = (v[n] for n in "NT D S EPS".split())
    G, DH = 4, 8
    HP = 2 * G
    with ExitStack() as ph, nc.Block() as block:
        def sb(name, shape, dt=F32):
            return ph.enter_context(nc.sbuf_tensor("a1_" + name, shape, dt))

        def pb(name, shape=(P, 512)):
            return ph.enter_context(nc.psum_tensor("a1_" + name, list(shape), F32))

        def sem(name):
            return ph.enter_context(nc.semaphore("a1_" + name))

        tmp = sb("tmp", [P, NT, 4])
        xn = sb("xn", [P, 2, 2, D])
        cT = sb("cT", [P, 2, 2, 2, S])
        xT = sb("xT", [P, 2, P])
        q = sb("q", [P, 2, 2, S])
        k4 = sb("k4", [P, 2, 2, 4, S])
        vals = sb("vals", [P, 2, HP, 2, 2, DH + 1])
        mx = sb("mx", [P, 2, G, 4])
        pr = sb("pr", [P, 2, 4 * G, S])
        prT = sb("prT", [P, 2, HP // 2, P])
        rs = sb("rs", [P, 2, 4 * G])
        att = sb("att", [P, 2, D])
        oT = sb("oT", [P, 2, 2 * S])
        xb = sb("xb", [P, 2, D])
        p_s = pb("s", (P, G, 512))
        p_T, p_qv, p_pT, p_o = (pb(n) for n in "T qv pT o".split())
        WIDE = 4 * (DH + 1)
        (var_ready, norm_ready, chain, zeroed, c_ready, xn_ready, turned, turned_out, qkv_done, q_ready,
         k4_ready, v_ready, scored, maxed, shifted, exped, pT_done, prT_ready, mixed, inverse, att_ready, aT_done,
         oT_ready, y_done, xb_ready, x_new) = (
            sem(n) for n in ("var_ready", "norm_ready", "chain", "zeroed", "c_ready", "xn_ready", "turned",
                             "turned_out", "qkv_done", "q_ready", "k4_ready", "v_ready", "scored", "maxed",
                             "shifted", "exped", "pT_done", "prT_ready", "mixed", "inverse", "att_ready", "aT_done",
                             "oT_ready", "y_done", "xb_ready", "x_new"))

        FIRST, LAST = -2, NT + 1

        @block.gpsimd
        def _(pool):
            pool.wait_ge(var_ready, 1)
            nc.gpsimd.tensor_tensor(rstd[:, 1, :], rstd[:, 1, :], neghalf[:, 0:NT], ALU.pow).then_inc(norm_ready, 1)

            def stage(t, tp):
                wait(pool, turned, t - 1)
                nc.gpsimd.tensor_copy(xn[:, tp, 0, :], cs[:, t, :]).then_inc(c_ready, 1)

            def biased(t, tp):
                wait(pool, x_new, t - 1)
                nc.gpsimd.tensor_tensor(xb[:, tp, :], xs[:, t, :], rows[:, 2, :], ALU.add).then_inc(xb_ready, 1)

            def turn(s, sp):
                if exists(s + 2, NT):
                    stage(s + 2, sp)
                if exists(s - 1, NT):
                    biased(s - 1, 1 - sp)

            turns(pool, NT, turn, FIRST, LAST)

        @block.tensor
        def _(pe):
            def turn_over(t, tp):
                pe.wait_ge(c_ready, t + 1)
                pe.wait_ge(xn_ready, t + 1)
                wait(pe, turned_out, 2 * t)
                wait(pe, k4_ready, t)
                nc.tensor.transpose(p_T[:, 0:P], xn[:, tp, 0, :], ident[:])
                nc.tensor.transpose(p_T[:, P:2 * P], xn[:, tp, 1, :], ident[:]).then_inc(turned, 1)

            def project(t, tp):
                pe.wait_ge(turned_out, 2 * t + 2)
                wait(pe, q_ready, t)
                wait(pe, v_ready, 4 * t)
                nc.tensor.matmul(p_T[:, 2 * P:3 * P], w_c[:, 1, :], cT[:, tp, :, 0, :], start=True, stop=True)
                nc.tensor.matmul(p_qv[:, 0:P], w_c[:, 0, :], xT[:, tp, :], start=True, stop=True)
                for b in range(2):
                    last = nc.tensor.matmul(p_qv[:, (1 + b) * P:(2 + b) * P], cT[:, tp, b].rearrange("p c s -> p (c s)"),
                                            w_c[:, 2, :], start=True, stop=True)
                last.then_inc(qkv_done, 1)

            def scores(t, tp, b):
                if b == 0:
                    pe.wait_ge(k4_ready, t + 1)
                    pe.wait_ge(q_ready, t + 1)
                    wait(pe, shifted, t)
                for g in range(G):
                    r = slice(32 * g, 32 * g + 32)
                    last = nc.tensor.matmul(p_s[b * S:(b + 1) * S, g, 0:4 * S], q[r, tp, b, :],
                                            k4[r, tp, b].rearrange("p h s -> p (h s)"), start=True, stop=True)
                if b == 1:
                    last.then_inc(scored, 1)

            def probs_T(t, tp, j):
                pe.wait_ge(exped, t + 1)
                wait(pe, prT_ready, 2 * t + j)
                for i in range(HP // 2):
                    n = j * HP // 2 + i
                    last = nc.tensor.transpose(p_pT[:, i * P:(i + 1) * P],
                                               pr[:, tp, 2 * n:2 * n + 2, :].rearrange("p h s -> p (h s)"), ident[:])
                last.then_inc(pT_done, 1)

            def mix(t, tp, j):
                pe.wait_ge(prT_ready, 2 * t + j + 1)
                pe.wait_ge(v_ready, 4 * t + 4)
                wait(pe, x_new, t)
                for i in range(HP // 2):
                    n = j * HP // 2 + i
                    last = nc.tensor.matmul(p_o[:, n * WIDE:(n + 1) * WIDE], prT[:, j, i, :],
                                            vals[:, tp, n].rearrange("p b h e -> p (b h e)"), start=True, stop=True)
                last.then_inc(mixed, 1)

            def att_T(t, tp):
                pe.wait_ge(att_ready, t + 1)
                nc.tensor.transpose(p_o[:, 320:320 + P], att[:, tp, :], ident[:]).then_inc(aT_done, 1)

            def out_proj(t, tp):
                pe.wait_ge(oT_ready, t + 1)
                nc.tensor.matmul(p_o[:, 0:D], oT[:, tp, :], w_c[:, 3, :], start=True, stop=True).then_inc(y_done, 1)

            def turn(s, sp):
                now, back, tail, ahead = exists(s, NT), exists(s - 1, NT), exists(s - 2, NT), exists(s + 1, NT)
                if now:
                    scores(s, sp, 0)
                if tail:
                    att_T(s - 2, sp)
                if now:
                    scores(s, sp, 1)
                if back:
                    probs_T(s - 1, 1 - sp, 0)
                if tail:
                    out_proj(s - 2, sp)
                if ahead:
                    project(s + 1, 1 - sp)
                if back:
                    probs_T(s - 1, 1 - sp, 1)
                    mix(s - 1, 1 - sp, 0)
                if exists(s + 2, NT):
                    turn_over(s + 2, sp)
                if back:
                    mix(s - 1, 1 - sp, 1)

            pe.wait_ge(zeroed, 3)
            turns(pe, NT, turn, FIRST, LAST)

        @block.scalar
        def _(act):
            def turn_out(t, tp):
                act.wait_ge(turned, t + 1)
                wait(act, qkv_done, t - 1)
                nc.scalar.copy(cT[:, tp], p_T[:, 0:P].rearrange("p (b s) -> p b s", b=2).unsqueeze(2)
                               .to_broadcast([P, 2, 2, S])).then_inc(turned_out, 1)
                nc.scalar.copy(xT[:, tp, :], p_T[:, P:2 * P]).then_inc(turned_out, 1)

            def queries_out(t, tp):
                act.wait_ge(qkv_done, t + 1)
                wait(act, scored, t - 1)
                nc.scalar.activation(q[:, tp].rearrange("p b s -> p (b s)"), p_qv[:, 0:P], ACT.Identity,
                                     bias=cols[:, 5:6]).then_inc(q_ready, 1)

            def values_out(t, tp):
                act.wait_ge(qkv_done, t + 1)
                wait(act, mixed, 2 * (t - 1))
                for b in range(2):
                    for a in range(2):
                        src = p_qv[a * S:(a + 1) * S, (1 + b) * P:(2 + b) * P].rearrange("p (n h e) -> p n h e", n=HP, h=2)
                        nc.scalar.copy(vals[a * S:(a + 1) * S, tp, :, b, a, 0:DH], src[:, :, a]).then_inc(v_ready, 1)

            def exp(t, tp):
                act.wait_ge(shifted, t + 1)
                flat = pr[:, tp].rearrange("p h s -> p (h s)")
                nc.scalar.activation(flat, flat, ACT.Exp).then_inc(exped, 1)

            def probs_out(t, b):
                act.wait_ge(pT_done, 2 * t + b + 1)
                wait(act, mixed, 2 * (t - 1) + b + 1)
                nc.scalar.copy(prT[:, b].rearrange("p i k -> p (i k)"), p_pT[:]).then_inc(prT_ready, 1)

            def att_out(t, tp):
                act.wait_ge(aT_done, t + 1)
                wait(act, y_done, t)
                nc.scalar.activation(oT[:, tp, :], p_o[:, 320:320 + P], ACT.Identity, bias=cols[:, 7:8]).then_inc(oT_ready, 1)

            def turn(s, sp):
                back, ahead = exists(s - 1, NT), exists(s + 1, NT)
                if exists(s - 2, NT):
                    att_out(s - 2, sp)
                if back:
                    probs_out(s - 1, 0)
                if ahead:
                    queries_out(s + 1, 1 - sp)
                if back:
                    probs_out(s - 1, 1)
                if ahead:
                    values_out(s + 1, 1 - sp)
                if exists(s + 2, NT):
                    turn_out(s + 2, sp)
                if exists(s, NT):
                    exp(s, sp)

            act.wait_ge(zeroed, 3)
            turns(act, NT, turn, FIRST, LAST)

        @block.vector
        def _(dve):
            finish_stats(nc, dve, Steps(dve, chain), stats, mean, rstd, tmp, D, EPS).then_inc(var_ready, 1)
            nc.vector.memset(vals[:], 0.0).then_inc(zeroed, 1)
            dve.wait_ge(zeroed, 1)
            for a in range(2):
                last = nc.vector.memset(vals[a * S:(a + 1) * S, :, :, :, a, DH:DH + 1].rearrange("p x n b o -> p (x n b) o"), 1.0)
                last.then_inc(zeroed, 1)
            dve.wait_ge(norm_ready, 1)
            s4 = p_s[:, :, 0:4 * S].rearrange("p g (i s) -> p g i s", s=S)

            def normalise(t, tp):
                wait(dve, turned, t - 1)
                nc.vector.tensor_scalar(xn[:, tp, 1, :], xs[:, t, :], mean[:, 1, bass.ds(t, 1)], rstd[:, 1, bass.ds(t, 1)],
                                        ALU.subtract, ALU.mult).then_inc(xn_ready, 1)

            def keys(t, tp):
                dve.wait_ge(qkv_done, t + 1)
                wait(dve, scored, t - 1)
                for b in range(2):
                    last = nc.vector.scalar_tensor_tensor(
                        k4[:, tp, b], p_T[:, 2 * P + b * S:2 * P + (b + 1) * S].unsqueeze(1).to_broadcast([P, 4, S]),
                        cols[:, 6:7], quad[:].unsqueeze(2).to_broadcast([P, 4, S]), ALU.add, ALU.mult)
                last.then_inc(k4_ready, 1)

            def row_max(t, tp):
                dve.wait_ge(scored, t + 1)
                nc.vector.tensor_reduce(mx[:, tp], s4, AX.X, ALU.max).then_inc(maxed, 1)

            def shift(t, tp):
                dve.wait_ge(maxed, t + 1)
                wait(dve, pT_done, 2 * (t - 1))
                nc.vector.tensor_tensor(pr[:, tp].rearrange("p (g h) s -> p g h s", g=G), s4,
                                        mx[:, tp].unsqueeze(3).to_broadcast([P, G, 4, S]),
                                        ALU.subtract).then_inc(shifted, 1)

            def attend(t, tp):
                dve.wait_ge(mixed, 2 * t + 2)
                o5 = p_o[:, 0:HP * WIDE].rearrange("p (n b h e) -> p n b h e", n=HP, b=2, h=2)
                nc.vector.reciprocal(rs[:, tp, :].rearrange("p (n h) -> p n h", h=2), o5[:, :, 0, :, DH])\
                    .then_inc(inverse, 1)
                dve.wait_ge(inverse, t + 1)
                wait(dve, aT_done, t)
                for b in range(2):
                    r = slice(b * S, (b + 1) * S)
                    last = nc.vector.tensor_tensor(att[r, tp, :].rearrange("p (n h e) -> p n h e", n=HP, h=2),
                                                   o5[r, :, b, :, 0:DH],
                                                   rs[r, tp, :].rearrange("p (n h) -> p n h", h=2).unsqueeze(3)
                                                   .to_broadcast([S, HP, 2, DH]), ALU.mult)
                last.then_inc(att_ready, 1)

            def output(t, tp):
                dve.wait_ge(y_done, t + 1)
                dve.wait_ge(xb_ready, t + 1)
                nc.vector.tensor_tensor(xs[:, t, :], p_o[:, 0:D], xb[:, tp, :], ALU.add).then_inc(x_new, 1)

            def next_stats(t):
                dve.wait_ge(x_new, t + 1)
                nc.vector.bn_stats(stats[:, 1, t, :], xs[:, t, :])

            def turn(s, sp):
                now, tail = exists(s, NT), exists(s - 2, NT)
                if tail:
                    attend(s - 2, sp)
                if exists(s + 2, NT):
                    normalise(s + 2, sp)
                if now:
                    row_max(s, sp)
                if tail:
                    output(s - 2, sp)
                if exists(s + 1, NT):
                    keys(s + 1, 1 - sp)
                if now:
                    shift(s, sp)
                if tail:
                    next_stats(s - 2)

            turns(dve, NT, turn, FIRST, LAST)


def ffn_1(nc, v, o_tiles):
    xs, mean, rstd, stats, neghalf, identb = (v[n] for n in "xs mean rstd stats neghalf identb".split())
    gates, rows, b1row, w1_t, w2_t, wmean = (v[n] for n in "gates rows b1row w1_t w2_t wmean".split())
    NT, D, FF, EPS, MAGIC = (v[n] for n in "NT D FF EPS MAGIC".split())
    C = FF // P
    with ExitStack() as ph, nc.Block() as block:
        def sb(name, shape, dt=F32):
            return ph.enter_context(nc.sbuf_tensor("f_" + name, shape, dt))

        def pb(name, dt=F32, n=512):
            return ph.enter_context(nc.psum_tensor("f_" + name, [P, n], dt))

        def sem(name):
            return ph.enter_context(nc.semaphore("f_" + name))

        tmp = sb("tmp", [P, NT, 4])
        hn = sb("hn", [P, 2, D])
        hq = sb("hq", [P, 2, D], BF16)
        hT = sb("hT", [P, 2, P], BF16)
        hid = sb("hid", [P, 2, FF])
        ge = sb("ge", [P, 2, FF])
        gq = sb("gq", [P, 2, FF], BF16)
        gT = sb("gT", [P, 2, C, P], BF16)
        small = sb("small", [P, 2, 2, 4])
        wback = sb("wback", [P, 2])
        xb = sb("xb", [P, 2, D])
        p_a0, p_a1 = pb("a0", BF16, 1024), pb("a1", BF16, 1024)
        p_b0, p_b1 = pb("b0", BF16, 1024), pb("b1", BF16, 1024)
        p_h0, p_h1, p_y0, p_y1 = (pb(n) for n in "h0 h1 y0 y1".split())
        p_a, p_b, p_h, p_y = (p_a0, p_a1), (p_b0, p_b1), (p_h0, p_h1), (p_y0, p_y1)
        (var_ready, norm_ready, chain, norm_chain, hq_ready, aT_done, aT_ready, up_done, hid_ready, gelu_done,
         quant_chain, gq_ready, bT_done, bT_ready, y_done, xb_ready, x_new, stored) = (
            sem(n) for n in ("var_ready", "norm_ready", "chain", "norm_chain", "hq_ready", "aT_done", "aT_ready",
                             "up_done", "hid_ready", "gelu_done", "quant_chain", "gq_ready", "bT_done", "bT_ready",
                             "y_done", "xb_ready", "x_new", "stored"))

        @block.sync
        def _(sp):
            with sp.Fori(0, NT) as t:
                sp.wait_ge(x_new, t + 1)
                sp.dma_start(o_tiles[:, t, :], xs[:, t, :]).then_inc(stored, 16)
            sp.wait_ge(stored, 16 * NT)

        @block.gpsimd
        def _(pool):
            pool.wait_ge(var_ready, 1)
            nc.gpsimd.tensor_tensor(rstd[:, 1, :], rstd[:, 1, :], neghalf[:, 0:NT], ALU.pow).then_inc(norm_ready, 1)

            def front(t, tp):
                wait(pool, x_new, t - 1)
                nc.gpsimd.tensor_tensor(xb[:, tp, :], xs[:, t, :], rows[:, 3, :], ALU.add).then_inc(xb_ready, 1)

            pipelined(pool, NT, front, lambda t, tp: None)

        @block.tensor
        def _(pe):
            def turn(t, tp):
                pe.wait_ge(hq_ready, t + 1)
                wait(pe, aT_ready, t - 1)
                nc.tensor.transpose(p_a[tp][:, 0:P], hq[:, tp, :], identb[:]).then_inc(aT_done, 1)

            def up(t, tp):
                pe.wait_ge(aT_ready, t + 1)
                wait(pe, hid_ready, t - 1)
                nc.tensor.matmul(p_h[tp][:], hT[:, tp, :], w1_t[:], start=True, stop=True).then_inc(up_done, 1)

            def turn_hidden(t, tp):
                pe.wait_ge(gq_ready, t + 1)
                wait(pe, bT_ready, t - 1)
                for c in range(C):
                    last = nc.tensor.transpose(p_b[tp][:, c * P:(c + 1) * P], gq[:, tp, c * P:(c + 1) * P], identb[:])
                last.then_inc(bT_done, 1)

            def down(t, tp):
                pe.wait_ge(bT_ready, t + 1)
                wait(pe, x_new, t - 1)
                for c in range(C):
                    last = nc.tensor.matmul(p_y[tp][:, 0:D], gT[:, tp, c, :], w2_t[:, c, :], start=(c == 0), stop=(c == C - 1))
                last.then_inc(y_done, 1)

            def both(t, tp):
                turn(t + 1, 1 - tp)
                turn_hidden(t, tp)
                up(t + 1, 1 - tp)
                down(t, tp)

            pipelined(pe, NT, lambda t, tp: (turn(t, tp), up(t, tp)),
                      lambda t, tp: (turn_hidden(t, tp), down(t, tp)), both)

        @block.scalar
        def _(act):
            def front(t, tp):
                act.wait_ge(aT_done, t + 1)
                wait(act, up_done, t - 1)
                nc.scalar.copy(hT[:, tp, :], p_a[tp][:, 0:P]).then_inc(aT_ready, 1)

            def gelu(t, tp):
                act.wait_ge(hid_ready, t + 1)
                wait(act, gq_ready, t - 1)
                nc.scalar.activation(ge[:, tp, :], hid[:, tp, :], ACT.Gelu).then_inc(gelu_done, 1)

            def back(t, tp):
                act.wait_ge(bT_done, t + 1)
                wait(act, y_done, t - 1)
                nc.scalar.copy(gT[:, tp].rearrange("p c k -> p (c k)"), p_b[tp][:, 0:FF]).then_inc(bT_ready, 1)

            def both(t, tp):
                front(t + 1, 1 - tp)
                back(t, tp)
                gelu(t + 1, 1 - tp)

            pipelined(act, NT, lambda t, tp: (front(t, tp), gelu(t, tp)), back, both)

        @block.vector
        def _(dve):
            step = Steps(dve, chain)
            step(nc.vector.tensor_scalar(wback[:], wmean[:], 1.0 / 127.0, None, ALU.mult))
            step(nc.vector.tensor_scalar(wback[:, 1:2], wback[:, 1:2], gates[:, 3:4], None, ALU.mult))
            finish_stats(nc, dve, step, stats, mean, rstd, tmp, D, EPS).then_inc(var_ready, 1)
            dve.wait_ge(norm_ready, 1)

            def quantise(step, src, dst, sm, layer):
                step(nc.vector.tensor_reduce(sm[:, 0:1], src, AX.X, ALU.max, apply_absolute_value=True))
                step(nc.vector.tensor_scalar(sm[:, 0:1], sm[:, 0:1], EPS, None, ALU.max))
                step(nc.vector.reciprocal(sm[:, 1:2], sm[:, 0:1]))
                step(nc.vector.tensor_scalar(sm[:, 2:3], sm[:, 0:1], wback[:, layer:layer + 1], None, ALU.mult))
                step(nc.vector.tensor_scalar(sm[:, 1:2], sm[:, 1:2], 127.0, None, ALU.mult))
                step(nc.vector.tensor_scalar(src, src, sm[:, 1:2], MAGIC, ALU.mult, ALU.add))
                return nc.vector.tensor_scalar(dst, src, MAGIC, 127.0, ALU.subtract, ALU.min)

            def norm(t, tp):
                step = Steps(dve, norm_chain, 8 * t)
                step(nc.vector.scalar_tensor_tensor(hn[:, tp, :], xs[:, t, :], mean[:, 1, bass.ds(t, 1)], rows[:, 4, :],
                                                    ALU.subtract, ALU.mult))
                step(nc.vector.scalar_tensor_tensor(hn[:, tp, :], hn[:, tp, :], rstd[:, 1, bass.ds(t, 1)], rows[:, 5, :],
                                                    ALU.mult, ALU.add))
                wait(dve, aT_done, t - 1)
                quantise(step, hn[:, tp, :], hq[:, tp, :], small[:, tp, 0, :], 0).then_inc(hq_ready, 1)

            def hidden(t, tp):
                dve.wait_ge(up_done, t + 1)
                wait(dve, gelu_done, t - 1)
                nc.vector.scalar_tensor_tensor(hid[:, tp, :], p_h[tp][:], small[:, tp, 0, 2:3], v["b1row"][:],
                                               ALU.mult, ALU.add).then_inc(hid_ready, 1)

            def requantise(t, tp):
                dve.wait_ge(gelu_done, t + 1)
                wait(dve, bT_done, t - 1)
                quantise(Steps(dve, quant_chain, 6 * t), ge[:, tp, :], gq[:, tp, :], small[:, tp, 1, :], 1)\
                    .then_inc(gq_ready, 1)

            def output(t, tp):
                dve.wait_ge(y_done, t + 1)
                dve.wait_ge(xb_ready, t + 1)
                nc.vector.scalar_tensor_tensor(xs[:, t, :], p_y[tp][:, 0:D], small[:, tp, 1, 2:3], xb[:, tp, :],
                                               ALU.mult, ALU.add).then_inc(x_new, 1)

            def both(t, tp):
                norm(t + 1, 1 - tp)
                requantise(t, tp)
                hidden(t + 1, 1 - tp)
                output(t, tp)

            pipelined(dve, NT, lambda t, tp: (norm(t, tp), hidden(t, tp)),
                      lambda t, tp: (requantise(t, tp), output(t, tp)), both)


_INS = ["x", "ctx_1024", "mask_BxS2_bk0", "g_xattn", "g_ffn",
        "L0_xattn_ln_x_w", "L0_xattn_ln_x_b", "L0_xattn_ln_l_w", "L0_xattn_ln_l_b", "L0_xattn_Wq", "L0_xattn_Wkv",
        "L0_xattn_q_scale", "L0_xattn_k_scale", "L0_xattn_Wo", "L0_xattn_ln_o_w", "L0_xattn_ln_o_b",
        "L0_ffn_gate_w", "L0_ffn_Wg", "L0_ffn_Wu", "L0_ffn_Wd", "L0_ffn_Ws_g", "L0_ffn_Ws_u", "L0_ffn_Ws_d",
        "L1_xattn_wq_w", "L1_xattn_wq_b", "L1_xattn_wk_w", "L1_xattn_wk_b", "L1_xattn_wv_w", "L1_xattn_wv_b",
        "L1_xattn_wo_w", "L1_xattn_wo_b", "L1_ffn_w1", "L1_ffn_b1", "L1_ffn_w2", "L1_ffn_b2", "L1_ffn_gamma",
        "L1_ffn_beta"]
_OUTS = [((32, 64, 128), "float32")]


def kernel(**inputs):
    import numpy as _np
    import concourse.bacc as _bacc
    from concourse import mybir as _mybir
    from concourse.bass_utils import run_bass_kernel_spmd as _run

    nc = _bacc.Bacc("TRN2", target_bir_lowering=False, num_devices=1)
    arrays, args = {}, []
    for name in _INS:
        a = _np.ascontiguousarray(inputs[name])
        arrays[f"in_{name}_dram"] = a
        args.append(nc.dram_tensor(f"in_{name}_dram", a.shape, _mybir.dt.from_np(a.dtype), kind="ExternalInput").ap())
    for i, (shape, dtype) in enumerate(_OUTS):
        dt = _mybir.dt.from_np(_np.dtype(dtype))
        args.append(nc.dram_tensor(f"out_{i}_dram", shape, dt, kind="ExternalOutput").ap())
    build(nc, *args)
    r = _run(nc, [arrays], core_ids=[0])
    got = tuple(r.results[0][f"out_{i}_dram"] for i in range(len(_OUTS)))
    return got[0]
```

```python
from contextlib import ExitStack

import concourse.bass as bass
from concourse import mybir

ALU = mybir.AluOpType
ACT = mybir.ActivationFunctionType
AX = mybir.AxisListType
F32 = mybir.dt.float32
BF16 = mybir.dt.bfloat16
U8 = mybir.dt.uint8
U32 = mybir.dt.uint32

P = 128


def wait(eng, sem, count):
    if isinstance(count, int) and count <= 0:
        return
    eng.wait_ge(sem, count)


class Steps:

    def __init__(self, eng, sem, base=0):
        self.eng, self.sem, self.base, self.n = eng, sem, base, 0

    def __call__(self, ins):
        self.n += 1
        ins.then_inc(self.sem, 1)
        self.eng.wait_ge(self.sem, self.base + self.n)


def turns(eng, tiles, turn, first, last):
    for s in range(first, 3):
        turn(s, s % 2)
    ahead = -first
    passes = (tiles - ahead - 3) // 2
    with eng.Fori(0, passes) as j:
        turn(2 * j + 3, 1)
        turn(2 * j + 4, 0)
    for s in range(3 + 2 * passes, last + 1):
        turn(s, s % 2)


def exists(t, tiles):
    return not isinstance(t, int) or 0 <= t < tiles


def next_norm(nc, v, ph, name):
    xs, moments, eps_row, neghalf = (v[n] for n in "xs moments eps_row neghalf".split())
    stats, mv, spare = (
        ph.enter_context(nc.sbuf_tensor(f"{name}_n{n}", [P, 2, k], F32)) for n, k in (("st", 6), ("mv", 2), ("sp", 1)))
    stats_ready, mv_ready, var_ready = (
        ph.enter_context(nc.semaphore(f"{name}_{n}")) for n in ("stats_ready", "mv_ready", "var_ready"))

    def row_stats(dve, t, tp, x_new):
        dve.wait_ge(x_new, t + 1)
        nc.vector.memset(spare[:, tp, :], 0.0)
        nc.vector.bn_stats(stats[:, tp, :], xs[:, t, :]).then_inc(stats_ready, 1)

    def row_moments(dve, t, tp):
        dve.wait_ge(stats_ready, t + 1)
        nc.vector.memset(spare[:, tp, :], 0.0)
        nc.vector.bn_aggr(mv[:, tp, :], stats[:, tp, :]).then_inc(mv_ready, 1)

    def keep_moments(dve, t, tp):
        dve.wait_ge(mv_ready, t + 1)
        nc.vector.tensor_tensor(moments[:, 1, t, :], mv[:, tp, :], eps_row[:], ALU.add).then_inc(var_ready, 1)

    def inverse_root(pool, t):
        pool.wait_ge(var_ready, t + 1)
        nc.gpsimd.tensor_tensor(moments[:, 1, t, 1:2], moments[:, 1, t, 1:2], neghalf[:, 0:1], ALU.pow)

    return row_stats, row_moments, keep_moments, inverse_root


def build(nc, x, ctx, mask, g_xattn, g_ffn, ln_x_w, ln_x_b, ln_l_w, ln_l_b, Wq, Wkv, q_scale, k_scale, Wo,
          ln_o_w, ln_o_b, gate_w, Wg, Wu, Wd, Ws_g, Ws_u, Ws_d, wq_w, wq_b, wk_w, wk_b, wv_w, wv_b,
          wo_w, wo_b, w1, b1, w2, b2, gamma, beta, out):
    B, S, D = x.shape
    NT = B * S // P
    E = Wg.shape[0]
    CAP = S * 2 // E
    FE = Wg.shape[1]
    INNER = Wq.shape[1]
    DH0 = q_scale.shape[0]
    H0 = INNER // DH0
    HP = H0 // 2
    FF = w1.shape[0]
    EPS = 1e-5
    MAGIC = 1.5 * 2.0 ** 23
    NEG = -1e30

    x_tiles = x.rearrange("b s d -> (b s) d").rearrange("(t p) d -> p t d", p=P)
    c_tiles = ctx.rearrange("b s d -> (b s) d").rearrange("(t p) d -> p t d", p=P)
    o_tiles = out.rearrange("b s d -> (b s) d").rearrange("(t p) d -> p t d", p=P)

    with ExitStack() as whole:
        def sb(name, shape, dt=F32, at=whole):
            return at.enter_context(nc.sbuf_tensor(name, shape, dt))

        def sem(name, at=whole):
            return at.enter_context(nc.semaphore(name))

        xs = sb("xs", [P, NT, D])
        cs = sb("cs", [P, NT, D])
        moments = sb("moments", [P, 2, NT, 2])
        eps_row = sb("eps_row", [P, 2])
        neghalf = sb("neghalf", [P, 2 * NT])
        ident = sb("ident", [P, P])
        identb = sb("identb", [P, P], BF16)
        tokid = sb("tokid", [P, 1])
        quad = sb("quad", [P, 4])
        gates = sb("gates", [P, 4])
        cols = sb("cols", [P, 12])
        rows = sb("rows", [P, 6, D])
        b1row = sb("b1row", [P, FF])
        wq_a = sb("wq_a", [P, INNER])
        wkv_a = sb("wkv_a", [P, 2 * INNER])
        wo_a = sb("wo_a", [P, HP // 2, 2, D])
        maskrow = sb("maskrow", [1, B, S], U8)
        maskbias = sb("maskbias", [1, NT, 4, S], BF16)
        ones = sb("ones", [1, P], BF16)
        gw_t = sb("gw_t", [P, E])
        ws_t = sb("ws_t", [P, 6, P])
        w_c = sb("w_c", [P, 4, P])
        w1_t = sb("w1_t", [P, FF], BF16)
        w2_t = sb("w2_t", [P, FF // P, P], BF16)
        wmean = sb("wmean", [P, 2])

        wa_in = sem("wa_in")
        late_in = sem("late_in")
        LATE = 16 * 18
        FIRST_TILES = 2
        nat = sb("nat", [P, 6, P])
        nat_c = sb("nat_c", [P, 4, P])
        nat_g = sb("nat_g", [E, P])
        nat_1 = sb("nat_1", [P, FF // P, P])
        nat_2 = sb("nat_2", [P, FF])
        with ExitStack() as ph, nc.Block() as block:
            rows_in, cols_in, gates_in, mask_in = (sem(n, ph) for n in ("rows_in", "cols_in", "gates_in", "mask_in"))
            x_in = [sem(f"x_in{c}", ph) for c in range(4)]
            c_in = [sem(f"c_in{c}", ph) for c in range(4)]
            s_const, s_dve, s_gate, s_stats, s_pool = (
                sem(n, ph) for n in ("s_const", "s_dve", "s_gate", "s_stats", "s_pool"))
            tokrow = sb("tokrow", [P, P], at=ph)
            tmp = sb("tmp", [P, P], at=ph)
            tmp2 = sb("tmp2", [P, 2, NT, 4], at=ph)
            stats = sb("stats", [P, 2, NT, 6], at=ph)
            tmp3 = sb("tmp3", [P, P // 8], at=ph)
            gin = sb("gin", [P, 4], at=ph)

            @block.sync
            def _(sp):
                for c in range(4):
                    n = NT // 4
                    sp.dma_start(xs[:, c * n:(c + 1) * n, :], x_tiles[:, c * n:(c + 1) * n, :]).then_inc(x_in[c], 16)
                sp.dma_start(wq_a[:], Wq).then_inc(wa_in, 16)
                sp.dma_start(wkv_a[:], Wkv).then_inc(wa_in, 16)
                for a in range(2):
                    for j in range(HP // 2):
                        src = Wo.rearrange("(j a h d) n -> j a d h n", j=HP // 2, a=2, h=2)[j, a]
                        sp.dma_start(wo_a[a * DH0:(a + 1) * DH0, j], src).then_inc(wa_in, 16)

            @block.scalar
            def _(act):
                for c in range(4):
                    n = NT // 4
                    act.dma_start(cs[:, c * n:(c + 1) * n, :], c_tiles[:, c * n:(c + 1) * n, :]).then_inc(c_in[c], 16)
                for i, v in enumerate((g_xattn, g_ffn)):
                    act.dma_start(gin[:, 2 * i:2 * i + 2], v.rearrange("(o d) -> o d", o=1).to_broadcast([P, 2])).then_inc(gates_in, 16)
                for i, v in enumerate((ln_o_w, ln_o_b)):
                    act.dma_start(rows[:, i, :], v.rearrange("(o d) -> o d", o=1).to_broadcast([P, D])).then_inc(rows_in, 16)
                act.wait_ge(mask_in, 16)
                nc.scalar.activation(maskbias[:, :, 0:4:3, :], maskrow[:].rearrange("o (t b) s -> o t b s", b=2),
                                     ACT.Copy, scale=-NEG, bias=NEG)
                nc.scalar.activation(maskbias[:, :, 1:3, :], maskrow[:].rearrange("o (t b) s -> o t b s", b=2),
                                     ACT.Copy, scale=0.0)
                act.wait_ge(gates_in, 32)
                nc.scalar.activation(gates[:], gin[:], ACT.Tanh).then_inc(s_gate, 1)

            @block.gpsimd
            def _(pool):
                pc = Steps(pool, s_pool)
                pc(nc.gpsimd.memset(ident[:], 0.0))
                pc(nc.gpsimd.affine_select(out=ident[:], in_=ident[:], compare_op=ALU.not_equal, fill=1.0,
                                           base=0, pattern=[[-1, P]], channel_multiplier=1))
                nc.gpsimd.iota(tokrow[:], pattern=[[0, 2], [1, S]], base=0, channel_multiplier=0,
                               allow_small_or_imprecise_dtypes=True).then_inc(s_const, 1)
                pool.dma_start(maskrow[:], mask.rearrange("(o b) s -> o b s", o=1)).then_inc(mask_in, 16)
                for i, v in enumerate((ln_x_w, ln_x_b, ln_l_w, ln_l_b)):
                    pool.dma_start(cols[:, i:i + 1], v.rearrange("(d o) -> d o", o=1)).then_inc(cols_in, 16)
                for i, v in ((8, q_scale), (9, k_scale)):
                    for a in range(2):
                        pool.dma_start(cols[a * DH0:(a + 1) * DH0, i:i + 1],
                                       v.rearrange("(d o) -> d o", o=1)).then_inc(cols_in, 16)
                pool.wait_ge(s_stats, 1)
                nc.gpsimd.tensor_tensor(moments[:, :, 0:FIRST_TILES, 1], moments[:, :, 0:FIRST_TILES, 1],
                                        neghalf[:, 0:2 * FIRST_TILES].rearrange("p (a t) -> p a t", a=2), ALU.pow)

            @block.vector
            def _(dve):
                d = Steps(dve, s_dve)
                nc.vector.memset(neghalf[:], -0.5)
                nc.vector.memset(eps_row[:, 0:1], 0.0)
                nc.vector.memset(eps_row[:, 1:2], EPS)
                nc.vector.memset(ones[:], 1.0)
                dve.wait_ge(s_pool, 2)
                dve.wait_ge(s_const, 1)
                nc.vector.tensor_copy(identb[:], ident[:])
                nc.vector.tensor_tensor(tmp[:], ident[:], tokrow[:], ALU.mult)
                d(nc.vector.tensor_reduce(tmp3[:], ident[:].rearrange("p (h e) -> p h e", e=8), AX.X, ALU.add))
                nc.vector.tensor_reduce(tokid[:], tmp[:], AX.X, ALU.add)
                d(nc.vector.tensor_reduce(quad[:], tmp3[:].rearrange("p (g h) -> p h g", h=4), AX.X, ALU.add))
                nc.vector.tensor_scalar(quad[:], quad[:], 8.0 ** -0.5, None, ALU.mult)
                for c in range(4):
                    for which, src, landed in ((1, xs, x_in), (0, cs, c_in)):
                        dve.wait_ge(landed[c], 16)
                        for t in range(c * NT // 4, (c + 1) * NT // 4):
                            last = nc.vector.bn_stats(stats[:, which, t, :], src[:, t, :])
                d(last)
                m_sum, m_dif, var = tmp2[:, :, :, 0], tmp2[:, :, :, 1], tmp2[:, :, :, 2]
                nc.vector.tensor_tensor(m_sum, stats[:, :, :, 1], stats[:, :, :, 4], ALU.add)
                nc.vector.tensor_tensor(var, stats[:, :, :, 2], stats[:, :, :, 5], ALU.add)
                d(nc.vector.tensor_tensor(m_dif, stats[:, :, :, 1], stats[:, :, :, 4], ALU.subtract))
                nc.vector.tensor_scalar(moments[:, :, :, 0], m_sum, 0.5, None, ALU.mult)
                d(nc.vector.scalar_tensor_tensor(m_dif, m_dif, 0.25, m_dif, ALU.mult, ALU.mult))
                d(nc.vector.scalar_tensor_tensor(var, var, 1.0 / D, m_dif, ALU.mult, ALU.add))
                nc.vector.tensor_scalar(moments[:, 0, :, 1], var[:, 0], EPS, None, ALU.add)
                nc.vector.tensor_scalar(moments[:, 1, :, 1], var[:, 1], 1.0 + EPS, EPS * EPS, ALU.mult, ALU.add).then_inc(s_stats, 1)
                dve.wait_ge(cols_in, 16 * 8)
                nc.vector.scalar_tensor_tensor(cols[:, 4:5], cols[:, 8:9], 8.0, cols[:, 9:10], ALU.mult, ALU.mult)
                dve.wait_ge(s_gate, 1)
                dve.wait_ge(rows_in, 32)
                nc.vector.tensor_scalar(rows[:, 0:2, :], rows[:, 0:2, :], gates[:, 0:1], None, ALU.mult)

        attention_0(nc, locals())
        with ExitStack() as moe:
            x_tok = sb("x_tok", [P, E, NT, 2, CAP], at=moe)
            eo_T = sb("eo_T", [P, B, E, CAP], at=moe)
            sel_w = sb("sel_w", [P, NT, E * CAP], at=moe)
            xnT_all = sb("xnT_all", [P, NT, P], at=moe)
            w_nat = sb("w_nat", [P, 2, 6, P], at=moe)
            w_in = (sem("w_in0", moe), sem("w_in1", moe))
            routing(nc, locals())
            experts(nc, locals())
            combine(nc, locals())
        attention_1(nc, locals())
        ffn_1(nc, locals(), o_tiles)


def attention_0(nc, v):
    xs, cs, moments, neghalf, ident = (v[n] for n in "xs cs moments neghalf ident".split())
    cols, rows, wq_a, wkv_a, wo_a, maskbias, ones = (
        v[n] for n in "cols rows wq_a wkv_a wo_a maskbias ones".split())
    NT, D, S, INNER, H0, HP, DH0, EPS, FF = (v[n] for n in "NT D S INNER H0 HP DH0 EPS FF".split())
    FIRST_TILES, late_in, nat, nat_c, nat_g, nat_1, nat_2, b1row = (
        v[n] for n in "FIRST_TILES late_in nat nat_c nat_g nat_1 nat_2 b1row".split())
    Ws_g, Ws_u, Ws_d, gate_w, wq_w, wk_w, wv_w, wo_w, w1, w2, wq_b, wk_b, wv_b, wo_b, b1, b2, gamma, beta = (
        v[n] for n in "Ws_g Ws_u Ws_d gate_w wq_w wk_w wv_w wo_w w1 w2 wq_b wk_b wv_b wo_b b1 b2 gamma beta".split())
    with ExitStack() as ph, nc.Block() as block:
        def sb(name, shape, dt=F32):
            return ph.enter_context(nc.sbuf_tensor("a0_" + name, shape, dt))

        def pb(name):
            return ph.enter_context(nc.psum_tensor("a0_" + name, [P, 512], F32))

        def sem(name):
            return ph.enter_context(nc.semaphore("a0_" + name))

        xn = sb("xn", [P, 2, 2, D])
        kvT = sb("kvT", [P, 2, 4 * S])
        sq = sb("sq", [P, 2, INNER])
        ssq = sb("ssq", [P, 2, 3, H0])
        rn = sb("rn", [P, 2, 3, H0])
        qn = sb("qn", [P, 2, INNER])
        kn = sb("kn", [P, 2, INNER])
        qbd = sb("qbd", [P, 2, 2, HP, 2, S])
        kT = sb("kT", [P, 2, 2, HP, P])
        vaug = sb("vaug", [P, 2, 2, H0, DH0 + 1])
        mx = sb("mx", [P, 2, HP])
        pr = sb("pr", [P, 2, HP, P])
        prT = sb("prT", [P, 2, HP, P])
        rsum = sb("rsum", [P, 2, HP])
        att = sb("att", [P, 2, HP, DH0])
        attT = sb("attT", [P, 2, HP // 2, 2, 2, S])
        xb = sb("xb", [P, 2, D])
        yst = sb("yst", [P, 2, 6])
        ymv = sb("ymv", [P, 2, 2])
        yr = sb("yr", [P, 2, 1])
        yw = sb("yw", [P, 2, D])
        spare = sb("spare", [P, 1])
        p_q, p_k0, p_k1, p_v, p_tr, p_s, p_pT, p_o = (pb(n) for n in "q k0 k1 v tr s pT o".split())
        qk_bank = (p_q, p_k0, p_k1)
        vproj_done, norms_ready = (sem(n) for n in ("vproj_done", "norms_ready"))
        row_stats, row_moments, keep_moments, inverse_root = next_norm(nc, v, ph, "a0")
        zeroed, xn_ready, xT_done, kvT_ready, proj_done, squared, reduced, normed, scaled, v_ready = (
            sem(n) for n in ("zeroed", "xn_ready", "xT_done", "kvT_ready", "proj_done", "squared", "reduced",
                             "normed", "scaled", "v_ready"))
        turned, turned_out, scored, shifted, exped, pT_done, prT_ready, mixed, att_ready, attT_done, attT_ready = (
            sem(n) for n in ("turned", "turned_out", "scored", "shifted", "exped", "pT_done", "prT_ready", "mixed",
                             "att_ready", "attT_done", "attT_ready"))
        y_done, y_stats, y_rstd, y_read, xb_ready, y_chain, x_new, maxed, inverted = (
            sem(n) for n in ("y_done", "y_stats", "y_rstd", "y_read", "xb_ready", "y_chain", "x_new",
                             "maxed", "inverted"))

        @block.sync
        def _(sp):
            for i, w in enumerate((Ws_g, Ws_u)):
                sp.dma_start(nat[:, 2 * i:2 * i + 2, :], w.rearrange("(c p) d -> p c d", p=P)).then_inc(late_in, 16)
            sp.dma_start(nat[:, 4:6, :], Ws_d.rearrange("d (c f) -> d c f", f=P)).then_inc(late_in, 16)
            sp.dma_start(nat_g[:], gate_w).then_inc(late_in, 16)
            for i, w in enumerate((wq_w, wk_w, wv_w, wo_w)):
                sp.dma_start(nat_c[:, i, :], w).then_inc(late_in, 16)
            sp.dma_start(nat_1[:], w1.rearrange("(c p) d -> p c d", p=P)).then_inc(late_in, 16)
            sp.dma_start(nat_2[:], w2).then_inc(late_in, 16)
            for i, v in enumerate((wq_b, wk_b, wv_b)):
                sp.dma_start(cols[:, 5 + i:6 + i], v.rearrange("(d o) -> d o", o=1)).then_inc(late_in, 16)
            for i, v in enumerate((wo_b, b2, gamma, beta)):
                sp.dma_start(rows[:, 2 + i, :], v.rearrange("(o d) -> o d", o=1).to_broadcast([P, D])).then_inc(late_in, 16)
            sp.dma_start(b1row[:], b1.rearrange("(o d) -> o d", o=1).to_broadcast([P, FF])).then_inc(late_in, 16)

        FIRST, LAST = -1, NT + 1

        @block.gpsimd
        def _(pool):
            nc.gpsimd.tensor_tensor(moments[:, :, FIRST_TILES:NT, 1], moments[:, :, FIRST_TILES:NT, 1],
                                    neghalf[:, 0:2 * (NT - FIRST_TILES)].rearrange("p (a t) -> p a t", a=2),
                                    ALU.pow).then_inc(norms_ready, 1)

            def inverse_norm(t, tp, i):
                pool.wait_ge(reduced, 3 * t + i + 1)
                nc.gpsimd.tensor_tensor(rn[:, tp, i, :], ssq[:, tp, i, :], neghalf[:, 0:H0], ALU.pow)\
                    .then_inc(normed, 1)

            def out_norm(t, tp):
                nc.gpsimd.tensor_tensor(xb[:, tp, :], xs[:, t, :], rows[:, 1, :], ALU.add).then_inc(xb_ready, 1)
                pool.wait_ge(y_stats, t + 1)
                nc.gpsimd.tensor_tensor(yr[:, tp, :], ymv[:, tp, 1:2], neghalf[:, 0:1], ALU.pow).then_inc(y_rstd, 1)

            def turn(s, sp):
                if exists(s, NT):
                    inverse_norm(s, sp, 0)
                    inverse_norm(s, sp, 1)
                if exists(s - 2, NT):
                    out_norm(s - 2, sp)
                if exists(s, NT):
                    inverse_norm(s, sp, 2)
                if exists(s - 2, NT):
                    inverse_root(pool, s - 2)

            turns(pool, NT, turn, FIRST, LAST)

        @block.tensor
        def _(pe):
            pe.wait_ge(v["wa_in"], 16 * 6)

            def xT(t, tp):
                pe.wait_ge(xn_ready, t + 1)
                wait(pe, turned_out, 4 * (t - 1))
                nc.tensor.transpose(p_tr[:, 0:P], xn[:, tp, 0, :], ident[:])
                nc.tensor.transpose(p_tr[:, P:2 * P], xn[:, tp, 1, :], ident[:]).then_inc(xT_done, 1)

            def project(t, tp, i):
                if i == 0:
                    pe.wait_ge(kvT_ready, 2 * t + 2)
                wait(pe, scaled, 3 * (t - 1) + i + 1)
                cols_ = slice(S, 3 * S) if i == 0 else slice((i - 1) * 2 * S, i * 2 * S)
                nc.tensor.matmul(qk_bank[i][:], kvT[:, tp, cols_], wq_a[:] if i == 0 else wkv_a[:, 0:INNER],
                                 start=True, stop=True).then_inc(proj_done, 1)

            def project_v(t, tp, b):
                wait(pe, v_ready, 2 * t + b)
                nc.tensor.matmul(p_v[:], kvT[:, tp, b * 2 * S:(b + 1) * 2 * S], wkv_a[:, INNER:2 * INNER],
                                 start=True, stop=True).then_inc(vproj_done, 1)

            def turn_over(t, tp, i):
                pe.wait_ge(scaled, 3 * t + i + 1)
                if i == 0:
                    pe.wait_ge(kvT_ready, 2 * t + (4 if exists(t + 1, NT) else 2))
                else:
                    pe.wait_ge(turned_out, 4 * t + i + 1)
                src = qn[:, tp, :] if i == 0 else kn[:, i - 1, :]
                for h in range(HP):
                    last = nc.tensor.transpose(p_tr[:, h * P:(h + 1) * P], src[:, h * P:(h + 1) * P], ident[:])
                last.then_inc(turned, 1)

            def scores(t, tp, b):
                pe.wait_ge(turned_out, 4 * t + 3 + b)
                wait(pe, shifted, 2 * t + b)
                nc.tensor.matmul(p_s[:], ones[:],
                                 maskbias[:, t, 2 * b:2 * b + 2, :].rearrange("o c s -> o (c s)").unsqueeze(1)
                                 .to_broadcast([1, HP, P]), start=True, stop=False, skip_group_check=True)
                for h in range(HP):
                    last = nc.tensor.matmul(p_s[:, h * P:(h + 1) * P], qbd[:, tp, b, h, :, :], kT[:, tp, b, h, :],
                                            start=False, stop=True, skip_group_check=True)
                last.then_inc(scored, 1)

            def probs_T(t, tp, b):
                pe.wait_ge(exped, 2 * t + b + 1)
                wait(pe, prT_ready, 2 * t + b)
                for h in range(HP):
                    last = nc.tensor.transpose(p_pT[:, h * P:(h + 1) * P], pr[:, b, h, :], ident[:])
                last.then_inc(pT_done, 1)

            def mix(t, tp, b):
                pe.wait_ge(prT_ready, 2 * t + b + 1)
                pe.wait_ge(v_ready, 2 * t + b + 1)
                if b == 0:
                    wait(pe, y_read, t)
                else:
                    pe.wait_ge(attT_ready, 2 * t + 1)
                for h in range(HP):
                    for a in range(2):
                        last = nc.tensor.matmul(p_o[a * S:(a + 1) * S, h * (DH0 + 1):(h + 1) * (DH0 + 1)],
                                                prT[:, b, h, a * S:(a + 1) * S], vaug[:, tp, b, 2 * h + a, :],
                                                start=True, stop=True)
                last.then_inc(mixed, 1)

            def att_T(t, tp, b):
                pe.wait_ge(att_ready, 2 * t + b + 1)
                for j in range(HP // 2):
                    last = nc.tensor.transpose(p_o[:, j * P:(j + 1) * P],
                                               att[:, b, 2 * j:2 * j + 2, :], ident[:])
                last.then_inc(attT_done, 1)

            def out_proj(t, tp):
                pe.wait_ge(attT_ready, 2 * t + 2)
                for n in range(HP):
                    j, a = n // 2, n % 2
                    last = nc.tensor.matmul(p_o[:, 0:D], attT[:, tp, j, a, :, :], wo_a[:, j, a, :],
                                            start=(n == 0), stop=(n == HP - 1))
                last.then_inc(y_done, 1)

            def turn(s, sp):
                now, back, tail = exists(s, NT), exists(s - 1, NT), exists(s - 2, NT)
                if now:
                    project(s, sp, 0)
                if back:
                    turn_over(s - 1, 1 - sp, 2)
                    scores(s - 1, 1 - sp, 0)
                if tail:
                    att_T(s - 2, sp, 1)
                if now:
                    project(s, sp, 1)
                if exists(s + 1, NT):
                    xT(s + 1, 1 - sp)
                if tail:
                    out_proj(s - 2, sp)
                if back:
                    scores(s - 1, 1 - sp, 1)
                if now:
                    project(s, sp, 2)
                if back:
                    probs_T(s - 1, 1 - sp, 0)
                if now:
                    project_v(s, sp, 0)
                if back:
                    mix(s - 1, 1 - sp, 0)
                    probs_T(s - 1, 1 - sp, 1)
                if now:
                    turn_over(s, sp, 0)
                    project_v(s, sp, 1)
                if back:
                    att_T(s - 1, 1 - sp, 0)
                if now:
                    turn_over(s, sp, 1)
                if back:
                    mix(s - 1, 1 - sp, 1)

            turns(pe, NT, turn, FIRST, LAST)

        @block.scalar
        def _(act):
            def affine(t, tp):
                act.wait_ge(xT_done, t + 1)
                wait(act, vproj_done, 2 * (t - 1))
                groups = kvT[:, tp, :].rearrange("p (g s) -> p g s", g=4)
                for c, dst in ((0, groups[:, 0:4:3, :]), (1, groups[:, 1:3, :])):
                    nc.scalar.activation(dst, p_tr[:, c * P:(c + 1) * P].rearrange("p (b s) -> p b s", b=2),
                                         ACT.Identity, bias=cols[:, 2 * c + 1:2 * c + 2],
                                         scale=cols[:, 2 * c:2 * c + 1]).then_inc(kvT_ready, 1)

            def square(t, tp, i):
                act.wait_ge(proj_done, 3 * t + i + 1)
                wait(act, reduced, 3 * t + i - 1)
                nc.scalar.activation(sq[:, (3 * tp + i) % 2, :], qk_bank[i][:], ACT.Square).then_inc(squared, 1)

            def values(t, tp, b):
                if isinstance(t, int) and t == 0:
                    act.wait_ge(zeroed, 1)
                act.wait_ge(vproj_done, 2 * t + b + 1)
                wait(act, mixed, 2 * (t - 2) + b + 1)
                nc.scalar.copy(vaug[:, tp, b, :, 0:DH0],
                               p_v[:].rearrange("p (h d) -> p h d", h=H0)).then_inc(v_ready, 1)

            def queries_out(t, tp):
                if isinstance(t, int) and t == 0:
                    act.wait_ge(zeroed, 2)
                act.wait_ge(turned, 3 * t + 1)
                wait(act, scored, 2 * (t - 1))
                for a in range(2):
                    nc.scalar.activation(qbd[a * S:(a + 1) * S, tp, :, :, a, :],
                                         p_tr[a * S:(a + 1) * S, :].rearrange("p (h b s) -> p b h s", h=HP, b=2),
                                         ACT.Copy).then_inc(turned_out, 1)

            def keys_out(t, tp, b):
                act.wait_ge(turned, 3 * t + 2 + b)
                wait(act, scored, 2 * (t - 2) + b + 1)
                nc.scalar.activation(kT[:, tp, b, :, :], p_tr[:].rearrange("p (h k) -> p h k", h=HP), ACT.Copy,
                                     scale=cols[:, 4:5]).then_inc(turned_out, 1)

            def exp(t, b):
                act.wait_ge(shifted, 2 * t + b + 1)
                nc.scalar.activation(pr[:, b], pr[:, b], ACT.Exp).then_inc(exped, 1)

            def probs_out(t, b):
                act.wait_ge(pT_done, 2 * t + b + 1)
                wait(act, mixed, 2 * (t - 1) + b + 1)
                nc.scalar.copy(prT[:, b].rearrange("p h k -> p (h k)"), p_pT[:]).then_inc(prT_ready, 1)

            def att_out(t, tp, b):
                act.wait_ge(attT_done, 2 * t + b + 1)
                wait(act, y_done, t)
                nc.scalar.copy(attT[:, tp, :, :, b, :],
                               p_o[:, 0:HP // 2 * P].rearrange("p (j a s) -> p j a s", j=HP // 2, a=2)).then_inc(attT_ready, 1)

            def turn(s, sp):
                now, back = exists(s, NT), exists(s - 1, NT)
                if now:
                    square(s, sp, 0)
                if back:
                    keys_out(s - 1, 1 - sp, 1)
                if exists(s - 2, NT):
                    att_out(s - 2, sp, 1)
                if now:
                    square(s, sp, 1)
                if exists(s + 1, NT):
                    affine(s + 1, 1 - sp)
                if back:
                    exp(s - 1, 0)
                if now:
                    square(s, sp, 2)
                if back:
                    probs_out(s - 1, 0)
                    exp(s - 1, 1)
                if now:
                    values(s, sp, 0)
                if back:
                    probs_out(s - 1, 1)
                if now:
                    queries_out(s, sp)
                if back:
                    att_out(s - 1, 1 - sp, 0)
                if now:
                    keys_out(s, sp, 0)
                    values(s, sp, 1)

            turns(act, NT, turn, FIRST, LAST)

        @block.vector
        def _(dve):
            def normalise(t, tp):
                wait(dve, xT_done, t - 1)
                nc.vector.tensor_scalar(xn[:, tp, 0, :], cs[:, t, :], moments[:, 0, t, 0:1], moments[:, 0, t, 1:2],
                                        ALU.subtract, ALU.mult)
                nc.vector.tensor_scalar(xn[:, tp, 1, :], xs[:, t, :], moments[:, 1, t, 0:1], moments[:, 1, t, 1:2],
                                        ALU.subtract, ALU.mult).then_inc(xn_ready, 1)

            def reduce(t, tp, i):
                dve.wait_ge(squared, 3 * t + i + 1)
                wait(dve, normed, 3 * (t - 2) + i + 1)
                nc.vector.tensor_reduce(ssq[:, tp, i, :], sq[:, (3 * tp + i) % 2, :].rearrange("p (h d) -> p h d", h=H0),
                                        AX.X, ALU.add).then_inc(reduced, 1)

            def scale(t, tp, i):
                dve.wait_ge(normed, 3 * t + i + 1)
                if i == 0:
                    wait(dve, turned, 3 * (t - 2) + 1)
                    dst = qn[:, tp, :]
                else:
                    wait(dve, turned, 3 * (t - 1) + i + 1)
                    dst = kn[:, i - 1, :]
                nc.vector.scalar_tensor_tensor(dst.rearrange("p (h d) -> p h d", h=H0),
                                               rn[:, tp, i, :].unsqueeze(2).to_broadcast([P, H0, DH0]), 1e12,
                                               qk_bank[i][:].rearrange("p (h d) -> p h d", h=H0),
                                               ALU.min, ALU.mult).then_inc(scaled, 1)

            s3 = p_s[:].rearrange("p (h k) -> p h k", h=HP)

            def shift(t, b):
                dve.wait_ge(scored, 2 * t + b + 1)
                nc.vector.tensor_reduce(mx[:, b, :], s3, AX.X, ALU.max).then_inc(maxed, 1)
                dve.wait_ge(maxed, 2 * t + b + 1)
                wait(dve, pT_done, 2 * (t - 1) + b + 1)
                nc.vector.tensor_tensor(pr[:, b], s3, mx[:, b, :].unsqueeze(2).to_broadcast([P, HP, P]),
                                        ALU.subtract).then_inc(shifted, 1)

            def attend(t, b):
                dve.wait_ge(mixed, 2 * t + b + 1)
                o3 = p_o[:, 0:HP * (DH0 + 1)].rearrange("p (h d) -> p h d", h=HP)
                nc.vector.reciprocal(rsum[:, b, :], o3[:, :, DH0]).then_inc(inverted, 1)
                dve.wait_ge(inverted, 2 * t + b + 1)
                wait(dve, attT_done, 2 * (t - 1) + b + 1)
                nc.vector.tensor_tensor(att[:, b], o3[:, :, 0:DH0],
                                        rsum[:, b, :].unsqueeze(2).to_broadcast([P, HP, DH0]),
                                        ALU.mult).then_inc(att_ready, 1)

            def read_output(t, tp):
                dve.wait_ge(y_done, t + 1)
                y = Steps(dve, y_chain, 2 * t)
                y(nc.vector.bn_stats(yst[:, tp, :], p_o[:, 0:D]))
                nc.vector.memset(spare[:], 0.0)
                y(nc.vector.bn_aggr(ymv[:, tp, :], yst[:, tp, :]))
                nc.vector.tensor_scalar(ymv[:, tp, 1:2], ymv[:, tp, 1:2], EPS, None, ALU.add).then_inc(y_stats, 1)
                nc.vector.scalar_tensor_tensor(yw[:, tp, :], p_o[:, 0:D], ymv[:, tp, 0:1], rows[:, 0, :],
                                               ALU.subtract, ALU.mult).then_inc(y_read, 1)

            def write_output(t, tp):
                dve.wait_ge(y_read, t + 1)
                dve.wait_ge(y_rstd, t + 1)
                dve.wait_ge(xb_ready, t + 1)
                nc.vector.scalar_tensor_tensor(xs[:, t, :], yw[:, tp, :], yr[:, tp, :], xb[:, tp, :],
                                               ALU.mult, ALU.add).then_inc(x_new, 1)

            def turn(s, sp):
                now, back, tail = exists(s, NT), exists(s - 1, NT), exists(s - 2, NT)
                if tail:
                    attend(s - 2, 1)
                if exists(s + 1, NT):
                    if isinstance(s, int) and s + 1 == FIRST_TILES:
                        dve.wait_ge(norms_ready, 1)
                    normalise(s + 1, 1 - sp)
                if isinstance(s, int) and s == 0:
                    nc.vector.memset(vaug[:], 1.0).then_inc(zeroed, 1)
                    nc.vector.memset(qbd[:], 0.0).then_inc(zeroed, 1)
                if now:
                    reduce(s, sp, 0)
                if back:
                    shift(s - 1, 0)
                if now:
                    reduce(s, sp, 1)
                if tail:
                    read_output(s - 2, sp)
                if back:
                    shift(s - 1, 1)
                if now:
                    scale(s, sp, 0)
                if tail:
                    write_output(s - 2, sp)
                if now:
                    scale(s, sp, 1)
                if tail:
                    row_stats(dve, s - 2, sp, x_new)
                if now:
                    reduce(s, sp, 2)
                if back:
                    attend(s - 1, 0)
                if tail:
                    row_moments(dve, s - 2, sp)
                    keep_moments(dve, s - 2, sp)
                if now:
                    scale(s, sp, 2)

            turns(dve, NT, turn, FIRST, LAST)


def routing(nc, v):
    xs, moments, neghalf, ident, tokid, gw_t = (
        v[n] for n in "xs moments neghalf ident tokid gw_t".split())
    x_tok, sel_w, xnT_all = (v[n] for n in "x_tok sel_w xnT_all".split())
    NT, D, S, E, CAP, EPS = (v[n] for n in "NT D S E CAP EPS".split())
    nat, nat_c, nat_g, nat_1, nat_2, ws_t, w_c, w1_t, w2_t = (
        v[n] for n in "nat nat_c nat_g nat_1 nat_2 ws_t w_c w1_t w2_t".split())
    wmean, gates, rows, late_in, LATE, FF, MAGIC = (v[n] for n in "wmean gates rows late_in LATE FF MAGIC".split())
    QT = 4
    HT = P // E
    with ExitStack() as ph, nc.Block() as block:
        def sb(name, shape, dt=F32):
            return ph.enter_context(nc.sbuf_tensor("r_" + name, shape, dt))

        def pb(name):
            return ph.enter_context(nc.psum_tensor("r_" + name, [P, 512], F32))

        def sem(name):
            return ph.enter_context(nc.semaphore("r_" + name))

        xn = sb("xn", [P, NT, D])
        ex = sb("ex", [P, NT, E])
        mx = sb("mx", [P, NT])
        esum = sb("esum", [P, NT])
        sc = sb("sc", [P, NT, E])
        scT = sb("scT", [P, 2, P])
        top = sb("top", [P, 2, 2, CAP])
        idx = sb("idx", [P, 2, 2, CAP], U32)
        idxf = sb("idxf", [P, 2, 2, CAP])
        own_e = sb("own_e", [P, E])
        own_t = sb("own_t", [P, HT])
        tile_ones = sb("tile_ones", [P, HT, S], BF16)
        spread = sb("spread", [P, 2, 2, E * CAP], BF16)
        sel = sb("sel", [P, 2, QT, E * CAP])
        onesf = sb("onesf", [P, P])
        wsum = sb("wsum", [P, 2])
        wscale = sb("wscale", [P, 2])
        tern = sb("tern", [P, 2, FF])
        p_T = (pb("T0"), pb("T1"))
        p_L, p_sT = pb("L"), pb("sT")
        p_I = (pb("I0"), pb("I1"))
        p_g = ((pb("g0"), pb("g1")), p_T)
        (xn_ready, xT_done, xT_ready, logits_done, shifted, exp_done, soft, sc_ready,
         scT_done, scT_ready, choice, spread_ready, index_done, sel_ready, sel_w_ready, gathered, taken, w_turned,
         w_out, wsum_ready, wmean_done, tern_ready, tern_turned, tern_out, tern_chain) = (
            sem(n) for n in ("xn_ready", "xT_done", "xT_ready", "logits_done",
                             "shifted", "exp_done", "soft", "sc_ready", "scT_done", "scT_ready", "choice",
                             "spread_ready", "index_done", "sel_ready", "sel_w_ready", "gathered", "taken", "w_turned",
                             "w_out", "wsum_ready", "wmean_done", "tern_ready", "tern_turned", "tern_out", "tern_chain"))

        @block.sync
        def _(sp):
            load_expert(sp, v, 0, 0)
            load_expert(sp, v, 1, 1)

        @block.gpsimd
        def _(pool):
            pool.wait_ge(late_in, LATE)
            for i, gate in ((2, 1), (3, 3)):
                nc.gpsimd.tensor_scalar(rows[:, i, :], rows[:, i, :], gates[:, gate:gate + 1], None, ALU.mult)
            for c in range(NT // QT):
                pool.wait_ge(sel_ready, c + 1)
                pool.wait_ge(sc_ready, 2)
                nc.gpsimd.tensor_tensor(sel_w[:, c * QT:(c + 1) * QT, :].rearrange("p t (e c) -> p (t e) c", c=CAP),
                                        sel[:, c % 2].rearrange("p t (e c) -> p (t e) c", c=CAP),
                                        sc[:, c * QT:(c + 1) * QT, :].rearrange("p t e -> p (t e)").unsqueeze(2)
                                        .to_broadcast([P, QT * E, CAP]), ALU.mult).then_inc(sel_w_ready, 1)

        @block.tensor
        def _(pe):
            def logits(c):
                pe.wait_ge(xT_ready, c + 1)
                for t in range(c * QT, (c + 1) * QT):
                    last = nc.tensor.matmul(p_L[:, t * E:(t + 1) * E], xnT_all[:, t, :], gw_t[:], start=True, stop=True)
                last.then_inc(logits_done, 1)

            def indices(c):
                pe.wait_ge(spread_ready, c * QT // HT + 1)
                wait(pe, sel_ready, c - 1)
                for i in range(QT):
                    t = c * QT + i
                    for b in range(2):
                        last = nc.tensor.matmul(p_I[c % 2][b * S:(b + 1) * S, i * P:(i + 1) * P], tile_ones[:, t % HT, :],
                                                spread[:, t // HT, b, :], start=True, stop=True)
                last.then_inc(index_done, 1)

            pe.wait_ge(late_in, LATE)
            for i in range(2):
                nc.tensor.transpose(p_I[1][:, i * P:(i + 1) * P], nat[:, 4 + i, :], ident[:])
            nc.tensor.transpose(p_I[1][:, 2 * P:2 * P + E], nat_g[:], ident[0:E, 0:E]).then_inc(w_turned, 1)
            for i in range(4):
                last = nc.tensor.transpose(p_g[0][0][:, i * P:(i + 1) * P], nat_c[:, i, :], ident[:])
            last.then_inc(w_turned, 1)
            for i in range(4):
                last = nc.tensor.transpose(p_I[0][:, i * P:(i + 1) * P], nat[:, i, :], ident[:])
            last.then_inc(w_turned, 1)
            for c in range(NT // QT):
                pe.wait_ge(xn_ready, c + 1)
                wait(pe, xT_ready, c - 1)
                for i in range(QT):
                    last = nc.tensor.transpose(p_T[c % 2][:, i * P:(i + 1) * P], xn[:, c * QT + i, :], ident[:])
                last.then_inc(xT_done, 1)
                if c > 0:
                    logits(c - 1)
            logits(NT // QT - 1)
            pe.wait_ge(wsum_ready, 1)
            nc.tensor.matmul(p_sT[:, 0:2], onesf[:], wsum[:], start=True, stop=True).then_inc(wmean_done, 1)
            for h in range(2):
                pe.wait_ge(sc_ready, h + 1)
                nc.tensor.transpose(p_sT[:, h * P:(h + 1) * P],
                                    sc[:, h * HT:(h + 1) * HT, :].rearrange("p t e -> p (t e)"), ident[:]).then_inc(scT_done, 1)
                wait(pe, scT_ready, h + 1)
            pe.wait_ge(tern_ready, 1)
            for i in range(FF // P):
                last = nc.tensor.transpose(p_L[:, i * P:(i + 1) * P], tern[:, 0, i * P:(i + 1) * P], ident[:])
            last.then_inc(tern_turned, 1)
            for i in range(FF // P):
                last = nc.tensor.transpose(p_sT[:, i * P:(i + 1) * P], tern[:, 1, i * P:(i + 1) * P], ident[:])
            last.then_inc(tern_turned, 1)
            pe.wait_ge(w_out, 5)
            indices(0)
            for c in range(NT // QT):
                if c + 1 < NT // QT:
                    indices(c + 1)
                pe.wait_ge(sel_ready, c + 1)
                wait(pe, taken, 2 * (c - 1))
                for i in range(QT):
                    for b in range(2):
                        last = nc.tensor.matmul(p_g[c % 2][b][:, i * P:(i + 1) * P], xn[b * S:(b + 1) * S, c * QT + i, :],
                                                sel[b * S:(b + 1) * S, c % 2, i, :], start=True, stop=True)
                        if i == QT - 1:
                            last.then_inc(gathered, 1)

        @block.scalar
        def _(act):
            act.wait_ge(w_turned, 1)
            nc.scalar.copy(gw_t[:], p_I[1][:, 2 * P:2 * P + E]).then_inc(w_out, 1)
            nc.scalar.copy(ws_t[:, 4:6, :].rearrange("p i k -> p (i k)"), p_I[1][:, 0:2 * P]).then_inc(w_out, 1)
            act.wait_ge(w_turned, 2)
            nc.scalar.copy(w_c[:, 0:3, :].rearrange("p i k -> p (i k)"), p_g[0][0][:, 0:3 * P]).then_inc(w_out, 1)
            nc.scalar.activation(w_c[:, 3, :], p_g[0][0][:, 3 * P:4 * P], ACT.Copy, scale=gates[:, 1:2]).then_inc(w_out, 1)
            act.wait_ge(w_turned, 3)
            nc.scalar.copy(ws_t[:, 0:4, :].rearrange("p i k -> p (i k)"), p_I[0][:]).then_inc(w_out, 1)
            for c in range(NT // QT):
                act.wait_ge(xT_done, c + 1)
                nc.scalar.copy(xnT_all[:, c * QT:(c + 1) * QT, :].rearrange("p t k -> p (t k)"), p_T[c % 2][:]).then_inc(xT_ready, 1)
            act.wait_ge(shifted, 1)
            nc.scalar.activation(ex[:], ex[:], ACT.Exp).then_inc(exp_done, 1)
            for h in range(2):
                act.wait_ge(scT_done, h + 1)
                nc.scalar.copy(scT[:, h, :], p_sT[:, h * P:(h + 1) * P]).then_inc(scT_ready, 1)
            for i, w in enumerate((w1_t[:], w2_t[:].rearrange("p c k -> p (c k)"))):
                act.wait_ge(tern_turned, i + 1)
                nc.scalar.copy(w, (p_L, p_sT)[i][:]).then_inc(tern_out, 1)
            for c in range(NT // QT):
                for b in range(2):
                    act.wait_ge(gathered, 2 * c + b + 1)
                    nc.scalar.copy(x_tok[:, :, c * QT:(c + 1) * QT, b, :],
                                   p_g[c % 2][b][:].rearrange("p (t e c) -> p e t c", t=QT, e=E)).then_inc(taken, 1)

        @block.vector
        def _(dve):
            def choose(h):
                dve.wait_ge(scT_ready, h + 1)
                step = Steps(dve, choice, 3 * h)
                for b in range(2):
                    last = nc.vector.max(top[:, h, b, :], scT[:, h, b * S:(b + 1) * S])
                step(last)
                for b in range(2):
                    last = nc.vector.max_index(idx[:, h, b, :], top[:, h, b, :], scT[:, h, b * S:(b + 1) * S])
                step(last)
                step(nc.vector.tensor_copy(idxf[:, h], idx[:, h]))
                for b in range(2):
                    last = nc.vector.tensor_tensor(spread[:, h, b, :].rearrange("p (e c) -> p e c", c=CAP),
                                                   own_e[:].unsqueeze(2).to_broadcast([P, E, CAP]),
                                                   idxf[:, h, b, :].unsqueeze(1).to_broadcast([P, E, CAP]), ALU.mult)
                last.then_inc(spread_ready, 1)

            nc.vector.memset(onesf[:], 1.0)
            ident_te = ident[:].rearrange("p (t e) -> p t e", e=E)
            nc.vector.tensor_reduce(own_e[:], ident[:].rearrange("p (t e) -> p e t", e=E), AX.X, ALU.add)
            nc.vector.tensor_reduce(own_t[:], ident_te, AX.X, ALU.add).then_inc(soft, 1)
            dve.wait_ge(soft, 1)
            nc.vector.tensor_copy(tile_ones[:], own_t[:].unsqueeze(2).to_broadcast([P, HT, S]))
            for c in range(NT // QT):
                for t in range(c * QT, (c + 1) * QT):
                    last = nc.vector.tensor_scalar(xn[:, t, :], xs[:, t, :], moments[:, 1, t, 0:1], moments[:, 1, t, 1:2],
                                                   ALU.subtract, ALU.mult)
                last.then_inc(xn_ready, 1)
            wst = Steps(dve, tern_chain)
            dve.wait_ge(late_in, LATE)
            w_nats = (nat_1[:].rearrange("p c d -> p (c d)"), nat_2[:])
            for i in range(2):
                last = nc.vector.tensor_reduce(wsum[:, i:i + 1], w_nats[i], AX.X, ALU.add, apply_absolute_value=True)
            last.then_inc(wsum_ready, 1)
            step = Steps(dve, soft, 1)
            dve.wait_ge(logits_done, NT // QT)
            lg = p_L[:, 0:NT * E].rearrange("p (t e) -> p t e", e=E)
            step(nc.vector.tensor_reduce(mx[:], lg, AX.X, ALU.max))
            nc.vector.tensor_tensor(ex[:], lg, mx[:].unsqueeze(2).to_broadcast([P, NT, E]), ALU.subtract).then_inc(shifted, 1)
            dve.wait_ge(exp_done, 1)
            step(nc.vector.tensor_reduce(esum[:], ex[:], AX.X, ALU.add))
            step(nc.vector.reciprocal(esum[:], esum[:]))
            dve.wait_ge(wmean_done, 1)
            wst(nc.vector.tensor_scalar(wmean[:], p_sT[:, 0:2], 1.0 / (FF * D), EPS, ALU.mult, ALU.max))
            wst(nc.vector.reciprocal(wscale[:], wmean[:]))
            for h in range(2):
                r = slice(h * HT, (h + 1) * HT)
                nc.vector.tensor_tensor(sc[:, r, :], ex[:, r, :], esum[:, r].unsqueeze(2).to_broadcast([P, HT, E]),
                                        ALU.mult).then_inc(sc_ready, 1)
            for i in range(2):
                last = nc.vector.tensor_scalar(tern[:, i, :], w_nats[i], wscale[:, i:i + 1], MAGIC, ALU.mult, ALU.add)
            wst(last)
            wst(nc.vector.tensor_scalar(tern[:], tern[:], MAGIC, 1.0, ALU.subtract, ALU.min))
            nc.vector.tensor_scalar(tern[:], tern[:], -1.0, None, ALU.max).then_inc(tern_ready, 1)
            for h in range(2):
                choose(h)
            for c in range(NT // QT):
                dve.wait_ge(index_done, c + 1)
                wait(dve, gathered, 2 * (c - 1))
                wait(dve, sel_w_ready, c - 1)
                nc.vector.tensor_scalar(sel[:, c % 2].rearrange("p t k -> p (t k)"), p_I[c % 2][:], tokid[:], None,
                                        ALU.is_equal).then_inc(sel_ready, 1)


def load_expert(sp, v, e, ep):
    w_nat, w_in, Wg, Wu, Wd = (v[n] for n in "w_nat w_in Wg Wu Wd".split())
    sp.dma_start(w_nat[:, ep, 0:2, :], Wg[e].rearrange("(c p) d -> p c d", p=P)).then_inc(w_in[ep], 16)
    sp.dma_start(w_nat[:, ep, 2:4, :], Wu[e].rearrange("(c p) d -> p c d", p=P)).then_inc(w_in[ep], 16)
    sp.dma_start(w_nat[:, ep, 4:6, :], Wd[e].rearrange("d (c f) -> d c f", f=P)).then_inc(w_in[ep], 16)


def experts(nc, v):
    ident, x_tok, eo_T, w_nat, w_in = (v[n] for n in "ident x_tok eo_T w_nat w_in".split())
    NT, E, CAP, B = (v[n] for n in "NT E CAP B".split())
    N = B * CAP
    with ExitStack() as ph, nc.Block() as block:
        def sb(name, shape, dt=F32):
            return ph.enter_context(nc.sbuf_tensor("e_" + name, shape, dt))

        def pb(name):
            return ph.enter_context(nc.psum_tensor("e_" + name, [P, 512], F32))

        def sem(name):
            return ph.enter_context(nc.semaphore("e_" + name))

        w_T = sb("w_T", [P, 2, 6, P])
        hg = sb("hg", [P, 2, 2 * N])
        h = sb("h", [P, 2, 2 * N])
        p_w0, p_w1, p_g0, p_g1, p_u0, p_u1, p_e0, p_e1 = (pb(n) for n in "w0 w1 g0 g1 u0 u1 e0 e1".split())
        p_g, p_u, p_e = (p_g0, p_g1), (p_u0, p_u1), (p_e0, p_e1)
        turned, wT_gu, wT_d, gate_done, up_done, act_done, h_ready, down_done, out_ready = (
            sem(n) for n in ("turned", "wT_gu", "wT_d", "gate_done", "up_done", "act_done", "h_ready", "down_done",
                             "out_ready"))

        FIRST, LAST = -1, E

        @block.sync
        def _(sp):
            def load(e, ep):
                sp.wait_ge(turned, 2 * (e - 1))
                load_expert(sp, v, e, ep)

            with sp.Fori(1, E // 2) as j:
                load(2 * j, 0)
                load(2 * j + 1, 1)

        @block.tensor
        def _(pe):
            def turn_over(e, ep):
                pe.wait_ge(w_in[ep], 24 * e + 24 * (2 - ep))
                wait(pe, wT_gu, e)
                for i in range(4):
                    last = nc.tensor.transpose(p_w0[:, i * P:(i + 1) * P], w_nat[:, ep, i, :], ident[:])
                last.then_inc(turned, 1)
                wait(pe, wT_d, e)
                for i in range(2):
                    last = nc.tensor.transpose(p_w1[:, i * P:(i + 1) * P], w_nat[:, ep, 4 + i, :], ident[:])
                last.then_inc(turned, 1)

            def up(e, ep):
                pe.wait_ge(wT_gu, e + 1)
                tokens = x_tok[:, e].rearrange("p t b c -> p (t b c)")
                wait(pe, act_done, e - 1)
                for i in range(2):
                    last = nc.tensor.matmul(p_g[ep][:, i * N:(i + 1) * N], w_T[:, ep, i, :], tokens,
                                            start=True, stop=True)
                last.then_inc(gate_done, 1)
                wait(pe, h_ready, e - 1)
                for i in range(2):
                    last = nc.tensor.matmul(p_u[ep][:, i * N:(i + 1) * N], w_T[:, ep, 2 + i, :], tokens,
                                            start=True, stop=True)
                last.then_inc(up_done, 1)

            def down(e, ep):
                pe.wait_ge(h_ready, e + 1)
                pe.wait_ge(wT_d, e + 1)
                wait(pe, out_ready, e - 1)
                for i in range(2):
                    last = nc.tensor.matmul(p_e[ep][:, 0:N], w_T[:, ep, 4 + i, :], h[:, ep, i * N:(i + 1) * N],
                                            start=(i == 0), stop=(i == 1))
                last.then_inc(down_done, 1)

            def turn(s, sp):
                if exists(s, E):
                    up(s, sp)
                if exists(s + 1, E):
                    turn_over(s + 1, 1 - sp)
                if exists(s - 1, E):
                    down(s - 1, 1 - sp)

            turns(pe, E, turn, FIRST, LAST)

        @block.scalar
        def _(act):
            def front(e, ep):
                act.wait_ge(turned, 2 * e + 1)
                wait(act, up_done, e - 1)
                nc.scalar.copy(w_T[:, ep, 0:4, :].rearrange("p i k -> p (i k)"), p_w0[:]).then_inc(wT_gu, 1)

            def gelu(e, ep):
                act.wait_ge(gate_done, e + 1)
                wait(act, h_ready, e - 1)
                nc.scalar.activation(hg[:, ep, :], p_g[ep][:], ACT.Gelu).then_inc(act_done, 1)

            def turn(s, sp):
                if exists(s, E):
                    gelu(s, sp)
                if exists(s + 1, E):
                    front(s + 1, 1 - sp)

            turns(act, E, turn, FIRST, LAST)

        @block.vector
        def _(dve):
            def front(e, ep):
                dve.wait_ge(turned, 2 * e + 2)
                wait(dve, down_done, e - 1)
                nc.vector.tensor_copy(w_T[:, ep, 4:6, :].rearrange("p i k -> p (i k)"), p_w1[:, 0:2 * P]).then_inc(wT_d, 1)

            def product(e, ep):
                dve.wait_ge(act_done, e + 1)
                dve.wait_ge(up_done, e + 1)
                wait(dve, down_done, e - 1)
                nc.vector.tensor_tensor(h[:, ep, :], hg[:, ep, :], p_u[ep][:], ALU.mult).then_inc(h_ready, 1)

            def back(e, ep):
                dve.wait_ge(down_done, e + 1)
                nc.vector.tensor_copy(eo_T[:, :, e, :], p_e[ep][:, 0:N].rearrange("p (b c) -> p b c", c=CAP))\
                    .then_inc(out_ready, 1)

            def turn(s, sp):
                if exists(s, E):
                    product(s, sp)
                if exists(s - 1, E):
                    back(s - 1, 1 - sp)
                if exists(s + 1, E):
                    front(s + 1, 1 - sp)

            turns(dve, E, turn, FIRST, LAST)


def combine(nc, v):
    xs, ident, gates, ws_t = (v[n] for n in "xs ident gates ws_t".split())
    eo_T, sel_w, xnT_all = (v[n] for n in "eo_T sel_w xnT_all".split())
    NT, D, S, E, CAP = (v[n] for n in "NT D S E CAP".split())
    with ExitStack() as ph, nc.Block() as block:
        def sb(name, shape, dt=F32):
            return ph.enter_context(nc.sbuf_tensor("c_" + name, shape, dt))

        def pb(name):
            return ph.enter_context(nc.psum_tensor("c_" + name, [P, 512], F32))

        def sem(name):
            return ph.enter_context(nc.semaphore("c_" + name))

        staged = sb("staged", [P, 2, 3, P])
        turned = sb("turned", [P, 2, 3, P])
        hg = sb("hg", [P, 2, 2 * P])
        h = sb("h", [P, 2, 2, P])
        p_t0, p_t1, p_h0, p_h1, p_y0, p_y1 = (pb(n) for n in "t0 t1 h0 h1 y0 y1".split())
        row_stats, row_moments, keep_moments, inverse_root = next_norm(nc, v, ph, "c")
        p_t, p_h, p_y = (p_t0, p_t1), (p_h0, p_h1), (p_y0, p_y1)
        stage_ready, weights_ready, turn_done, turn_ready, up_done, act_done, h_ready, y_done, x_new = (
            sem(n) for n in ("stage_ready", "weights_ready", "turn_done", "turn_ready", "up_done", "act_done", "h_ready", "y_done", "x_new"))

        @block.gpsimd
        def _(pool):
            def stage(t, tp):
                wait(pool, turn_done, t - 1)
                nc.gpsimd.tensor_copy(staged[:, tp, 0:2, :],
                                      eo_T[:, bass.ds(2 * t, 2), :, :].rearrange("p b e c -> p b (e c)")).then_inc(stage_ready, 1)

            def turn(s, sp):
                if exists(s + 1, NT):
                    stage(s + 1, 1 - sp)
                if exists(s - 2, NT):
                    inverse_root(pool, s - 2)

            turns(pool, NT, turn, -1, NT + 1)

        @block.tensor
        def _(pe):
            def front(t, tp):
                pe.wait_ge(stage_ready, t + 1)
                pe.wait_ge(weights_ready, t + 1)
                wait(pe, turn_ready, t - 1)
                for i in range(3):
                    last = nc.tensor.transpose(p_t[tp][:, i * P:(i + 1) * P], staged[:, tp, i, :], ident[:])
                last.then_inc(turn_done, 1)
                wait(pe, h_ready, t - 1)
                for i in range(4):
                    last = nc.tensor.matmul(p_h[tp][:, i * P:(i + 1) * P], ws_t[:, i, :], xnT_all[:, t, :],
                                            start=True, stop=True)
                last.then_inc(up_done, 1)

            def back(t, tp):
                pe.wait_ge(h_ready, t + 1)
                pe.wait_ge(turn_ready, t + 1)
                wait(pe, x_new, t - 1)
                for i in range(2):
                    nc.tensor.matmul(p_y[tp][:, 0:D], h[:, tp, i, :], ws_t[:, 4 + i, :], start=(i == 0), stop=False,
                                     skip_group_check=True)
                for b in range(2):
                    last = nc.tensor.matmul(p_y[tp][b * S:(b + 1) * S, 0:D], turned[:, tp, 2, b * S:(b + 1) * S],
                                            turned[:, tp, b, :], start=False, stop=True, skip_group_check=True)
                last.then_inc(y_done, 1)

            def turn(s, sp):
                if exists(s, NT):
                    front(s, sp)
                if exists(s - 1, NT):
                    back(s - 1, 1 - sp)

            turns(pe, NT, turn, 0, NT)

        @block.scalar
        def _(act):
            def front(t, tp):
                act.wait_ge(turn_done, t + 1)
                wait(act, y_done, t - 1)
                nc.scalar.copy(turned[:, tp].rearrange("p i k -> p (i k)"), p_t[tp][:, 0:3 * P]).then_inc(turn_ready, 1)
                act.wait_ge(up_done, t + 1)
                wait(act, h_ready, t - 1)
                nc.scalar.activation(hg[:, tp, :], p_h[tp][:, 0:2 * P], ACT.Gelu).then_inc(act_done, 1)

            def stage_weights(t, tp):
                wait(act, turn_done, t - 1)
                nc.scalar.copy(staged[:, tp, 2, :], sel_w[:, t, :]).then_inc(weights_ready, 1)

            def turn(s, sp):
                if exists(s + 1, NT):
                    stage_weights(s + 1, 1 - sp)
                if exists(s, NT):
                    front(s, sp)

            turns(act, NT, turn, -1, NT - 1)

        @block.vector
        def _(dve):
            def front(t, tp):
                dve.wait_ge(act_done, t + 1)
                wait(dve, y_done, t - 1)
                nc.vector.tensor_tensor(h[:, tp].rearrange("p i k -> p (i k)"), hg[:, tp, :], p_h[tp][:, 2 * P:4 * P],
                                        ALU.mult).then_inc(h_ready, 1)

            def back(t, tp):
                dve.wait_ge(y_done, t + 1)
                nc.vector.scalar_tensor_tensor(xs[:, t, :], p_y[tp][:, 0:D], gates[:, 2:3], xs[:, t, :],
                                               ALU.mult, ALU.add).then_inc(x_new, 1)
                row_stats(dve, t, tp, x_new)

            def norm(t, tp):
                row_moments(dve, t, tp)
                keep_moments(dve, t, tp)

            def turn(s, sp):
                if exists(s - 2, NT):
                    norm(s - 2, sp)
                if exists(s, NT):
                    front(s, sp)
                if exists(s - 1, NT):
                    back(s - 1, 1 - sp)

            turns(dve, NT, turn, 0, NT + 1)


def attention_1(nc, v):
    xs, cs, moments, neghalf, ident, quad = (
        v[n] for n in "xs cs moments neghalf ident quad".split())
    cols, rows, w_c = (v[n] for n in "cols rows w_c".split())
    NT, D, S, EPS = (v[n] for n in "NT D S EPS".split())
    G, DH = 4, 8
    HP = 2 * G
    with ExitStack() as ph, nc.Block() as block:
        def sb(name, shape, dt=F32):
            return ph.enter_context(nc.sbuf_tensor("a1_" + name, shape, dt))

        def pb(name, shape=(P, 512)):
            return ph.enter_context(nc.psum_tensor("a1_" + name, list(shape), F32))

        def sem(name):
            return ph.enter_context(nc.semaphore("a1_" + name))

        xn = sb("xn", [P, 2, 2, D])
        cT = sb("cT", [P, 2, 2, 2, S])
        xT = sb("xT", [P, 2, P])
        q = sb("q", [P, 2, 2, S])
        k4 = sb("k4", [P, 2, 2, 4, S])
        vals = sb("vals", [P, 2, HP, 2, 2, DH + 1])
        mx = sb("mx", [P, 2, G, 4])
        pr = sb("pr", [P, 2, 4 * G, S])
        prT = sb("prT", [P, 2, HP // 2, P])
        rs = sb("rs", [P, 2, 4 * G])
        att = sb("att", [P, 2, D])
        oT = sb("oT", [P, 2, 2 * S])
        xb = sb("xb", [P, 2, D])
        p_s = pb("s", (P, G, 512))
        p_T, p_qv, p_pT, p_o = (pb(n) for n in "T qv pT o".split())
        WIDE = 4 * (DH + 1)
        (zeroed, c_ready, xn_ready, turned, turned_out, qkv_done, q_ready,
         k4_ready, v_ready, scored, maxed, shifted, exped, pT_done, prT_ready, mixed, inverse, att_ready, aT_done,
         oT_ready, y_done, xb_ready, x_new) = (
            sem(n) for n in ("zeroed", "c_ready", "xn_ready", "turned",
                             "turned_out", "qkv_done", "q_ready", "k4_ready", "v_ready", "scored", "maxed",
                             "shifted", "exped", "pT_done", "prT_ready", "mixed", "inverse", "att_ready", "aT_done",
                             "oT_ready", "y_done", "xb_ready", "x_new"))

        row_stats, row_moments, keep_moments, inverse_root = next_norm(nc, v, ph, "a1")
        FIRST, LAST = -2, NT + 1

        @block.gpsimd
        def _(pool):

            def stage(t, tp):
                wait(pool, turned, t - 1)
                nc.gpsimd.tensor_copy(xn[:, tp, 0, :], cs[:, t, :]).then_inc(c_ready, 1)

            def biased(t, tp):
                wait(pool, x_new, t - 1)
                nc.gpsimd.tensor_tensor(xb[:, tp, :], xs[:, t, :], rows[:, 2, :], ALU.add).then_inc(xb_ready, 1)

            def turn(s, sp):
                if exists(s + 2, NT):
                    stage(s + 2, sp)
                if exists(s - 1, NT):
                    biased(s - 1, 1 - sp)
                if exists(s - 2, NT):
                    inverse_root(pool, s - 2)

            turns(pool, NT, turn, FIRST, LAST)

        @block.tensor
        def _(pe):
            def turn_over(t, tp):
                pe.wait_ge(c_ready, t + 1)
                pe.wait_ge(xn_ready, t + 1)
                wait(pe, turned_out, 2 * t)
                wait(pe, k4_ready, t)
                nc.tensor.transpose(p_T[:, 0:P], xn[:, tp, 0, :], ident[:])
                nc.tensor.transpose(p_T[:, P:2 * P], xn[:, tp, 1, :], ident[:]).then_inc(turned, 1)

            def project(t, tp):
                pe.wait_ge(turned_out, 2 * t + 2)
                wait(pe, q_ready, t)
                wait(pe, v_ready, 4 * t)
                nc.tensor.matmul(p_T[:, 2 * P:3 * P], w_c[:, 1, :], cT[:, tp, :, 0, :], start=True, stop=True)
                nc.tensor.matmul(p_qv[:, 0:P], w_c[:, 0, :], xT[:, tp, :], start=True, stop=True)
                for b in range(2):
                    last = nc.tensor.matmul(p_qv[:, (1 + b) * P:(2 + b) * P], cT[:, tp, b].rearrange("p c s -> p (c s)"),
                                            w_c[:, 2, :], start=True, stop=True)
                last.then_inc(qkv_done, 1)

            def scores(t, tp, b):
                if b == 0:
                    pe.wait_ge(k4_ready, t + 1)
                    pe.wait_ge(q_ready, t + 1)
                    wait(pe, shifted, t)
                for g in range(G):
                    r = slice(32 * g, 32 * g + 32)
                    last = nc.tensor.matmul(p_s[b * S:(b + 1) * S, g, 0:4 * S], q[r, tp, b, :],
                                            k4[r, tp, b].rearrange("p h s -> p (h s)"), start=True, stop=True)
                if b == 1:
                    last.then_inc(scored, 1)

            def probs_T(t, tp, j):
                pe.wait_ge(exped, t + 1)
                wait(pe, prT_ready, 2 * t + j)
                for i in range(HP // 2):
                    n = j * HP // 2 + i
                    last = nc.tensor.transpose(p_pT[:, i * P:(i + 1) * P],
                                               pr[:, tp, 2 * n:2 * n + 2, :].rearrange("p h s -> p (h s)"), ident[:])
                last.then_inc(pT_done, 1)

            def mix(t, tp, j):
                pe.wait_ge(prT_ready, 2 * t + j + 1)
                pe.wait_ge(v_ready, 4 * t + 4)
                wait(pe, x_new, t)
                for i in range(HP // 2):
                    n = j * HP // 2 + i
                    last = nc.tensor.matmul(p_o[:, n * WIDE:(n + 1) * WIDE], prT[:, j, i, :],
                                            vals[:, tp, n].rearrange("p b h e -> p (b h e)"), start=True, stop=True)
                last.then_inc(mixed, 1)

            def att_T(t, tp):
                pe.wait_ge(att_ready, t + 1)
                nc.tensor.transpose(p_o[:, 320:320 + P], att[:, tp, :], ident[:]).then_inc(aT_done, 1)

            def out_proj(t, tp):
                pe.wait_ge(oT_ready, t + 1)
                nc.tensor.matmul(p_o[:, 0:D], oT[:, tp, :], w_c[:, 3, :], start=True, stop=True).then_inc(y_done, 1)

            def turn(s, sp):
                now, back, tail, ahead = exists(s, NT), exists(s - 1, NT), exists(s - 2, NT), exists(s + 1, NT)
                if now:
                    scores(s, sp, 0)
                if tail:
                    att_T(s - 2, sp)
                if now:
                    scores(s, sp, 1)
                if back:
                    probs_T(s - 1, 1 - sp, 0)
                if tail:
                    out_proj(s - 2, sp)
                if ahead:
                    project(s + 1, 1 - sp)
                if back:
                    probs_T(s - 1, 1 - sp, 1)
                    mix(s - 1, 1 - sp, 0)
                if exists(s + 2, NT):
                    turn_over(s + 2, sp)
                if back:
                    mix(s - 1, 1 - sp, 1)

            pe.wait_ge(zeroed, 3)
            turns(pe, NT, turn, FIRST, LAST)

        @block.scalar
        def _(act):
            def turn_out(t, tp):
                act.wait_ge(turned, t + 1)
                wait(act, qkv_done, t - 1)
                nc.scalar.copy(cT[:, tp], p_T[:, 0:P].rearrange("p (b s) -> p b s", b=2).unsqueeze(2)
                               .to_broadcast([P, 2, 2, S])).then_inc(turned_out, 1)
                nc.scalar.copy(xT[:, tp, :], p_T[:, P:2 * P]).then_inc(turned_out, 1)

            def queries_out(t, tp):
                act.wait_ge(qkv_done, t + 1)
                wait(act, scored, t - 1)
                nc.scalar.activation(q[:, tp].rearrange("p b s -> p (b s)"), p_qv[:, 0:P], ACT.Identity,
                                     bias=cols[:, 5:6]).then_inc(q_ready, 1)

            def values_out(t, tp):
                act.wait_ge(qkv_done, t + 1)
                wait(act, mixed, 2 * (t - 1))
                for b in range(2):
                    for a in range(2):
                        src = p_qv[a * S:(a + 1) * S, (1 + b) * P:(2 + b) * P].rearrange("p (n h e) -> p n h e", n=HP, h=2)
                        nc.scalar.copy(vals[a * S:(a + 1) * S, tp, :, b, a, 0:DH], src[:, :, a]).then_inc(v_ready, 1)

            def exp(t, tp):
                act.wait_ge(shifted, t + 1)
                flat = pr[:, tp].rearrange("p h s -> p (h s)")
                nc.scalar.activation(flat, flat, ACT.Exp).then_inc(exped, 1)

            def probs_out(t, b):
                act.wait_ge(pT_done, 2 * t + b + 1)
                wait(act, mixed, 2 * (t - 1) + b + 1)
                nc.scalar.copy(prT[:, b].rearrange("p i k -> p (i k)"), p_pT[:]).then_inc(prT_ready, 1)

            def att_out(t, tp):
                act.wait_ge(aT_done, t + 1)
                wait(act, y_done, t)
                nc.scalar.activation(oT[:, tp, :], p_o[:, 320:320 + P], ACT.Identity, bias=cols[:, 7:8]).then_inc(oT_ready, 1)

            def turn(s, sp):
                back, ahead = exists(s - 1, NT), exists(s + 1, NT)
                if exists(s - 2, NT):
                    att_out(s - 2, sp)
                if back:
                    probs_out(s - 1, 0)
                if ahead:
                    queries_out(s + 1, 1 - sp)
                if back:
                    probs_out(s - 1, 1)
                if ahead:
                    values_out(s + 1, 1 - sp)
                if exists(s + 2, NT):
                    turn_out(s + 2, sp)
                if exists(s, NT):
                    exp(s, sp)

            act.wait_ge(zeroed, 3)
            turns(act, NT, turn, FIRST, LAST)

        @block.vector
        def _(dve):
            nc.vector.memset(vals[:], 0.0).then_inc(zeroed, 1)
            dve.wait_ge(zeroed, 1)
            for a in range(2):
                last = nc.vector.memset(vals[a * S:(a + 1) * S, :, :, :, a, DH:DH + 1].rearrange("p x n b o -> p (x n b) o"), 1.0)
                last.then_inc(zeroed, 1)
            s4 = p_s[:, :, 0:4 * S].rearrange("p g (i s) -> p g i s", s=S)

            def normalise(t, tp):
                wait(dve, turned, t - 1)
                nc.vector.tensor_scalar(xn[:, tp, 1, :], xs[:, t, :], moments[:, 1, t, 0:1], moments[:, 1, t, 1:2],
                                        ALU.subtract, ALU.mult).then_inc(xn_ready, 1)

            def keys(t, tp):
                dve.wait_ge(qkv_done, t + 1)
                wait(dve, scored, t - 1)
                for b in range(2):
                    last = nc.vector.scalar_tensor_tensor(
                        k4[:, tp, b], p_T[:, 2 * P + b * S:2 * P + (b + 1) * S].unsqueeze(1).to_broadcast([P, 4, S]),
                        cols[:, 6:7], quad[:].unsqueeze(2).to_broadcast([P, 4, S]), ALU.add, ALU.mult)
                last.then_inc(k4_ready, 1)

            def row_max(t, tp):
                dve.wait_ge(scored, t + 1)
                nc.vector.tensor_reduce(mx[:, tp], s4, AX.X, ALU.max).then_inc(maxed, 1)

            def shift(t, tp):
                dve.wait_ge(maxed, t + 1)
                wait(dve, pT_done, 2 * (t - 1))
                nc.vector.tensor_tensor(pr[:, tp].rearrange("p (g h) s -> p g h s", g=G), s4,
                                        mx[:, tp].unsqueeze(3).to_broadcast([P, G, 4, S]),
                                        ALU.subtract).then_inc(shifted, 1)

            def attend(t, tp):
                dve.wait_ge(mixed, 2 * t + 2)
                o5 = p_o[:, 0:HP * WIDE].rearrange("p (n b h e) -> p n b h e", n=HP, b=2, h=2)
                nc.vector.reciprocal(rs[:, tp, :].rearrange("p (n h) -> p n h", h=2), o5[:, :, 0, :, DH])\
                    .then_inc(inverse, 1)
                dve.wait_ge(inverse, t + 1)
                wait(dve, aT_done, t)
                for b in range(2):
                    r = slice(b * S, (b + 1) * S)
                    last = nc.vector.tensor_tensor(att[r, tp, :].rearrange("p (n h e) -> p n h e", n=HP, h=2),
                                                   o5[r, :, b, :, 0:DH],
                                                   rs[r, tp, :].rearrange("p (n h) -> p n h", h=2).unsqueeze(3)
                                                   .to_broadcast([S, HP, 2, DH]), ALU.mult)
                last.then_inc(att_ready, 1)

            def output(t, tp):
                dve.wait_ge(y_done, t + 1)
                dve.wait_ge(xb_ready, t + 1)
                nc.vector.tensor_tensor(xs[:, t, :], p_o[:, 0:D], xb[:, tp, :], ALU.add).then_inc(x_new, 1)

            def turn(s, sp):
                now, tail = exists(s, NT), exists(s - 2, NT)
                if tail:
                    attend(s - 2, sp)
                if exists(s + 2, NT):
                    normalise(s + 2, sp)
                if now:
                    row_max(s, sp)
                if tail:
                    output(s - 2, sp)
                if now:
                    shift(s, sp)
                if tail:
                    row_stats(dve, s - 2, sp, x_new)
                    row_moments(dve, s - 2, sp)
                if exists(s + 1, NT):
                    keys(s + 1, 1 - sp)
                if tail:
                    keep_moments(dve, s - 2, sp)

            turns(dve, NT, turn, FIRST, LAST)


def ffn_1(nc, v, o_tiles):
    xs, moments, neghalf, identb = (v[n] for n in "xs moments neghalf identb".split())
    gates, rows, b1row, w1_t, w2_t, wmean = (v[n] for n in "gates rows b1row w1_t w2_t wmean".split())
    NT, D, FF, EPS, MAGIC = (v[n] for n in "NT D FF EPS MAGIC".split())
    C = FF // P
    NP = NT // 2
    with ExitStack() as ph, nc.Block() as block:
        def sb(name, shape, dt=F32):
            return ph.enter_context(nc.sbuf_tensor("f_" + name, shape, dt))

        def pb(name, dt=F32, n=512):
            return ph.enter_context(nc.psum_tensor("f_" + name, [P, n], dt))

        def sem(name):
            return ph.enter_context(nc.semaphore("f_" + name))

        hn = sb("hn", [P, 2, 2, D])
        hq = sb("hq", [P, 2, 2, D], BF16)
        hT = sb("hT", [P, 2, 2, P], BF16)
        hid = sb("hid", [P, 2, 2, FF])
        ge = sb("ge", [P, 2, 2, FF])
        gq = sb("gq", [P, 2, 2, FF], BF16)
        gT = sb("gT", [P, 2, 2, C, P], BF16)
        top = sb("top", [P, 2, 2, 2])
        fine = sb("fine", [P, 2, 2, 2])
        back_ = sb("back_", [P, 2, 2, 2])
        wback = sb("wback", [P, 2])
        xb = sb("xb", [P, 2, 2, D])
        p_a, p_y = pb("a", BF16, 1024), pb("y")
        p_b = (pb("b0", BF16, 1024), pb("b1", BF16, 1024))
        p_h = ((pb("h00"), pb("h01")), (pb("h10"), pb("h11")))
        (chain, norm_chain, hq_ready, aT_done, aT_ready, up_done, hid_ready, gelu_done,
         quant_chain, gq_ready, bT_done, bT_ready, y_done, xb_ready, x_new, stored) = (
            sem(n) for n in ("chain", "norm_chain", "hq_ready", "aT_done", "aT_ready",
                             "up_done", "hid_ready", "gelu_done", "quant_chain", "gq_ready", "bT_done", "bT_ready",
                             "y_done", "xb_ready", "x_new", "stored"))

        FIRST, LAST = -1, NP + 1

        @block.sync
        def _(sp):
            with sp.Fori(0, NP) as t:
                sp.wait_ge(x_new, t + 1)
                sp.dma_start(o_tiles[:, bass.ds(2 * t, 2), :], xs[:, bass.ds(2 * t, 2), :]).then_inc(stored, 16)
            sp.wait_ge(stored, 16 * NP)

        @block.gpsimd
        def _(pool):

            def turn(s, sp):
                if exists(s, NP):
                    wait(pool, x_new, s - 1)
                    for i in range(2):
                        last = nc.gpsimd.tensor_tensor(xb[:, sp, i, :], xs[:, 2 * s + i, :], rows[:, 3, :], ALU.add)
                    last.then_inc(xb_ready, 1)

            turns(pool, NP, turn, FIRST, LAST)

        @block.tensor
        def _(pe):
            def turn_over(t, tp):
                pe.wait_ge(hq_ready, t + 1)
                wait(pe, aT_ready, t)
                for i in range(2):
                    last = nc.tensor.transpose(p_a[:, i * P:(i + 1) * P], hq[:, tp, i, :], identb[:])
                last.then_inc(aT_done, 1)

            def up(t, tp):
                pe.wait_ge(aT_ready, t + 1)
                wait(pe, hid_ready, 2 * (t - 1))
                for i in range(2):
                    nc.tensor.matmul(p_h[tp][i][:], hT[:, tp, i, :], w1_t[:], start=True, stop=True).then_inc(up_done, 1)

            def turn_hidden(t, tp):
                pe.wait_ge(gq_ready, t + 1)
                wait(pe, bT_ready, t - 1)
                for i in range(2):
                    for c in range(C):
                        last = nc.tensor.transpose(p_b[tp][:, (i * C + c) * P:(i * C + c + 1) * P],
                                                   gq[:, tp, i, c * P:(c + 1) * P], identb[:])
                last.then_inc(bT_done, 1)

            def down(t, tp):
                pe.wait_ge(bT_ready, t + 1)
                wait(pe, x_new, t)
                for i in range(2):
                    for c in range(C):
                        last = nc.tensor.matmul(p_y[:, i * D:(i + 1) * D], gT[:, tp, i, c, :], w2_t[:, c, :],
                                                start=(c == 0), stop=(c == C - 1))
                last.then_inc(y_done, 1)

            def turn(s, sp):
                if exists(s, NP):
                    turn_over(s, sp)
                if exists(s - 2, NP):
                    down(s - 2, sp)
                if exists(s, NP):
                    up(s, sp)
                if exists(s - 1, NP):
                    turn_hidden(s - 1, 1 - sp)

            turns(pe, NP, turn, FIRST, LAST)

        @block.scalar
        def _(act):
            def turned_out(t, tp):
                act.wait_ge(aT_done, t + 1)
                wait(act, up_done, 2 * (t - 1))
                nc.scalar.copy(hT[:, tp].rearrange("p i k -> p (i k)"), p_a[:, 0:2 * P]).then_inc(aT_ready, 1)

            def gelu(t, tp):
                wait(act, gq_ready, t - 1)
                for i in range(2):
                    act.wait_ge(hid_ready, 2 * t + i + 1)
                    nc.scalar.activation(ge[:, tp, i, :], hid[:, tp, i, :], ACT.Gelu).then_inc(gelu_done, 1)

            def hidden_out(t, tp):
                act.wait_ge(bT_done, t + 1)
                wait(act, y_done, t - 1 if isinstance(t, int) else t)
                nc.scalar.copy(gT[:, tp].rearrange("p i c k -> p (i c k)"), p_b[tp][:]).then_inc(bT_ready, 1)

            def turn(s, sp):
                if exists(s - 2, NP):
                    hidden_out(s - 2, sp)
                if exists(s, NP):
                    turned_out(s, sp)
                    gelu(s, sp)

            turns(act, NP, turn, FIRST, LAST)

        @block.vector
        def _(dve):
            step = Steps(dve, chain)
            step(nc.vector.tensor_scalar(wback[:], wmean[:], 1.0 / 127.0, None, ALU.mult))
            step(nc.vector.tensor_scalar(wback[:, 1:2], wback[:, 1:2], gates[:, 3:4], None, ALU.mult))

            class Quantise:

                def __init__(self, sem, base, src, dst, tp, layer):
                    self.sem, self.base, self.n = sem, base, 0
                    self.src, self.dst = src, dst
                    self.top, self.fine, self.back = (x[:, tp, layer, :] for x in (top, fine, back_))
                    self.wback = wback[:, layer:layer + 1]

                def mark(self, ins):
                    ins.then_inc(self.sem, 1)
                    self.n += 1

                def follow(self):
                    dve.wait_ge(self.sem, self.base + self.n)

                def largest(self):
                    self.mark(nc.vector.tensor_reduce(self.top, self.src, AX.X, ALU.max, apply_absolute_value=True))

                def bound(self):
                    self.follow()
                    self.mark(nc.vector.tensor_scalar(self.top, self.top, EPS, None, ALU.max))

                def factors(self):
                    self.follow()
                    nc.vector.tensor_scalar(self.back, self.top, self.wback, None, ALU.mult)
                    self.mark(nc.vector.reciprocal(self.fine, self.top))

                def invert(self):
                    self.follow()
                    self.mark(nc.vector.tensor_scalar(self.fine, self.fine, 127.0, None, ALU.mult))

                def round(self):
                    self.follow()
                    for i in range(2):
                        last = nc.vector.tensor_scalar(self.src[:, i, :], self.src[:, i, :], self.fine[:, i:i + 1], MAGIC,
                                                       ALU.mult, ALU.add)
                    self.mark(last)

                def finish(self):
                    self.follow()
                    return nc.vector.tensor_scalar(self.dst, self.src, MAGIC, 127.0, ALU.subtract, ALU.min)

            def hidden(t, tp, i):
                dve.wait_ge(up_done, 2 * t + i + 1)
                wait(dve, gelu_done, 2 * (t - 1))
                nc.vector.scalar_tensor_tensor(hid[:, tp, i, :], p_h[tp][i][:], back_[:, tp, 0, i:i + 1], b1row[:],
                                               ALU.mult, ALU.add).then_inc(hid_ready, 1)

            def output(t, tp):
                dve.wait_ge(y_done, t + 1)
                dve.wait_ge(xb_ready, t + 1)
                for i in range(2):
                    last = nc.vector.scalar_tensor_tensor(xs[:, 2 * t + i, :], p_y[:, i * D:(i + 1) * D],
                                                          back_[:, tp, 1, i:i + 1], xb[:, tp, i, :], ALU.mult, ALU.add)
                last.then_inc(x_new, 1)

            def turn(s, sp):
                now, back, ahead = exists(s, NP), exists(s - 1, NP), exists(s + 1, NP)
                first = Quantise(norm_chain, 7 * (s + 1), hn[:, 1 - sp], hq[:, 1 - sp], 1 - sp, 0)
                second = Quantise(quant_chain, 5 * (s - 1), ge[:, 1 - sp], gq[:, 1 - sp], 1 - sp, 1)
                if back:
                    dve.wait_ge(gelu_done, 2 * s)
                    second.largest()
                if ahead:
                    for i in range(2):
                        last = nc.vector.scalar_tensor_tensor(hn[:, 1 - sp, i, :], xs[:, 2 * s + 2 + i, :],
                                                              moments[:, 1, 2 * s + 2 + i, 0:1], rows[:, 4, :],
                                                              ALU.subtract, ALU.mult)
                    first.mark(last)
                if back:
                    second.bound()
                if ahead:
                    first.follow()
                    for i in range(2):
                        last = nc.vector.scalar_tensor_tensor(hn[:, 1 - sp, i, :], hn[:, 1 - sp, i, :],
                                                              moments[:, 1, 2 * s + 2 + i, 1:2], rows[:, 5, :],
                                                              ALU.mult, ALU.add)
                    first.mark(last)
                if back:
                    second.factors()
                if ahead:
                    first.follow()
                    first.largest()
                if back:
                    second.invert()
                if ahead:
                    first.bound()
                if back:
                    second.round()
                if ahead:
                    first.factors()
                if now:
                    hidden(s, sp, 0)
                if ahead:
                    first.invert()
                if back:
                    wait(dve, bT_done, s - 2)
                    second.finish().then_inc(gq_ready, 1)
                if ahead:
                    first.round()
                if now:
                    hidden(s, sp, 1)
                if ahead:
                    wait(dve, aT_done, s)
                    first.finish().then_inc(hq_ready, 1)
                if exists(s - 2, NP):
                    output(s - 2, sp)

            turns(dve, NP, turn, FIRST, LAST)


_INS = ["x", "ctx_1024", "mask_BxS2_bk0", "g_xattn", "g_ffn",
        "L0_xattn_ln_x_w", "L0_xattn_ln_x_b", "L0_xattn_ln_l_w", "L0_xattn_ln_l_b", "L0_xattn_Wq", "L0_xattn_Wkv",
        "L0_xattn_q_scale", "L0_xattn_k_scale", "L0_xattn_Wo", "L0_xattn_ln_o_w", "L0_xattn_ln_o_b",
        "L0_ffn_gate_w", "L0_ffn_Wg", "L0_ffn_Wu", "L0_ffn_Wd", "L0_ffn_Ws_g", "L0_ffn_Ws_u", "L0_ffn_Ws_d",
        "L1_xattn_wq_w", "L1_xattn_wq_b", "L1_xattn_wk_w", "L1_xattn_wk_b", "L1_xattn_wv_w", "L1_xattn_wv_b",
        "L1_xattn_wo_w", "L1_xattn_wo_b", "L1_ffn_w1", "L1_ffn_b1", "L1_ffn_w2", "L1_ffn_b2", "L1_ffn_gamma",
        "L1_ffn_beta"]
_OUTS = [((32, 64, 128), "float32")]


def kernel(**inputs):
    import numpy as _np
    import concourse.bacc as _bacc
    from concourse import mybir as _mybir
    from concourse.bass_utils import run_bass_kernel_spmd as _run

    nc = _bacc.Bacc("TRN2", target_bir_lowering=False, num_devices=1)
    arrays, args = {}, []
    for name in _INS:
        a = _np.ascontiguousarray(inputs[name])
        arrays[f"in_{name}_dram"] = a
        args.append(nc.dram_tensor(f"in_{name}_dram", a.shape, _mybir.dt.from_np(a.dtype), kind="ExternalInput").ap())
    for i, (shape, dtype) in enumerate(_OUTS):
        dt = _mybir.dt.from_np(_np.dtype(dtype))
        args.append(nc.dram_tensor(f"out_{i}_dram", shape, dt, kind="ExternalOutput").ap())
    build(nc, *args)
    r = _run(nc, [arrays], core_ids=[0])
    got = tuple(r.results[0][f"out_{i}_dram"] for i in range(len(_OUTS)))
    return got[0]
```
